# Optimizing a Trainium2 kernel written in Bass

```python
import numpy as np
import jax
import jax.numpy as jnp

def _softmax(x, axis=-1):
    return jax.nn.softmax(x, axis=axis)

def _gelu(x):
    return jax.nn.gelu(x, approximate=True)

def _silu(x):
    return jax.nn.silu(x)

def _sigmoid(x):
    return jax.nn.sigmoid(x)

def _layernorm(x, axis=-1, eps=1e-05):
    m = jnp.mean(x, axis=axis, keepdims=True)
    v = jnp.var(x, axis=axis, keepdims=True)
    return (x - m) / jnp.sqrt(v + eps)

def _scatter_add(tgt, idx, src, axis=0):
    return tgt.at[idx].add(src)

def _segment_sum(src, seg, n):
    return jax.ops.segment_sum(src, seg, n)
kernel_name = 'mk_hybrid_d4_jaxref_r8_dc3492'

def setup_inputs(seed: int=0):
    np.random.seed(seed)
    _w = jnp.asarray

    def _L0_attn_a_setup():
        import jax, jax.numpy as jnp
        import numpy as np
        B, L, C = (2, 256, 128)
        H, POS = (8, 16)
        D = C // H
        MAXS = 32
        S = MAXS + 1
        MAX_FREQ, MIN_FREQ = (16.0, 1.0)
        SCALE = POS ** (-0.5)
        key = jax.random.key(seed)
        ks = jax.random.split(key, 12)

        def w(k, shape, s=0.02):
            return jax.random.normal(k, shape, dtype=jnp.float32) * s
        return {'x': jax.random.normal(ks[0], (B, L, C), dtype=jnp.float32), 'w_wave': w(ks[1], (C, 3 * H)), 'b_wave': w(ks[2], (3 * H,)), 'w_query': w(ks[3], (C, H * POS)), 'b_query': w(ks[4], (H * POS,)), 'key_weight': w(ks[5], (POS,)), 'w_se1': w(ks[6], (C, C // 4)), 'b_se1': w(ks[7], (C // 4,)), 'w_se2': w(ks[8], (C // 4, C)), 'b_se2': w(ks[9], (C,)), 'w_out': w(ks[10], (C, C))}
    _L0_attn_a_in = _L0_attn_a_setup()

    def _L0_attn_b_setup():
        import jax, jax.numpy as jnp
        import numpy as np
        B, T, D_MODEL, N = (4, 256, 128, 16)
        D_INNER = 2 * D_MODEL

        def _ssm_scan(x_in, A, B_ssm, C_ssm):

            def step(state, ins):
                x_t, a_t, b_t, c_t = ins
                decay = jnp.exp(a_t)
                state = state * decay[:, None, :] + x_t[:, :, None] * b_t[:, None, :]
                out_t = (state * c_t[:, None, :]).sum(-1)
                return (state, out_t)
            b, t, d = x_in.shape
            n = A.shape[-1]
            init = jnp.zeros((b, d, n), dtype=x_in.dtype)
            xs = (jnp.swapaxes(x_in, 0, 1), jnp.swapaxes(A, 0, 1), jnp.swapaxes(B_ssm, 0, 1), jnp.swapaxes(C_ssm, 0, 1))
            _, outs = jax.lax.scan(step, init, xs)
            return jnp.swapaxes(outs, 0, 1)
        key = jax.random.key(seed)
        ks = jax.random.split(key, 7)
        s = 0.02
        return {'x': jax.random.normal(ks[0], (B, T, D_MODEL), dtype=jnp.float32), 'W_in': jax.random.normal(ks[1], (D_MODEL, 2 * D_INNER), dtype=jnp.float32) * s, 'W_A': jax.random.normal(ks[2], (D_INNER, N), dtype=jnp.float32) * s, 'W_B': jax.random.normal(ks[3], (D_INNER, N), dtype=jnp.float32) * s, 'W_C': jax.random.normal(ks[4], (D_INNER, N), dtype=jnp.float32) * s, 'W_out': jax.random.normal(ks[5], (D_INNER, D_MODEL), dtype=jnp.float32) * s, 'norm_w': jnp.ones((D_INNER,), dtype=jnp.float32)}
    _L0_attn_b_in = _L0_attn_b_setup()

    def _L0_ffn_setup():
        import jax, jax.numpy as jnp
        import numpy as np
        D = 128
        H = 16
        DK = D // H
        E = 8
        DFF = 4 * D
        TOPK = 2
        EPS = 1e-05

        def _layernorm(x, g, b):
            m = jnp.mean(x, axis=-1, keepdims=True)
            v = jnp.mean(jnp.square(x - m), axis=-1, keepdims=True)
            return (x - m) * jax.lax.rsqrt(v + EPS) * g + b
        key = jax.random.key(seed)
        ks = jax.random.split(key, 16)
        s_in = 1.0 / np.sqrt(D)
        s_ff = 1.0 / np.sqrt(DFF)
        return {'x': jax.random.normal(ks[0], (2, 256, D), dtype=jnp.float32), 'ln1_g': jnp.ones((D,), jnp.float32), 'ln1_b': jnp.zeros((D,), jnp.float32), 'w_qkv': jax.random.normal(ks[1], (D, 3 * D), jnp.float32) * s_in, 'b_qkv': jnp.zeros((3 * D,), jnp.float32), 'w_o': jax.random.normal(ks[2], (D, D), jnp.float32) * s_in, 'b_o': jnp.zeros((D,), jnp.float32), 'ln2_g': jnp.ones((D,), jnp.float32), 'ln2_b': jnp.zeros((D,), jnp.float32), 'gate_w': jax.random.normal(ks[3], (D, E), jnp.float32) * s_in, 'gate_b': jnp.zeros((E,), jnp.float32), 'W1': jax.random.normal(ks[4], (E, D, DFF), jnp.float32) * s_in, 'b1': jnp.zeros((E, DFF), jnp.float32), 'W2': jax.random.normal(ks[5], (E, DFF, D), jnp.float32) * s_ff, 'b2': jnp.zeros((E, D), jnp.float32)}
    _L0_ffn_in = _L0_ffn_setup()

    def _L1_attn_a_setup():
        import jax, jax.numpy as jnp
        import numpy as np
        D_MODEL, D_INNER, D_STATE, DT_RANK, D_CONV = (128, 256, 16, 64, 4)
        B, L = (2, 256)

        def _rmsnorm(x, w, eps=1e-05):
            return x * jax.lax.rsqrt(jnp.mean(x * x, axis=-1, keepdims=True) + eps) * w

        def _causal_depthwise_conv(x, conv_w, conv_b):
            K = conv_w.shape[1]
            xp = jnp.pad(x, ((0, 0), (K - 1, 0), (0, 0)))
            Lx = x.shape[1]
            out = conv_b
            for k in range(K):
                out = out + xp[:, k:k + Lx, :] * conv_w[:, k]
            return out

        def _selective_scan(x, delta, Bm, Cm, A):
            h0 = jnp.zeros((x.shape[0], A.shape[0], A.shape[1]), x.dtype)

            def step(h, inp):
                xt, dt, bt, ct = inp
                A_bar = jnp.exp(dt[..., None] * A)
                h = A_bar * h + (dt * xt)[..., None] * bt[:, None, :]
                y = jnp.einsum('ben,bn->be', h, ct)
                return (h, y)
            xs = tuple((jnp.swapaxes(a, 0, 1) for a in (x, delta, Bm, Cm)))
            _, ys = jax.lax.scan(step, h0, xs)
            return jnp.swapaxes(ys, 0, 1)
        key = jax.random.key(seed)
        ks = jax.random.split(key, 14)
        s = lambda k, shp, fan: jax.random.normal(k, shp, jnp.float32) / np.sqrt(fan)
        return {'resid': jax.random.normal(ks[0], (B, L, D_MODEL), jnp.float32), 'norm_w': jnp.ones((D_MODEL,), jnp.float32), 'skip_w': s(ks[1], (D_INNER, D_MODEL), D_MODEL), 'in_w': s(ks[2], (D_INNER, D_MODEL), D_MODEL), 'conv_w': s(ks[3], (D_INNER, D_CONV), D_CONV), 'conv_b': jnp.zeros((D_INNER,), jnp.float32), 'wd1': s(ks[4], (DT_RANK, D_INNER), D_INNER), 'wd2': s(ks[5], (D_INNER, DT_RANK), DT_RANK), 'wd2_b': jnp.zeros((D_INNER,), jnp.float32), 'wb': s(ks[6], (D_STATE, D_INNER), D_INNER), 'wc': s(ks[7], (D_STATE, D_INNER), D_INNER), 'A_log': jax.random.normal(ks[8], (D_INNER, D_STATE), jnp.float32), 'W_D': jnp.ones((D_INNER,), jnp.float32), 'out_w': s(ks[9], (D_MODEL, D_INNER), D_INNER)}
    _L1_attn_a_in = _L1_attn_a_setup()

    def _L1_attn_b_setup():
        import jax, jax.numpy as jnp
        import numpy as np
        D_MODEL = 128
        D_STATE = 16
        D_CONV = 4
        D_INNER = 2 * D_MODEL
        B, T = (4, 512)
        EPS = 1e-05

        def _layernorm(x, w, b):
            mu = jnp.mean(x, axis=-1, keepdims=True)
            var = jnp.mean(jnp.square(x - mu), axis=-1, keepdims=True)
            return (x - mu) * jax.lax.rsqrt(var + EPS) * w + b

        def _silu(x):
            return x * jax.nn.sigmoid(x)
        key = jax.random.key(seed)
        ks = jax.random.split(key, 8)
        s = lambda k, shape, fan: jax.random.normal(k, shape, jnp.float32) * (1.0 / np.sqrt(fan))
        return {'x': jax.random.normal(ks[0], (B, T, D_MODEL), jnp.float32), 'norm_w': jnp.ones((D_MODEL,), jnp.float32), 'norm_b': jnp.zeros((D_MODEL,), jnp.float32), 'in_w': s(ks[1], (D_INNER * 2, D_MODEL), D_MODEL), 'in_b': jnp.zeros((D_INNER * 2,), jnp.float32), 'conv_w': s(ks[2], (D_INNER, 1, D_CONV), D_CONV), 'conv_b': jnp.zeros((D_INNER,), jnp.float32), 'xproj_w': s(ks[3], (2 * D_STATE + 1, D_INNER), D_INNER), 'A_log': jnp.log(jnp.arange(1, D_STATE + 1, dtype=jnp.float32)), 'D': jnp.ones((D_INNER,), jnp.float32), 'out_w': s(ks[4], (D_MODEL, D_INNER), D_INNER), 'out_b': jnp.zeros((D_MODEL,), jnp.float32)}
    _L1_attn_b_in = _L1_attn_b_setup()

    def _L1_ffn_setup():
        import jax, jax.numpy as jnp
        import numpy as np
        D_MODEL = 128
        FFN = 128
        N_EXPERTS = 8
        N_SHARED = 1
        TOP_K = 2
        B, S = (2, 256)

        def _swiglu(h):
            a, b = jnp.split(h, 2, axis=-1)
            return jax.nn.silu(a) * b
        key = jax.random.key(seed)
        ks = jax.random.split(key, 12)
        sc = 0.02
        return {'x': jax.random.normal(ks[0], (B, S, D_MODEL), dtype=jnp.float32), 'gate_w': jax.random.normal(ks[1], (D_MODEL, N_EXPERTS), dtype=jnp.float32) * sc, 'gate_b': jnp.zeros((N_EXPERTS,), dtype=jnp.float32), 'sw1': jax.random.normal(ks[2], (N_SHARED, D_MODEL, 2 * FFN), dtype=jnp.float32) * sc, 'sb1': jnp.zeros((N_SHARED, 2 * FFN), dtype=jnp.float32), 'sw2': jax.random.normal(ks[3], (N_SHARED, FFN, D_MODEL), dtype=jnp.float32) * sc, 'sb2': jnp.zeros((N_SHARED, D_MODEL), dtype=jnp.float32), 'rw1': jax.random.normal(ks[4], (N_EXPERTS, D_MODEL, 2 * FFN), dtype=jnp.float32) * sc, 'rb1': jnp.zeros((N_EXPERTS, 2 * FFN), dtype=jnp.float32), 'rw2': jax.random.normal(ks[5], (N_EXPERTS, FFN, D_MODEL), dtype=jnp.float32) * sc, 'rb2': jnp.zeros((N_EXPERTS, D_MODEL), dtype=jnp.float32)}
    _L1_ffn_in = _L1_ffn_setup()

    def _L2_attn_a_setup():
        import jax, jax.numpy as jnp
        import numpy as np
        EPS = 1e-05

        def _ln(x, g, b):
            m = jnp.mean(x, axis=-1, keepdims=True)
            v = jnp.mean((x - m) ** 2, axis=-1, keepdims=True)
            return (x - m) * jax.lax.rsqrt(v + EPS) * g + b

        def _forward(x, ln_attn_g, ln_attn_b, Wq, bq, Wk, bk, Wv, bv, ln_conv_g, ln_conv_b, conv_w, conv_b, ln_boom_g, ln_boom_b, Wb, bb, Wu, bu):
            B, S, D = x.shape
            K = conv_w.shape[-1]
            G = D // conv_w.shape[1]
            h = _ln(x, ln_conv_g, ln_conv_b)
            hc = jnp.transpose(h, (0, 2, 1))
            hc = jnp.pad(hc, ((0, 0), (0, 0), (K - 1, 0)))
            conv = jax.lax.conv_general_dilated(hc, conv_w, window_strides=(1,), padding='VALID', dimension_numbers=('NCH', 'OIH', 'NCH'), feature_group_count=G)
            conv = conv + conv_b[None, :, None]
            x = x + jnp.transpose(conv, (0, 2, 1))
            h = _ln(x, ln_attn_g, ln_attn_b)
            q = jnp.einsum('bsd,ed->bse', h, Wq) + bq
            k = jnp.einsum('bsd,ed->bse', h, Wk) + bk
            v = jnp.einsum('bsd,ed->bse', h, Wv) + bv
            scale = jnp.arange(1, S + 1, dtype=x.dtype)[None, :, None]
            pooled_q = jnp.cumsum(q, axis=1) / scale
            pooled_k = jnp.cumsum(pooled_q * k, axis=1) / scale
            x = x + pooled_k * v
            h = _ln(x, ln_boom_g, ln_boom_b)
            h = jax.nn.gelu(jnp.einsum('bsd,ed->bse', h, Wb) + bb, approximate=False)
            h = jnp.einsum('bse,de->bsd', h, Wu) + bu
            return x + h
        key = jax.random.key(seed)
        ks = jax.random.split(key, 8)
        B, S, D, K, G = (4, 256, 128, 4, 4)
        w = lambda k, shape: jax.random.normal(k, shape, jnp.float32) * 0.02
        return {'hidden_states': jax.random.normal(ks[0], (B, S, D), jnp.float32), 'attention_mask': jnp.ones((B, S), jnp.int32), 'ln_attn_g': jnp.ones((D,), jnp.float32), 'ln_attn_b': jnp.zeros((D,), jnp.float32), 'Wq': w(ks[1], (D, D)), 'bq': jnp.zeros((D,), jnp.float32), 'Wk': w(ks[2], (D, D)), 'bk': jnp.zeros((D,), jnp.float32), 'Wv': w(ks[3], (D, D)), 'bv': jnp.zeros((D,), jnp.float32), 'ln_conv_g': jnp.ones((D,), jnp.float32), 'ln_conv_b': jnp.zeros((D,), jnp.float32), 'conv_w': w(ks[4], (D, D // G, K)), 'conv_b': jnp.zeros((D,), jnp.float32), 'ln_boom_g': jnp.ones((D,), jnp.float32), 'ln_boom_b': jnp.zeros((D,), jnp.float32), 'Wb': w(ks[5], (4 * D, D)), 'bb': jnp.zeros((4 * D,), jnp.float32), 'Wu': w(ks[6], (D, 4 * D)), 'bu': jnp.zeros((D,), jnp.float32)}
    _L2_attn_a_in = _L2_attn_a_setup()

    def _L2_attn_b_setup():
        import jax, jax.numpy as jnp
        import numpy as np
        EMB = 128
        HEADS = 16
        HEAD_DIM = EMB // HEADS
        B, S = (2, 256)
        key = jax.random.key(seed)
        k1, k2, k3 = jax.random.split(key, 3)
        scale = 0.02
        return {'x': jax.random.normal(k1, (B, S, EMB), dtype=jnp.float32), 'W_qkv': jax.random.normal(k2, (3 * EMB, EMB), dtype=jnp.float32) * scale, 'b_qkv': jnp.zeros((3 * EMB,), dtype=jnp.float32), 'W_out': jax.random.normal(k3, (EMB, EMB), dtype=jnp.float32) * scale, 'b_out': jnp.zeros((EMB,), dtype=jnp.float32)}
    _L2_attn_b_in = _L2_attn_b_setup()

    def _L2_ffn_setup():
        import jax, jax.numpy as jnp
        import numpy as np
        B, S, H = (1, 256, 128)
        E, K = (16, 4)
        G, TG = (4, 2)
        I_MOE = 64
        N_SH = 2
        SCALE = 2.5

        def _mlp(x, gw, uw, dw):
            return jax.nn.silu(x @ gw.T) * (x @ uw.T) @ dw.T

        def _route(x2d, router_weight, e_bias):
            T = x2d.shape[0]
            scores = jax.nn.sigmoid(x2d @ router_weight.T)
            sc = scores + e_bias[None, :]
            group_scores = jnp.sum(jax.lax.top_k(sc.reshape(T, G, E // G), 2)[0], axis=-1)
            _, gidx = jax.lax.top_k(group_scores, TG)
            gmask = jnp.zeros((T, G), sc.dtype).at[jnp.arange(T)[:, None], gidx].set(1.0)
            smask = jnp.repeat(gmask, E // G, axis=1)
            masked = jnp.where(smask > 0, sc, 0.0)
            _, tidx = jax.lax.top_k(masked, K)
            tw = jnp.take_along_axis(scores, tidx, axis=1)
            tw = tw / (jnp.sum(tw, axis=-1, keepdims=True) + 1e-20)
            tw = tw * SCALE
            return (tidx, tw)

        def _moe_forward(hidden_states, router_weight, e_bias, gate_w, up_w, down_w, sh_gate_w, sh_up_w, sh_down_w):
            orig_shape = hidden_states.shape
            x = hidden_states.reshape(-1, H)
            T = x.shape[0]
            tidx, tw = _route(x, router_weight, e_bias)
            g = jnp.einsum('th,eih->tei', x, gate_w)
            u = jnp.einsum('th,eih->tei', x, up_w)
            h = jax.nn.silu(g) * u
            yo = jnp.einsum('tei,ehi->teh', h, down_w)
            combine = jnp.zeros((T, E), tw.dtype).at[jnp.arange(T)[:, None], tidx].add(tw)
            routed = jnp.einsum('te,teh->th', combine, yo)
            shared = _mlp(hidden_states.reshape(-1, H), sh_gate_w, sh_up_w, sh_down_w)
            return (routed + shared).reshape(orig_shape)
        key = jax.random.key(seed)
        ks = jax.random.split(key, 9)
        s = 0.02
        return {'hidden_states': jax.random.normal(ks[0], (B, S, H), jnp.float32), 'router_weight': jax.random.normal(ks[1], (E, H), jnp.float32) * s, 'e_bias': jnp.zeros((E,), jnp.float32), 'gate_w': jax.random.normal(ks[2], (E, I_MOE, H), jnp.float32) * s, 'up_w': jax.random.normal(ks[3], (E, I_MOE, H), jnp.float32) * s, 'down_w': jax.random.normal(ks[4], (E, H, I_MOE), jnp.float32) * s, 'sh_gate_w': jax.random.normal(ks[5], (N_SH * I_MOE, H), jnp.float32) * s, 'sh_up_w': jax.random.normal(ks[6], (N_SH * I_MOE, H), jnp.float32) * s, 'sh_down_w': jax.random.normal(ks[7], (H, N_SH * I_MOE), jnp.float32) * s}
    _L2_ffn_in = _L2_ffn_setup()

    def _L3_attn_a_setup():
        import jax, jax.numpy as jnp
        import numpy as np
        B, N, D, H = (4, 256, 128, 16)
        DH = D // H
        EPS = 1e-05
        key = jax.random.key(seed)
        k1, k2, k3, k4 = jax.random.split(key, 4)
        return {'x': jax.random.normal(k1, (B, N, D), dtype=jnp.float32), 'g_ln': jnp.ones((D,), dtype=jnp.float32), 'Wq': jax.random.normal(k2, (D, D), dtype=jnp.float32) * 0.02, 'Wkv': jax.random.normal(k3, (D, 2 * D), dtype=jnp.float32) * 0.02, 'Wo': jax.random.normal(k4, (D, D), dtype=jnp.float32) * 0.02}
    _L3_attn_a_in = _L3_attn_a_setup()

    def _L3_attn_b_setup():
        import jax, jax.numpy as jnp
        import numpy as np
        D_MODEL = 128
        N_HEADS = 16
        D_HEAD = D_MODEL // N_HEADS
        SCALE = 1.0 / np.sqrt(D_HEAD).astype(np.float32)

        def _feature_map(x):
            return jax.nn.elu(x) + 1.0
        key = jax.random.key(seed)
        ks = jax.random.split(key, 7)
        b, s = (4, 256)
        w = 1.0 / np.sqrt(D_MODEL).astype(np.float32)
        return {'x': jax.random.normal(ks[0], (b, s, D_MODEL), dtype=jnp.float32), 'Wq': jax.random.normal(ks[1], (D_MODEL, D_MODEL), dtype=jnp.float32) * w, 'Wk': jax.random.normal(ks[2], (D_MODEL, D_MODEL), dtype=jnp.float32) * w, 'Wv': jax.random.normal(ks[3], (D_MODEL, D_MODEL), dtype=jnp.float32) * w, 'Wo': jax.random.normal(ks[4], (D_MODEL, D_MODEL), dtype=jnp.float32) * w, 'Wg': jax.random.normal(ks[5], (N_HEADS, D_MODEL), dtype=jnp.float32) * w, 'bg': jax.random.normal(ks[6], (N_HEADS,), dtype=jnp.float32) * 0.02}
    _L3_attn_b_in = _L3_attn_b_setup()

    def _L3_ffn_setup():
        import jax, jax.numpy as jnp
        import numpy as np
        H, I, E, K = (128, 64, 32, 8)
        B, S = (4, 128)

        def silu(x):
            return x * jax.nn.sigmoid(x)
        key = jax.random.key(seed)
        ks = jax.random.split(key, 14)

        def w(k, shape, fan_in):
            return jax.random.normal(k, shape, jnp.float32) / np.float32(np.sqrt(fan_in))
        return {'hidden_states': jax.random.normal(ks[0], (B, S, H), jnp.float32), 'Wr': w(ks[1], (H, E), H), 'br': jnp.zeros((E,), jnp.float32), 'Wg_s': w(ks[2], (H, I), H), 'bg_s': jnp.zeros((I,), jnp.float32), 'Wu_s': w(ks[3], (H, I), H), 'bu_s': jnp.zeros((I,), jnp.float32), 'Wd_s': w(ks[4], (I, H), I), 'bd_s': jnp.zeros((H,), jnp.float32), 'Wg': w(ks[5], (E, H, I), H), 'bg': jnp.zeros((E, I), jnp.float32), 'Wu': w(ks[6], (E, H, I), H), 'bu': jnp.zeros((E, I), jnp.float32), 'Wd': w(ks[7], (E, I, H), I), 'bd': jnp.zeros((E, H), jnp.float32)}
    _L3_ffn_in = _L3_ffn_setup()
    _d = {'L0_attn_a_x': _L0_attn_a_in['x'], 'L0_attn_a_w_wave': _L0_attn_a_in['w_wave'], 'L0_attn_a_b_wave': _L0_attn_a_in['b_wave'], 'L0_attn_a_w_query': _L0_attn_a_in['w_query'], 'L0_attn_a_b_query': _L0_attn_a_in['b_query'], 'L0_attn_a_key_weight': _L0_attn_a_in['key_weight'], 'L0_attn_a_w_se1': _L0_attn_a_in['w_se1'], 'L0_attn_a_b_se1': _L0_attn_a_in['b_se1'], 'L0_attn_a_w_se2': _L0_attn_a_in['w_se2'], 'L0_attn_a_b_se2': _L0_attn_a_in['b_se2'], 'L0_attn_a_w_out': _L0_attn_a_in['w_out'], 'L0_attn_b_W_in': _L0_attn_b_in['W_in'], 'L0_attn_b_W_A': _L0_attn_b_in['W_A'], 'L0_attn_b_W_B': _L0_attn_b_in['W_B'], 'L0_attn_b_W_C': _L0_attn_b_in['W_C'], 'L0_attn_b_W_out': _L0_attn_b_in['W_out'], 'L0_attn_b_norm_w': _L0_attn_b_in['norm_w'], 'L0_ffn_ln1_g': _L0_ffn_in['ln1_g'], 'L0_ffn_ln1_b': _L0_ffn_in['ln1_b'], 'L0_ffn_w_qkv': _L0_ffn_in['w_qkv'], 'L0_ffn_b_qkv': _L0_ffn_in['b_qkv'], 'L0_ffn_w_o': _L0_ffn_in['w_o'], 'L0_ffn_b_o': _L0_ffn_in['b_o'], 'L0_ffn_ln2_g': _L0_ffn_in['ln2_g'], 'L0_ffn_ln2_b': _L0_ffn_in['ln2_b'], 'L0_ffn_gate_w': _L0_ffn_in['gate_w'], 'L0_ffn_gate_b': _L0_ffn_in['gate_b'], 'L0_ffn_W1': _L0_ffn_in['W1'], 'L0_ffn_b1': _L0_ffn_in['b1'], 'L0_ffn_W2': _L0_ffn_in['W2'], 'L0_ffn_b2': _L0_ffn_in['b2'], 'L1_attn_a_norm_w': _L1_attn_a_in['norm_w'], 'L1_attn_a_skip_w': _L1_attn_a_in['skip_w'], 'L1_attn_a_in_w': _L1_attn_a_in['in_w'], 'L1_attn_a_conv_w': _L1_attn_a_in['conv_w'], 'L1_attn_a_conv_b': _L1_attn_a_in['conv_b'], 'L1_attn_a_wd1': _L1_attn_a_in['wd1'], 'L1_attn_a_wd2': _L1_attn_a_in['wd2'], 'L1_attn_a_wd2_b': _L1_attn_a_in['wd2_b'], 'L1_attn_a_wb': _L1_attn_a_in['wb'], 'L1_attn_a_wc': _L1_attn_a_in['wc'], 'L1_attn_a_A_log': _L1_attn_a_in['A_log'], 'L1_attn_a_W_D': _L1_attn_a_in['W_D'], 'L1_attn_a_out_w': _L1_attn_a_in['out_w'], 'L1_attn_b_norm_w': _L1_attn_b_in['norm_w'], 'L1_attn_b_norm_b': _L1_attn_b_in['norm_b'], 'L1_attn_b_in_w': _L1_attn_b_in['in_w'], 'L1_attn_b_in_b': _L1_attn_b_in['in_b'], 'L1_attn_b_conv_w': _L1_attn_b_in['conv_w'], 'L1_attn_b_conv_b': _L1_attn_b_in['conv_b'], 'L1_attn_b_xproj_w': _L1_attn_b_in['xproj_w'], 'L1_attn_b_A_log': _L1_attn_b_in['A_log'], 'L1_attn_b_D': _L1_attn_b_in['D'], 'L1_attn_b_out_w': _L1_attn_b_in['out_w'], 'L1_attn_b_out_b': _L1_attn_b_in['out_b'], 'L1_ffn_gate_w': _L1_ffn_in['gate_w'], 'L1_ffn_gate_b': _L1_ffn_in['gate_b'], 'L1_ffn_sw1': _L1_ffn_in['sw1'], 'L1_ffn_sb1': _L1_ffn_in['sb1'], 'L1_ffn_sw2': _L1_ffn_in['sw2'], 'L1_ffn_sb2': _L1_ffn_in['sb2'], 'L1_ffn_rw1': _L1_ffn_in['rw1'], 'L1_ffn_rb1': _L1_ffn_in['rb1'], 'L1_ffn_rw2': _L1_ffn_in['rw2'], 'L1_ffn_rb2': _L1_ffn_in['rb2'], 'L2_attn_a_attention_mask': _L2_attn_a_in['attention_mask'], 'L2_attn_a_ln_attn_g': _L2_attn_a_in['ln_attn_g'], 'L2_attn_a_ln_attn_b': _L2_attn_a_in['ln_attn_b'], 'L2_attn_a_Wq': _L2_attn_a_in['Wq'], 'L2_attn_a_bq': _L2_attn_a_in['bq'], 'L2_attn_a_Wk': _L2_attn_a_in['Wk'], 'L2_attn_a_bk': _L2_attn_a_in['bk'], 'L2_attn_a_Wv': _L2_attn_a_in['Wv'], 'L2_attn_a_bv': _L2_attn_a_in['bv'], 'L2_attn_a_ln_conv_g': _L2_attn_a_in['ln_conv_g'], 'L2_attn_a_ln_conv_b': _L2_attn_a_in['ln_conv_b'], 'L2_attn_a_conv_w': _L2_attn_a_in['conv_w'], 'L2_attn_a_conv_b': _L2_attn_a_in['conv_b'], 'L2_attn_a_ln_boom_g': _L2_attn_a_in['ln_boom_g'], 'L2_attn_a_ln_boom_b': _L2_attn_a_in['ln_boom_b'], 'L2_attn_a_Wb': _L2_attn_a_in['Wb'], 'L2_attn_a_bb': _L2_attn_a_in['bb'], 'L2_attn_a_Wu': _L2_attn_a_in['Wu'], 'L2_attn_a_bu': _L2_attn_a_in['bu'], 'L2_attn_b_W_qkv': _L2_attn_b_in['W_qkv'], 'L2_attn_b_b_qkv': _L2_attn_b_in['b_qkv'], 'L2_attn_b_W_out': _L2_attn_b_in['W_out'], 'L2_attn_b_b_out': _L2_attn_b_in['b_out'], 'L2_ffn_router_weight': _L2_ffn_in['router_weight'], 'L2_ffn_e_bias': _L2_ffn_in['e_bias'], 'L2_ffn_gate_w': _L2_ffn_in['gate_w'], 'L2_ffn_up_w': _L2_ffn_in['up_w'], 'L2_ffn_down_w': _L2_ffn_in['down_w'], 'L2_ffn_sh_gate_w': _L2_ffn_in['sh_gate_w'], 'L2_ffn_sh_up_w': _L2_ffn_in['sh_up_w'], 'L2_ffn_sh_down_w': _L2_ffn_in['sh_down_w'], 'L3_attn_a_g_ln': _L3_attn_a_in['g_ln'], 'L3_attn_a_Wq': _L3_attn_a_in['Wq'], 'L3_attn_a_Wkv': _L3_attn_a_in['Wkv'], 'L3_attn_a_Wo': _L3_attn_a_in['Wo'], 'L3_attn_b_Wq': _L3_attn_b_in['Wq'], 'L3_attn_b_Wk': _L3_attn_b_in['Wk'], 'L3_attn_b_Wv': _L3_attn_b_in['Wv'], 'L3_attn_b_Wo': _L3_attn_b_in['Wo'], 'L3_attn_b_Wg': _L3_attn_b_in['Wg'], 'L3_attn_b_bg': _L3_attn_b_in['bg'], 'L3_ffn_Wr': _L3_ffn_in['Wr'], 'L3_ffn_br': _L3_ffn_in['br'], 'L3_ffn_Wg_s': _L3_ffn_in['Wg_s'], 'L3_ffn_bg_s': _L3_ffn_in['bg_s'], 'L3_ffn_Wu_s': _L3_ffn_in['Wu_s'], 'L3_ffn_bu_s': _L3_ffn_in['bu_s'], 'L3_ffn_Wd_s': _L3_ffn_in['Wd_s'], 'L3_ffn_bd_s': _L3_ffn_in['bd_s'], 'L3_ffn_Wg': _L3_ffn_in['Wg'], 'L3_ffn_bg': _L3_ffn_in['bg'], 'L3_ffn_Wu': _L3_ffn_in['Wu'], 'L3_ffn_bu': _L3_ffn_in['bu'], 'L3_ffn_Wd': _L3_ffn_in['Wd'], 'L3_ffn_bd': _L3_ffn_in['bd']}
    _x0 = _d['L0_attn_a_x']
    _d['L0_attn_a_x'] = jax.random.normal(jax.random.fold_in(jax.random.key(seed), 1), (4, 1024, 128), dtype=_x0.dtype)
    del _x0
    return _d

def reference(L0_attn_a_x, L0_attn_a_w_wave, L0_attn_a_b_wave, L0_attn_a_w_query, L0_attn_a_b_query, L0_attn_a_key_weight, L0_attn_a_w_se1, L0_attn_a_b_se1, L0_attn_a_w_se2, L0_attn_a_b_se2, L0_attn_a_w_out, L0_attn_b_W_in, L0_attn_b_W_A, L0_attn_b_W_B, L0_attn_b_W_C, L0_attn_b_W_out, L0_attn_b_norm_w, L0_ffn_ln1_g, L0_ffn_ln1_b, L0_ffn_w_qkv, L0_ffn_b_qkv, L0_ffn_w_o, L0_ffn_b_o, L0_ffn_ln2_g, L0_ffn_ln2_b, L0_ffn_gate_w, L0_ffn_gate_b, L0_ffn_W1, L0_ffn_b1, L0_ffn_W2, L0_ffn_b2, L1_attn_a_norm_w, L1_attn_a_skip_w, L1_attn_a_in_w, L1_attn_a_conv_w, L1_attn_a_conv_b, L1_attn_a_wd1, L1_attn_a_wd2, L1_attn_a_wd2_b, L1_attn_a_wb, L1_attn_a_wc, L1_attn_a_A_log, L1_attn_a_W_D, L1_attn_a_out_w, L1_attn_b_norm_w, L1_attn_b_norm_b, L1_attn_b_in_w, L1_attn_b_in_b, L1_attn_b_conv_w, L1_attn_b_conv_b, L1_attn_b_xproj_w, L1_attn_b_A_log, L1_attn_b_D, L1_attn_b_out_w, L1_attn_b_out_b, L1_ffn_gate_w, L1_ffn_gate_b, L1_ffn_sw1, L1_ffn_sb1, L1_ffn_sw2, L1_ffn_sb2, L1_ffn_rw1, L1_ffn_rb1, L1_ffn_rw2, L1_ffn_rb2, L2_attn_a_attention_mask, L2_attn_a_ln_attn_g, L2_attn_a_ln_attn_b, L2_attn_a_Wq, L2_attn_a_bq, L2_attn_a_Wk, L2_attn_a_bk, L2_attn_a_Wv, L2_attn_a_bv, L2_attn_a_ln_conv_g, L2_attn_a_ln_conv_b, L2_attn_a_conv_w, L2_attn_a_conv_b, L2_attn_a_ln_boom_g, L2_attn_a_ln_boom_b, L2_attn_a_Wb, L2_attn_a_bb, L2_attn_a_Wu, L2_attn_a_bu, L2_attn_b_W_qkv, L2_attn_b_b_qkv, L2_attn_b_W_out, L2_attn_b_b_out, L2_ffn_router_weight, L2_ffn_e_bias, L2_ffn_gate_w, L2_ffn_up_w, L2_ffn_down_w, L2_ffn_sh_gate_w, L2_ffn_sh_up_w, L2_ffn_sh_down_w, L3_attn_a_g_ln, L3_attn_a_Wq, L3_attn_a_Wkv, L3_attn_a_Wo, L3_attn_b_Wq, L3_attn_b_Wk, L3_attn_b_Wv, L3_attn_b_Wo, L3_attn_b_Wg, L3_attn_b_bg, L3_ffn_Wr, L3_ffn_br, L3_ffn_Wg_s, L3_ffn_bg_s, L3_ffn_Wu_s, L3_ffn_bu_s, L3_ffn_Wd_s, L3_ffn_bd_s, L3_ffn_Wg, L3_ffn_bg, L3_ffn_Wu, L3_ffn_bu, L3_ffn_Wd, L3_ffn_bd):

    def _L0_attn_a_ref(x, w_wave, b_wave, w_query, b_query, key_weight, w_se1, b_se1, w_se2, b_se2, w_out):
        import jax, jax.numpy as jnp
        import numpy as np
        B, L, C = (2, 256, 128)
        H, POS = (8, 16)
        D = C // H
        MAXS = 32
        S = MAXS + 1
        MAX_FREQ, MIN_FREQ = (16.0, 1.0)
        SCALE = POS ** (-0.5)
        b, l, c = x.shape
        stride_grid = jnp.arange(-MAXS // 2, MAXS // 2 + 1, dtype=x.dtype)
        wp = jax.nn.silu(x @ w_wave + b_wave).reshape(b, l, 3, H)
        freq = jax.nn.sigmoid(wp[:, :, 0, :]) * (MAX_FREQ - MIN_FREQ) + MIN_FREQ
        phase = jnp.tanh(wp[:, :, 1, :]) * MAX_FREQ
        decay = jax.nn.sigmoid(wp[:, :, 2, :]) * 9.5 + 0.5
        freq_avg = freq.mean(-1)
        phase_avg = phase.mean(-1)
        decay_avg = decay.mean(-1)
        q = jax.nn.silu(x @ w_query + b_query).reshape(b, l, H, POS)
        centers = jnp.arange(l, dtype=x.dtype)
        sample_pos = centers[None, :, None] + stride_grid[None, None, :] * freq_avg[..., None] + phase_avg[..., None]
        valid = (sample_pos >= 0) & (sample_pos < l)
        idx = jnp.clip(sample_pos.astype(jnp.int32), 0, l - 1)
        values = jnp.take_along_axis(x[:, :, None, :], idx[:, :, :, None], axis=1)
        values = values.reshape(b, l, S, H, D).transpose(0, 1, 3, 2, 4)
        rel = jnp.abs(stride_grid)[None, None, None, :] * freq_avg[:, :, None, None]
        qk = jnp.einsum('blhd,d->blh', q, key_weight)
        scores = qk[..., None] * rel * SCALE
        env = jnp.exp(-rel / jnp.clip(decay_avg, 0.1, None)[:, :, None, None])
        mask = valid[:, :, None, :]
        scores = jnp.where(mask, scores, -jnp.inf)
        attn = jax.nn.softmax(scores, axis=-1) * env * mask.astype(x.dtype)
        attn = attn / (attn.sum(-1, keepdims=True) + 1e-08)
        out = jnp.einsum('blhsd,blhs->blhd', values, attn).reshape(b, l, c)
        se = jax.nn.sigmoid(jax.nn.silu(out @ w_se1 + b_se1) @ w_se2 + b_se2)
        out = out * se
        out = jax.nn.silu(out @ w_out)
        return out

    def _L0_attn_b_ref(x, W_in, W_A, W_B, W_C, W_out, norm_w):
        import jax, jax.numpy as jnp
        import numpy as np
        B, T, D_MODEL, N = (4, 256, 128, 16)
        D_INNER = 2 * D_MODEL

        def _ssm_scan(x_in, A, B_ssm, C_ssm):

            def step(state, ins):
                x_t, a_t, b_t, c_t = ins
                decay = jnp.exp(a_t)
                state = state * decay[:, None, :] + x_t[:, :, None] * b_t[:, None, :]
                out_t = (state * c_t[:, None, :]).sum(-1)
                return (state, out_t)
            b, t, d = x_in.shape
            n = A.shape[-1]
            init = jnp.zeros((b, d, n), dtype=x_in.dtype)
            xs = (jnp.swapaxes(x_in, 0, 1), jnp.swapaxes(A, 0, 1), jnp.swapaxes(B_ssm, 0, 1), jnp.swapaxes(C_ssm, 0, 1))
            _, outs = jax.lax.scan(step, init, xs)
            return jnp.swapaxes(outs, 0, 1)
        D = W_A.shape[0]
        xz = jnp.einsum('btm,md->btd', x, W_in)
        x_in = jax.nn.silu(xz[..., :D]) * jax.nn.sigmoid(xz[..., D:])
        A = -jnp.exp(jnp.clip(jnp.einsum('btd,dn->btn', x_in, W_A), -5.0, 0.0))
        B_ssm = jnp.einsum('btd,dn->btn', x_in, W_B)
        C_ssm = jnp.einsum('btd,dn->btn', x_in, W_C)
        out = _ssm_scan(x_in.astype(jnp.float32), A.astype(jnp.float32), B_ssm.astype(jnp.float32), C_ssm.astype(jnp.float32))
        out = out.astype(x.dtype)
        eps = jnp.finfo(jnp.float32).eps
        out = out * jax.lax.rsqrt(jnp.mean(out * out, axis=-1, keepdims=True) + eps) * norm_w
        return jnp.einsum('btd,dm->btm', out, W_out)

    def _L0_ffn_ref(x, ln1_g, ln1_b, w_qkv, b_qkv, w_o, b_o, ln2_g, ln2_b, gate_w, gate_b, W1, b1, W2, b2):
        import jax, jax.numpy as jnp
        import numpy as np
        D = 128
        H = 16
        DK = D // H
        E = 8
        DFF = 4 * D
        TOPK = 2
        EPS = 1e-05

        def _layernorm(x, g, b):
            m = jnp.mean(x, axis=-1, keepdims=True)
            v = jnp.mean(jnp.square(x - m), axis=-1, keepdims=True)
            return (x - m) * jax.lax.rsqrt(v + EPS) * g + b
        B, S, _ = x.shape
        h = _layernorm(x, ln1_g, ln1_b)
        qkv = h @ w_qkv + b_qkv
        q, k, v = jnp.split(qkv, 3, axis=-1)
        q = q.reshape(B, S, H, DK)
        k = k.reshape(B, S, H, DK)
        v = v.reshape(B, S, H, DK)
        scores = jnp.einsum('bqhd,bkhd->bhqk', q, k) / np.sqrt(DK)
        attn = jax.nn.softmax(scores, axis=-1)
        o = jnp.einsum('bhqk,bkhd->bqhd', attn, v).reshape(B, S, D)
        x = x + o @ w_o + b_o
        h = _layernorm(x, ln2_g, ln2_b).reshape(B * S, D)
        logits = h @ gate_w + gate_b
        topv, topi = jax.lax.top_k(logits, TOPK)
        gw = jax.nn.softmax(topv, axis=-1)
        ew = jnp.sum(jax.nn.one_hot(topi, E, dtype=h.dtype) * gw[..., None], axis=1)
        hid = jax.nn.relu(jnp.einsum('td,edf->etf', h, W1) + b1[:, None, :])
        out_e = jnp.einsum('etf,efd->etd', hid, W2) + b2[:, None, :]
        moe = jnp.einsum('etd,te->td', out_e, ew)
        return x + moe.reshape(B, S, D)

    def _L1_attn_a_ref(resid, norm_w, skip_w, in_w, conv_w, conv_b, wd1, wd2, wd2_b, wb, wc, A_log, W_D, out_w):
        import jax, jax.numpy as jnp
        import numpy as np
        D_MODEL, D_INNER, D_STATE, DT_RANK, D_CONV = (128, 256, 16, 64, 4)
        B, L = (2, 256)

        def _rmsnorm(x, w, eps=1e-05):
            return x * jax.lax.rsqrt(jnp.mean(x * x, axis=-1, keepdims=True) + eps) * w

        def _causal_depthwise_conv(x, conv_w, conv_b):
            K = conv_w.shape[1]
            xp = jnp.pad(x, ((0, 0), (K - 1, 0), (0, 0)))
            Lx = x.shape[1]
            out = conv_b
            for k in range(K):
                out = out + xp[:, k:k + Lx, :] * conv_w[:, k]
            return out

        def _selective_scan(x, delta, Bm, Cm, A):
            h0 = jnp.zeros((x.shape[0], A.shape[0], A.shape[1]), x.dtype)

            def step(h, inp):
                xt, dt, bt, ct = inp
                A_bar = jnp.exp(dt[..., None] * A)
                h = A_bar * h + (dt * xt)[..., None] * bt[:, None, :]
                y = jnp.einsum('ben,bn->be', h, ct)
                return (h, y)
            xs = tuple((jnp.swapaxes(a, 0, 1) for a in (x, delta, Bm, Cm)))
            _, ys = jax.lax.scan(step, h0, xs)
            return jnp.swapaxes(ys, 0, 1)
        x = _rmsnorm(resid, norm_w)
        skip = x @ skip_w.T
        x = x @ in_w.T
        x = _causal_depthwise_conv(x, conv_w, conv_b)
        x = jax.nn.silu(x)
        A = -jnp.exp(A_log)
        delta = jax.nn.softplus(x @ wd1.T @ wd2.T + wd2_b)
        Bm = x @ wb.T
        Cm = x @ wc.T
        y = _selective_scan(x, delta, Bm, Cm, A)
        y = y + x * W_D
        y = y * jax.nn.silu(skip)
        y = y @ out_w.T
        return resid + y

    def _L1_attn_b_ref(x, norm_w, norm_b, in_w, in_b, conv_w, conv_b, xproj_w, A_log, D, out_w, out_b):
        import jax, jax.numpy as jnp
        import numpy as np
        D_MODEL = 128
        D_STATE = 16
        D_CONV = 4
        D_INNER = 2 * D_MODEL
        B, T = (4, 512)
        EPS = 1e-05

        def _layernorm(x, w, b):
            mu = jnp.mean(x, axis=-1, keepdims=True)
            var = jnp.mean(jnp.square(x - mu), axis=-1, keepdims=True)
            return (x - mu) * jax.lax.rsqrt(var + EPS) * w + b

        def _silu(x):
            return x * jax.nn.sigmoid(x)
        residual = x
        xn = _layernorm(x, norm_w, norm_b)
        xz = xn @ in_w.T + in_b
        xi, z = jnp.split(xz, 2, axis=-1)
        xc = jax.lax.conv_general_dilated(jnp.transpose(xi, (0, 2, 1)), conv_w, window_strides=(1,), padding=[(D_CONV - 1, 0)], dimension_numbers=('NCH', 'OIH', 'NCH'), feature_group_count=D_INNER) + conv_b[None, :, None]
        xc = _silu(jnp.transpose(xc, (0, 2, 1)))
        xp = xc @ xproj_w.T
        C = xp[..., 1 + D_STATE:]
        gate = jax.nn.sigmoid(jnp.mean(C, axis=-1, keepdims=True))
        y = xc * gate + D * xc
        y = y * _silu(z)
        y = y @ out_w.T + out_b
        return y + residual

    def _L1_ffn_ref(x, gate_w, gate_b, sw1, sb1, sw2, sb2, rw1, rb1, rw2, rb2):
        import jax, jax.numpy as jnp
        import numpy as np
        D_MODEL = 128
        FFN = 128
        N_EXPERTS = 8
        N_SHARED = 1
        TOP_K = 2
        B, S = (2, 256)

        def _swiglu(h):
            a, b = jnp.split(h, 2, axis=-1)
            return jax.nn.silu(a) * b
        hs = jnp.einsum('bsd,ndf->nbsf', x, sw1) + sb1[:, None, None, :]
        shared_out = jnp.einsum('nbsf,nfd->bsd', _swiglu(hs), sw2) + sb2.sum(0)
        probs = jax.nn.softmax(x @ gate_w + gate_b, axis=-1)
        topk_probs, topk_idx = jax.lax.top_k(probs, TOP_K)
        cw = jnp.sum(jax.nn.one_hot(topk_idx, N_EXPERTS, dtype=x.dtype) * topk_probs[..., None], axis=2)
        hr = jnp.einsum('bsd,edf->ebsf', x, rw1) + rb1[:, None, None, :]
        out_e = jnp.einsum('ebsf,efd->ebsd', _swiglu(hr), rw2) + rb2[:, None, None, :]
        routed_out = jnp.einsum('ebsd,bse->bsd', out_e, cw)
        return shared_out + routed_out

    def _L2_attn_a_ref(hidden_states, attention_mask, ln_attn_g, ln_attn_b, Wq, bq, Wk, bk, Wv, bv, ln_conv_g, ln_conv_b, conv_w, conv_b, ln_boom_g, ln_boom_b, Wb, bb, Wu, bu):
        import jax, jax.numpy as jnp
        import numpy as np
        EPS = 1e-05

        def _ln(x, g, b):
            m = jnp.mean(x, axis=-1, keepdims=True)
            v = jnp.mean((x - m) ** 2, axis=-1, keepdims=True)
            return (x - m) * jax.lax.rsqrt(v + EPS) * g + b

        def _forward(x, ln_attn_g, ln_attn_b, Wq, bq, Wk, bk, Wv, bv, ln_conv_g, ln_conv_b, conv_w, conv_b, ln_boom_g, ln_boom_b, Wb, bb, Wu, bu):
            B, S, D = x.shape
            K = conv_w.shape[-1]
            G = D // conv_w.shape[1]
            h = _ln(x, ln_conv_g, ln_conv_b)
            hc = jnp.transpose(h, (0, 2, 1))
            hc = jnp.pad(hc, ((0, 0), (0, 0), (K - 1, 0)))
            conv = jax.lax.conv_general_dilated(hc, conv_w, window_strides=(1,), padding='VALID', dimension_numbers=('NCH', 'OIH', 'NCH'), feature_group_count=G)
            conv = conv + conv_b[None, :, None]
            x = x + jnp.transpose(conv, (0, 2, 1))
            h = _ln(x, ln_attn_g, ln_attn_b)
            q = jnp.einsum('bsd,ed->bse', h, Wq) + bq
            k = jnp.einsum('bsd,ed->bse', h, Wk) + bk
            v = jnp.einsum('bsd,ed->bse', h, Wv) + bv
            scale = jnp.arange(1, S + 1, dtype=x.dtype)[None, :, None]
            pooled_q = jnp.cumsum(q, axis=1) / scale
            pooled_k = jnp.cumsum(pooled_q * k, axis=1) / scale
            x = x + pooled_k * v
            h = _ln(x, ln_boom_g, ln_boom_b)
            h = jax.nn.gelu(jnp.einsum('bsd,ed->bse', h, Wb) + bb, approximate=False)
            h = jnp.einsum('bse,de->bsd', h, Wu) + bu
            return x + h
        return _forward(hidden_states, ln_attn_g, ln_attn_b, Wq, bq, Wk, bk, Wv, bv, ln_conv_g, ln_conv_b, conv_w, conv_b, ln_boom_g, ln_boom_b, Wb, bb, Wu, bu)

    def _L2_attn_b_ref(x, W_qkv, b_qkv, W_out, b_out):
        import jax, jax.numpy as jnp
        import numpy as np
        EMB = 128
        HEADS = 16
        HEAD_DIM = EMB // HEADS
        B, S = (2, 256)
        b = x.shape[0]
        qkv = jnp.einsum('bse,fe->bsf', x, W_qkv) + b_qkv
        qkv = qkv.reshape(b, HEADS, -1, 3 * HEAD_DIM)
        q, k, v = jnp.split(qkv, 3, axis=-1)
        score = jnp.einsum('bhqd,bhkd->bhqk', q, k) / np.sqrt(HEAD_DIM).astype(np.float32)
        weights = jax.nn.softmax(score, axis=-1)
        context = jnp.einsum('bhqk,bhkd->bhqd', weights, v)
        context = jnp.transpose(context, (0, 2, 1, 3)).reshape(b, -1, EMB)
        out = jnp.einsum('bse,fe->bsf', context, W_out) + b_out
        return out

    def _L2_ffn_ref(hidden_states, router_weight, e_bias, gate_w, up_w, down_w, sh_gate_w, sh_up_w, sh_down_w):
        import jax, jax.numpy as jnp
        import numpy as np
        B, S, H = (1, 256, 128)
        E, K = (16, 4)
        G, TG = (4, 2)
        I_MOE = 64
        N_SH = 2
        SCALE = 2.5

        def _mlp(x, gw, uw, dw):
            return jax.nn.silu(x @ gw.T) * (x @ uw.T) @ dw.T

        def _route(x2d, router_weight, e_bias):
            T = x2d.shape[0]
            scores = jax.nn.sigmoid(x2d @ router_weight.T)
            sc = scores + e_bias[None, :]
            group_scores = jnp.sum(jax.lax.top_k(sc.reshape(T, G, E // G), 2)[0], axis=-1)
            _, gidx = jax.lax.top_k(group_scores, TG)
            gmask = jnp.zeros((T, G), sc.dtype).at[jnp.arange(T)[:, None], gidx].set(1.0)
            smask = jnp.repeat(gmask, E // G, axis=1)
            masked = jnp.where(smask > 0, sc, 0.0)
            _, tidx = jax.lax.top_k(masked, K)
            tw = jnp.take_along_axis(scores, tidx, axis=1)
            tw = tw / (jnp.sum(tw, axis=-1, keepdims=True) + 1e-20)
            tw = tw * SCALE
            return (tidx, tw)

        def _moe_forward(hidden_states, router_weight, e_bias, gate_w, up_w, down_w, sh_gate_w, sh_up_w, sh_down_w):
            orig_shape = hidden_states.shape
            x = hidden_states.reshape(-1, H)
            T = x.shape[0]
            tidx, tw = _route(x, router_weight, e_bias)
            g = jnp.einsum('th,eih->tei', x, gate_w)
            u = jnp.einsum('th,eih->tei', x, up_w)
            h = jax.nn.silu(g) * u
            yo = jnp.einsum('tei,ehi->teh', h, down_w)
            combine = jnp.zeros((T, E), tw.dtype).at[jnp.arange(T)[:, None], tidx].add(tw)
            routed = jnp.einsum('te,teh->th', combine, yo)
            shared = _mlp(hidden_states.reshape(-1, H), sh_gate_w, sh_up_w, sh_down_w)
            return (routed + shared).reshape(orig_shape)
        return _moe_forward(hidden_states, router_weight, e_bias, gate_w, up_w, down_w, sh_gate_w, sh_up_w, sh_down_w)

    def _L3_attn_a_ref(x, g_ln, Wq, Wkv, Wo):
        import jax, jax.numpy as jnp
        import numpy as np
        B, N, D, H = (4, 256, 128, 16)
        DH = D // H
        EPS = 1e-05
        mu = jnp.mean(x, axis=-1, keepdims=True)
        var = jnp.mean(jnp.square(x - mu), axis=-1, keepdims=True)
        xn = (x - mu) * jax.lax.rsqrt(var + EPS) * g_ln
        b, n, d = xn.shape
        q = (xn @ Wq).reshape(b, n, H, DH).transpose(0, 2, 1, 3)
        kv = xn @ Wkv
        k, v = jnp.split(kv, 2, axis=-1)
        k = k.reshape(b, n, H, DH).transpose(0, 2, 1, 3)
        v = v.reshape(b, n, H, DH).transpose(0, 2, 1, 3)
        scale = DH ** (-0.5)
        dots = jnp.einsum('bhid,bhjd->bhij', q, k) * scale
        mask_value = -jnp.finfo(dots.dtype).max
        causal = jnp.triu(jnp.ones((n, n), dtype=bool), k=1)
        dots = jnp.where(causal, mask_value, dots)
        attn = jax.nn.softmax(dots.astype(jnp.float32), axis=-1).astype(dots.dtype)
        out = jnp.einsum('bhij,bhjd->bhid', attn, v)
        out = out.transpose(0, 2, 1, 3).reshape(b, n, d)
        return out @ Wo

    def _L3_attn_b_ref(x, Wq, Wk, Wv, Wo, Wg, bg):
        import jax, jax.numpy as jnp
        import numpy as np
        D_MODEL = 128
        N_HEADS = 16
        D_HEAD = D_MODEL // N_HEADS
        SCALE = 1.0 / np.sqrt(D_HEAD).astype(np.float32)

        def _feature_map(x):
            return jax.nn.elu(x) + 1.0
        b, s, _ = x.shape
        q = (x @ Wq.T).reshape(b, s, N_HEADS, D_HEAD)
        k = (x @ Wk.T).reshape(b, s, N_HEADS, D_HEAD)
        v = (x @ Wv.T).reshape(b, s, N_HEADS, D_HEAD)
        q = _feature_map(q * SCALE)
        k = _feature_map(k)
        gate = jax.nn.sigmoid(x @ Wg.T + bg)
        qt = jnp.moveaxis(q, 1, 0)
        kt = jnp.moveaxis(k, 1, 0)
        vt = jnp.moveaxis(v, 1, 0)
        gt = jnp.moveaxis(gate, 1, 0)
        S0 = jnp.zeros((b, N_HEADS, D_HEAD, D_HEAD), dtype=x.dtype)

        def step(S, inp):
            q_t, k_t, v_t, g_t = inp
            S = g_t[:, :, None, None] * S + k_t[..., :, None] * v_t[..., None, :]
            y_t = jnp.einsum('bhi,bhij->bhj', q_t, S)
            return (S, y_t)
        _, ys = jax.lax.scan(step, S0, (qt, kt, vt, gt))
        y = jnp.moveaxis(ys, 0, 1).reshape(b, s, D_MODEL)
        return y @ Wo.T

    def _L3_ffn_ref(hidden_states, Wr, br, Wg_s, bg_s, Wu_s, bu_s, Wd_s, bd_s, Wg, bg, Wu, bu, Wd, bd):
        import jax, jax.numpy as jnp
        import numpy as np
        H, I, E, K = (128, 64, 32, 8)
        B, S = (4, 128)

        def silu(x):
            return x * jax.nn.sigmoid(x)
        b, s, h = hidden_states.shape
        T = b * s
        x = hidden_states.reshape(T, h)
        logits = jnp.dot(x.astype(jnp.float32), Wr) + br
        aff = jax.nn.sigmoid(logits)
        top_v, top_i = jax.lax.top_k(aff, K)
        top_w = top_v / (jnp.sum(top_v, axis=-1, keepdims=True) + 1e-09)
        top_w = top_w.astype(hidden_states.dtype)
        e_total = Wr.shape[1]
        w_full = jnp.zeros((T, e_total), hidden_states.dtype)
        w_full = w_full.at[jnp.arange(T)[:, None], top_i].set(top_w)
        shared = jnp.dot(silu(jnp.dot(x, Wg_s) + bg_s) * (jnp.dot(x, Wu_s) + bu_s), Wd_s) + bd_s
        gate = silu(jnp.einsum('th,ehi->eti', x, Wg) + bg[:, None, :])
        up = jnp.einsum('th,ehi->eti', x, Wu) + bu[:, None, :]
        down = jnp.einsum('eti,eih->eth', gate * up, Wd) + bd[:, None, :]
        routed = jnp.einsum('te,eth->th', w_full, down)
        return (shared + routed).reshape(b, s, h)
    x = L0_attn_a_x
    x = x + _L0_attn_a_ref(_layernorm(x, axis=-1), L0_attn_a_w_wave, L0_attn_a_b_wave, L0_attn_a_w_query, L0_attn_a_b_query, L0_attn_a_key_weight, L0_attn_a_w_se1, L0_attn_a_b_se1, L0_attn_a_w_se2, L0_attn_a_b_se2, L0_attn_a_w_out)
    x = x + _L0_ffn_ref(_layernorm(x, axis=-1), L0_ffn_ln1_g, L0_ffn_ln1_b, L0_ffn_w_qkv, L0_ffn_b_qkv, L0_ffn_w_o, L0_ffn_b_o, L0_ffn_ln2_g, L0_ffn_ln2_b, L0_ffn_gate_w, L0_ffn_gate_b, L0_ffn_W1, L0_ffn_b1, L0_ffn_W2, L0_ffn_b2)
    x = x + _L0_attn_b_ref(_layernorm(x, axis=-1), L0_attn_b_W_in, L0_attn_b_W_A, L0_attn_b_W_B, L0_attn_b_W_C, L0_attn_b_W_out, L0_attn_b_norm_w)
    x = x + _L0_ffn_ref(_layernorm(x, axis=-1), L0_ffn_ln1_g, L0_ffn_ln1_b, L0_ffn_w_qkv, L0_ffn_b_qkv, L0_ffn_w_o, L0_ffn_b_o, L0_ffn_ln2_g, L0_ffn_ln2_b, L0_ffn_gate_w, L0_ffn_gate_b, L0_ffn_W1, L0_ffn_b1, L0_ffn_W2, L0_ffn_b2)
    x = x + _L1_attn_a_ref(_layernorm(x, axis=-1), L1_attn_a_norm_w, L1_attn_a_skip_w, L1_attn_a_in_w, L1_attn_a_conv_w, L1_attn_a_conv_b, L1_attn_a_wd1, L1_attn_a_wd2, L1_attn_a_wd2_b, L1_attn_a_wb, L1_attn_a_wc, L1_attn_a_A_log, L1_attn_a_W_D, L1_attn_a_out_w)
    x = x + _L1_ffn_ref(_layernorm(x, axis=-1), L1_ffn_gate_w, L1_ffn_gate_b, L1_ffn_sw1, L1_ffn_sb1, L1_ffn_sw2, L1_ffn_sb2, L1_ffn_rw1, L1_ffn_rb1, L1_ffn_rw2, L1_ffn_rb2)
    x = x + _L1_attn_b_ref(_layernorm(x, axis=-1), L1_attn_b_norm_w, L1_attn_b_norm_b, L1_attn_b_in_w, L1_attn_b_in_b, L1_attn_b_conv_w, L1_attn_b_conv_b, L1_attn_b_xproj_w, L1_attn_b_A_log, L1_attn_b_D, L1_attn_b_out_w, L1_attn_b_out_b)
    x = x + _L1_ffn_ref(_layernorm(x, axis=-1), L1_ffn_gate_w, L1_ffn_gate_b, L1_ffn_sw1, L1_ffn_sb1, L1_ffn_sw2, L1_ffn_sb2, L1_ffn_rw1, L1_ffn_rb1, L1_ffn_rw2, L1_ffn_rb2)
    x = x + _L2_attn_a_ref(_layernorm(x, axis=-1), L2_attn_a_attention_mask, L2_attn_a_ln_attn_g, L2_attn_a_ln_attn_b, L2_attn_a_Wq, L2_attn_a_bq, L2_attn_a_Wk, L2_attn_a_bk, L2_attn_a_Wv, L2_attn_a_bv, L2_attn_a_ln_conv_g, L2_attn_a_ln_conv_b, L2_attn_a_conv_w, L2_attn_a_conv_b, L2_attn_a_ln_boom_g, L2_attn_a_ln_boom_b, L2_attn_a_Wb, L2_attn_a_bb, L2_attn_a_Wu, L2_attn_a_bu)
    x = x + _L2_ffn_ref(_layernorm(x, axis=-1), L2_ffn_router_weight, L2_ffn_e_bias, L2_ffn_gate_w, L2_ffn_up_w, L2_ffn_down_w, L2_ffn_sh_gate_w, L2_ffn_sh_up_w, L2_ffn_sh_down_w)
    x = x + _L2_attn_b_ref(_layernorm(x, axis=-1), L2_attn_b_W_qkv, L2_attn_b_b_qkv, L2_attn_b_W_out, L2_attn_b_b_out)
    x = x + _L2_ffn_ref(_layernorm(x, axis=-1), L2_ffn_router_weight, L2_ffn_e_bias, L2_ffn_gate_w, L2_ffn_up_w, L2_ffn_down_w, L2_ffn_sh_gate_w, L2_ffn_sh_up_w, L2_ffn_sh_down_w)
    x = x + _L3_attn_a_ref(_layernorm(x, axis=-1), L3_attn_a_g_ln, L3_attn_a_Wq, L3_attn_a_Wkv, L3_attn_a_Wo)
    x = x + _L3_ffn_ref(_layernorm(x, axis=-1), L3_ffn_Wr, L3_ffn_br, L3_ffn_Wg_s, L3_ffn_bg_s, L3_ffn_Wu_s, L3_ffn_bu_s, L3_ffn_Wd_s, L3_ffn_bd_s, L3_ffn_Wg, L3_ffn_bg, L3_ffn_Wu, L3_ffn_bu, L3_ffn_Wd, L3_ffn_bd)
    x = x + _L3_attn_b_ref(_layernorm(x, axis=-1), L3_attn_b_Wq, L3_attn_b_Wk, L3_attn_b_Wv, L3_attn_b_Wo, L3_attn_b_Wg, L3_attn_b_bg)
    x = x + _L3_ffn_ref(_layernorm(x, axis=-1), L3_ffn_Wr, L3_ffn_br, L3_ffn_Wg_s, L3_ffn_bg_s, L3_ffn_Wu_s, L3_ffn_bu_s, L3_ffn_Wd_s, L3_ffn_bd_s, L3_ffn_Wg, L3_ffn_bg, L3_ffn_Wu, L3_ffn_bu, L3_ffn_Wd, L3_ffn_bd)
    return x

_drawn_inputs = setup_inputs


def setup_inputs(seed=0):
    import zlib

    import numpy as np

    out = dict(_drawn_inputs(seed))
    spreads = {'L0_attn_b_norm_w': (1.0, 0.6),
     'L0_ffn_ln1_g': (1.0, 0.2),
     'L0_ffn_ln1_b': (0.0, 0.1),
     'L0_ffn_b_qkv': (0.0, 0.1),
     'L0_ffn_b_o': (0.0, 0.1),
     'L0_ffn_ln2_g': (1.0, 0.2),
     'L0_ffn_ln2_b': (0.0, 0.1),
     'L0_ffn_gate_b': (0.0, 0.1),
     'L0_ffn_b1': (0.0, 0.1),
     'L0_ffn_b2': (0.0, 0.1),
     'L1_attn_a_norm_w': (1.0, 0.2),
     'L1_attn_a_conv_b': (0.0, 0.1),
     'L1_attn_a_wd2_b': (0.0, 0.779),
     'L1_attn_a_W_D': (1.0, 0.6),
     'L1_attn_b_norm_w': (1.0, 0.2),
     'L1_attn_b_norm_b': (0.0, 0.358),
     'L1_attn_b_in_b': (0.0, 0.357),
     'L1_attn_b_conv_b': (0.0, 0.594),
     'L1_attn_b_D': (1.0, 0.6),
     'L1_attn_b_out_b': (0.0, 0.1),
     'L1_ffn_gate_b': (0.0, 0.8),
     'L1_ffn_sb1': (0.0, 0.8),
     'L1_ffn_sb2': (0.0, 0.1),
     'L1_ffn_rb1': (0.0, 0.8),
     'L1_ffn_rb2': (0.0, 0.724),
     'L2_attn_a_ln_attn_g': (1.0, 0.6),
     'L2_attn_a_ln_attn_b': (0.0, 0.8),
     'L2_attn_a_bq': (0.0, 0.8),
     'L2_attn_a_bk': (0.0, 0.8),
     'L2_attn_a_bv': (0.0, 0.8),
     'L2_attn_a_ln_conv_g': (1.0, 0.6),
     'L2_attn_a_ln_conv_b': (0.0, 0.8),
     'L2_attn_a_conv_b': (0.0, 0.356),
     'L2_attn_a_ln_boom_g': (1.0, 0.6),
     'L2_attn_a_ln_boom_b': (0.0, 0.8),
     'L2_attn_a_bb': (0.0, 0.8),
     'L2_attn_a_bu': (0.0, 0.304),
     'L2_attn_b_b_qkv': (0.0, 0.8),
     'L2_attn_b_b_out': (0.0, 1.087),
     'L2_ffn_e_bias': (0.0, 0.8),
     'L3_attn_a_g_ln': (1.0, 0.6),
     'L3_ffn_br': (0.0, 2.0),
     'L3_ffn_bg_s': (0.0, 0.792),
     'L3_ffn_bu_s': (0.0, 0.674),
     'L3_ffn_bd_s': (0.0, 0.999),
     'L3_ffn_bg': (0.0, 2.0),
     'L3_ffn_bu': (0.0, 2.0),
     'L3_ffn_bd': (0.0, 2.0)}
    factors = {'L0_attn_a_b_wave': 2.903,
     'L0_attn_a_w_query': 8.0,
     'L0_attn_a_b_query': 8.0,
     'L0_attn_a_key_weight': 8.0,
     'L0_attn_a_w_se1': 8.0,
     'L0_attn_a_b_se1': 28.065,
     'L0_attn_a_w_se2': 8.0,
     'L0_attn_a_b_se2': 8.0,
     'L0_attn_b_W_A': 31.256,
     'L1_attn_b_xproj_w': 8.0,
     'L1_ffn_gate_w': 6.456,
     'L1_ffn_sw1': 8.0,
     'L1_ffn_sw2': 8.0,
     'L1_ffn_rw1': 8.0,
     'L1_ffn_rw2': 8.0,
     'L2_attn_a_Wq': 8.0,
     'L2_attn_a_Wk': 8.0,
     'L2_attn_a_Wv': 8.0,
     'L2_attn_a_Wb': 5.556,
     'L2_attn_a_Wu': 4.556,
     'L2_attn_b_W_qkv': 8.0,
     'L2_attn_b_W_out': 8.0,
     'L2_ffn_router_weight': 8.0,
     'L2_ffn_gate_w': 8.0,
     'L2_ffn_up_w': 8.0,
     'L2_ffn_down_w': 8.0,
     'L2_ffn_sh_gate_w': 8.0,
     'L2_ffn_sh_up_w': 8.0,
     'L2_ffn_sh_down_w': 8.0,
     'L3_attn_a_Wq': 8.0,
     'L3_attn_a_Wkv': 8.0,
     'L3_attn_a_Wo': 8.0,
     'L3_attn_b_bg': 8.0,
     'L3_ffn_Wg': 2.992,
     'L3_ffn_Wu': 2.905}
    for name, (base, spread) in spreads.items():
        noise = np.random.default_rng([zlib.crc32(name.encode()), seed]).standard_normal(out[name].shape)
        drawn = base * np.exp(spread * noise) if base else spread * noise
        out[name] = jnp.asarray(drawn.astype(out[name].dtype))
    for name, factor in factors.items():
        out[name] = (out[name] * factor).astype(out[name].dtype)
    return out
```

```python
from collections import namedtuple
from contextlib import ExitStack

import concourse.bass as bass
from concourse import mybir

F32 = mybir.dt.float32
BF16 = mybir.dt.bfloat16
I32 = mybir.dt.int32
U32 = mybir.dt.uint32
ALU = mybir.AluOpType
ACT = mybir.ActivationFunctionType
AX = mybir.AxisListType

BATCH, SEQ, C = 4, 1024, 128
TOKENS = BATCH * SEQ
TB = 512
NTB = TOKENS // TB


def semaphores(nc, stage, names):
    return namedtuple("Semaphores", names)(*(nc.alloc_semaphore(f"{stage}_{n}") for n in names.split()))


def release(nc, sems):
    nc.clear_and_free_semaphores(list(sems))
    nc.all_engine_barrier()


def column(vector):
    return vector.rearrange("(p a) -> p a", a=1)


def norm(nc, name, src, dst, eps, center=True, gain=None, shift=None):
    nt = len(src)
    with ExitStack() as ctx:
        def sb(n, shape):
            return ctx.enter_context(nc.sbuf_tensor(f"{name}_{n}", shape, F32))

        mean_ps = ctx.enter_context(nc.psum_tensor(f"{name}_mean", [128, 2, TB], F32))
        var_ps = ctx.enter_context(nc.psum_tensor(f"{name}_var", [128, 2, TB], F32))
        average = sb("average", [128, 128])
        eps_col = sb("eps", [128, 1])
        cen = sb("cen", [128, 2, TB])
        sq = sb("sq", [128, 2, nt, TB])
        std = sb("std", [128, 2, TB])
        rstd = sb("rstd", [128, 2, TB])
        par = sb("par", [128, 2, nt])
        s = semaphores(nc, name, "consts params mean centered squared var std_ready rstd_ready scaled")
        n_par = (gain is not None) + (shift is not None)
        block = ctx.enter_context(nc.Block())

        @block.sync
        def _(sp):
            for n, vector in enumerate((gain, shift)):
                if vector is not None:
                    with nc.allow_non_contiguous_dma("one value per partition"):
                        sp.dma_start(par[:, n, :], vector.rearrange("(t p) -> p t", p=128)).then_inc(s.params, 16)

        @block.gpsimd
        def _(pool):
            pool.memset(average[:], 1.0 / (128 * nt)).then_inc(s.consts, 1)
            pool.memset(eps_col[:], eps).then_inc(s.consts, 1)

        @block.tensor
        def _(pe):
            pe.wait_ge(s.consts, 2)
            with pe.Fori(0, NTB // 2) as i:
                for j in range(2):
                    if center:
                        pe.wait_ge(s.centered, i * 2 + j + 1)
                        nc.tensor.matmul(mean_ps[:, j, :], average[:], src[0][:, bass.ds(i * (2 * TB) + j * TB, TB)],
                                         start=True, stop=True).then_inc(s.mean, 1)
                for j in range(2):
                    pe.wait_ge(s.squared, i * 2 + j + 1)
                    pe.wait_ge(s.std_ready, i * 2 + j + 1)
                    for t in range(nt):
                        mm = nc.tensor.matmul(var_ps[:, j, :], average[:], sq[:, j, t, :],
                                              start=(t == 0), stop=(t == nt - 1))
                    mm.then_inc(s.var, 1)

        @block.scalar
        def _(act):
            act.sem_inc(s.std_ready, 2)
            act.wait_ge(s.consts, 2)
            if n_par:
                act.wait_ge(s.params, 16 * n_par)
            with act.Fori(0, NTB // 2) as i:
                for j in range(2):
                    tok = bass.ds(i * (2 * TB) + j * TB, TB)
                    if center:
                        act.wait_ge(s.centered, i * 2 + j + 3)
                    for t in range(nt):
                        a = nc.scalar.activation(sq[:, j, t, :], cen[:, j, :] if center else src[t][:, tok],
                                                 ACT.Square)
                    a.then_inc(s.squared, 1)
                for j in range(2):
                    act.wait_ge(s.var, i * 2 + j + 1)
                    act.wait_ge(s.rstd_ready, i * 2 + j + 1)
                    nc.scalar.activation(std[:, j, :], var_ps[:, j, :], ACT.Sqrt,
                                         bias=eps_col[:]).then_inc(s.std_ready, 1)
                if n_par:
                    for j in range(2):
                        tok = bass.ds(i * (2 * TB) + j * TB, TB)
                        act.wait_ge(s.scaled, i * 2 + j + 3)
                        act.nop(nofuse=True)
                        for t in range(nt):
                            nc.scalar.activation(dst[t][:, tok], dst[t][:, tok], ACT.Identity,
                                                 scale=par[:, 0, t:t + 1] if gain is not None else 1.0,
                                                 bias=par[:, 1, t:t + 1] if shift is not None else 0.0)

        @block.vector
        def _(dve):
            dve.sem_inc(s.centered, 2)
            dve.sem_inc(s.rstd_ready, 2)
            dve.sem_inc(s.scaled, 2)
            with dve.Fori(0, NTB // 2) as i:
                dve.wait_ge(s.scaled, i * 2 + 2)
                if center:
                    for j in range(2):
                        dve.wait_ge(s.mean, i * 2 + j + 1)
                        nc.vector.tensor_tensor(cen[:, j, :], src[0][:, bass.ds(i * (2 * TB) + j * TB, TB)],
                                                mean_ps[:, j, :], ALU.subtract).then_inc(s.centered, 1)
                for j in range(2):
                    tok = bass.ds(i * (2 * TB) + j * TB, TB)
                    dve.wait_ge(s.std_ready, i * 2 + j + 3)
                    nc.vector.reciprocal(rstd[:, j, :], std[:, j, :]).then_inc(s.rstd_ready, 1)
                    dve.wait_ge(s.rstd_ready, i * 2 + j + 3)
                    for t in range(nt):
                        v = nc.vector.tensor_tensor(dst[t][:, tok], cen[:, j, :] if center else src[t][:, tok],
                                                    rstd[:, j, :], ALU.mult)
                    v.then_inc(s.scaled, 1)
    release(nc, s)


MOE = {
    "L0": dict(E=8, F=512, shared=0, glu=False),
    "L1": dict(E=8, F=128, shared=128, glu=True),
    "L2": dict(E=16, F=64, shared=128, glu=True),
    "L3": dict(E=32, F=64, shared=64, glu=True),
}


def moe(nc, name, kind, h, x, w):
    cfg = MOE[kind]
    E, F, shared, glu = cfg["E"], cfg["F"], cfg["shared"], cfg["glu"]
    n_routed = E * F // 128
    tiles = ([-1] if shared else []) + list(range(n_routed))
    NT = len(tiles)
    SUB = TB // 128
    has_bias = w.get("bias_a") is not None
    has_down_bias = w.get("down_bias") is not None
    with ExitStack() as ctx:
        def sb(n, shape, dt=F32):
            return ctx.enter_context(nc.sbuf_tensor(f"{name}_{n}", shape, dt))

        def ps(n, shape):
            return ctx.enter_context(nc.psum_tensor(f"{name}_{n}", shape, F32))

        gate_ps = ps("gate_ps", [128, 2, TB])
        up_ps = ps("up_ps", [128, 2, TB]) if glu else None
        weight_ps = ps("weight_ps", [128, 2, TB])
        out_ps = ps("out_ps", [128, TB])
        route_ps = ps("route_ps", [128, TB])

        wa = sb("wa", [128, n_routed, 128])
        wb = sb("wb", [128, n_routed, 128]) if glu else None
        wd = sb("wd", [128, n_routed, 128])
        sa, sbb, sd = (sb("sa", [128, shared]), sb("sbb", [128, shared]), sb("sd", [shared, 128])) if shared else (None,) * 3
        ba, bb = sb("ba", [128, n_routed]), sb("bb", [128, n_routed])
        bsa, bsb, bsd = sb("bsa", [128, 1]), sb("bsb", [128, 1]), sb("bsd", [128, 1])
        bd = sb("bd", [E, 128])
        wr = sb("wr", [128, E])
        br = sb("br", [128, E])
        sel = sb("sel", [E, n_routed, 128])
        ident = sb("ident", [128, 128])
        hb = sb("hb", [128, TB])
        gated = sb("gated", [128, 2, TB])
        hid1 = sb("hid1", [128, 2, TB])
        hid = sb("hid", [128, 2, TB])
        wT = sb("wT", [E, TB])
        lg = sb("lg", [128, SUB, E])
        rt = sb("rt", [128, SUB, E])
        rw = sb("rw", [128, SUB, E])
        small = sb("small", [128, 4, SUB])
        if kind != "L3":
            later = sb("later", [128, E, E])
            cmp = sb("cmp", [128, SUB, E, E])
            tie = sb("tie", [128, SUB, E, E])
            rank = sb("rank", [128, SUB, E])
        if kind == "L2":
            grank = sb("grank", [128, SUB, 4])
            gsc = sb("gsc", [128, SUB, 4])
            masked = sb("masked", [128, SUB, E])
        top8 = sb("top8", [128, SUB, 8])
        s = semaphores(nc, name, "loads consts copied logits route expd weights wt_ps wt gate up gated_ready "
                                 "hid1_ready hid_ready wps out out_read chain")

        loads = []
        for tile, key in ((wa, "wa"), (wb, "wb"), (wd, "wd"), (sa, "sa"), (sbb, "sb"), (sd, "sd"), (wr, "wr")):
            if w.get(key) is not None:
                loads.append((tile[:], w[key]))
        if has_bias:
            loads.append((ba[:], w["bias_a"]))
            if glu:
                loads.append((bb[:], w["bias_b"]))
        if shared and w.get("bias_sa") is not None:
            loads += [(bsa[0:shared, :], w["bias_sa"]), (bsb[0:shared, :], w["bias_sb"])]
        if shared and w.get("bias_sd") is not None:
            loads.append((bsd[:], w["bias_sd"]))
        if has_down_bias:
            loads.append((bd[:], w["down_bias"]))
        if w.get("br") is not None:
            loads.append((br[:], w["br"].partition_broadcast(128)))
        shared_bias = shared and w.get("bias_sa") is not None

        block = ctx.enter_context(nc.Block())

        @block.sync
        def _(sp):
            with nc.allow_non_contiguous_dma("parameters, one value per partition"):
                for to, source in loads:
                    sp.dma_start(to, source).then_inc(s.loads, 16)

        @block.gpsimd
        def _(pool):
            pool.memset(ident[:], 0.0).then_inc(s.consts, 1)
            pool.memset(sel[:], 1.0).then_inc(s.consts, 1)
            n = 2
            if kind != "L3":
                pool.memset(later[:], 1.0).then_inc(s.consts, 1)
                n += 1
            pool.wait_ge(s.consts, n)
            pool.affine_select(out=ident[:], in_=ident[:], compare_op=ALU.not_equal, fill=1.0, base=0,
                               pattern=[[-1, 128]], channel_multiplier=1).then_inc(s.consts, 1)
            pool.affine_select(out=sel[:], in_=sel[:], compare_op=ALU.is_ge, fill=0.0, base=0,
                               pattern=[[128, n_routed], [1, 128]], channel_multiplier=-F).then_inc(s.consts, 1)
            pool.wait_ge(s.consts, n + 2)
            pool.affine_select(out=sel[:], in_=sel[:], compare_op=ALU.is_ge, fill=0.0, base=F - 1,
                               pattern=[[-128, n_routed], [-1, 128]], channel_multiplier=F).then_inc(s.consts, 1)
            if kind != "L3":
                pool.affine_select(out=later[:], in_=later[:], compare_op=ALU.is_gt, fill=0.0, base=0,
                                   pattern=[[1, E], [-1, E]], channel_multiplier=0).then_inc(s.consts, 1)

        CONSTS = 5 if kind == "L3" else 7

        @block.tensor
        def _(pe):
            pe.wait_ge(s.consts, CONSTS)
            pe.wait_ge(s.loads, 16 * len(loads))
            with pe.Fori(0, NTB) as b:
                pe.wait_ge(s.copied, b + 2)
                pe.wait_ge(s.wt, b + 1)
                for q in range(SUB):
                    mm = nc.tensor.matmul(route_ps[:, q * E:(q + 1) * E], hb[:, q * 128:(q + 1) * 128], wr[:],
                                          start=True, stop=True)
                mm.then_inc(s.logits, 1)

                def project(n):
                    t = tiles[n]
                    rows = shared if t < 0 else 128
                    pe.wait_ge(s.gated_ready, b * NT + n + 1)
                    nc.tensor.matmul(gate_ps[0:rows, n % 2, :], sa[:] if t < 0 else wa[:, t, :], hb[:],
                                     start=True, stop=True).then_inc(s.gate, 1)
                    if glu:
                        pe.wait_ge(s.hid1_ready, b * NT + n + 1)
                        nc.tensor.matmul(up_ps[0:rows, n % 2, :], sbb[:] if t < 0 else wb[:, t, :], hb[:],
                                         start=True, stop=True).then_inc(s.up, 1)

                def spread(n):
                    t = tiles[n]
                    if t >= 0:
                        pe.wait_ge(s.hid_ready, b * NT + n + 1)
                        nc.tensor.matmul(weight_ps[:, n % 2, :], sel[:, t, :], wT[:],
                                         start=True, stop=True).then_inc(s.wps, 1)

                def down(n):
                    t = tiles[n]
                    rows = shared if t < 0 else 128
                    pe.wait_ge(s.hid_ready, b * NT + n + 3)
                    last = n == NT - 1
                    mm = nc.tensor.matmul(out_ps[:], sd[:] if t < 0 else wd[:, t, :], hid[0:rows, n % 2, :],
                                          start=(n == 0 and not has_down_bias), stop=last)
                    return mm

                project(0)
                project(1)
                pe.wait_ge(s.weights, b + 1)
                for q in range(SUB):
                    mm = nc.tensor.transpose(route_ps[0:E, q * 128:(q + 1) * 128], rw[:, q, :], ident[:])
                mm.then_inc(s.wt_ps, 1)
                pe.wait_ge(s.wt, b + 2)
                spread(0)
                pe.wait_ge(s.out_read, b + 1)
                if has_down_bias:
                    nc.tensor.matmul(out_ps[:], bd[:], wT[:], start=True, stop=False)
                spread(1)
                for n in range(2, NT):
                    project(n)
                    down(n - 2)
                    spread(n)
                down(NT - 2)
                down(NT - 1).then_inc(s.out, 1)

        @block.scalar
        def _(act):
            act.sem_inc(s.copied, 1)
            act.sem_inc(s.wt, 1)
            act.sem_inc(s.gated_ready, 2)
            act.wait_ge(s.loads, 16 * len(loads))
            with act.Fori(0, NTB) as b:
                act.wait_ge(s.out_read, b + 1)
                nc.scalar.activation(hb[:], h[:, bass.ds(b * TB, TB)], ACT.Copy).then_inc(s.copied, 1)

                def gate(n):
                    t = tiles[n]
                    rows = shared if t < 0 else 128
                    act.wait_ge(s.gate, b * NT + n + 1)
                    act.wait_ge(s.hid1_ready, b * NT + n + 1)
                    bias = 0.0
                    if t < 0 and shared_bias:
                        bias = bsa[0:rows, :]
                    elif t >= 0 and has_bias:
                        bias = ba[:, t:t + 1]
                    nc.scalar.activation(gated[0:rows, n % 2, :], gate_ps[0:rows, n % 2, :],
                                         ACT.Silu if glu else ACT.Relu, bias=bias).then_inc(s.gated_ready, 1)

                if kind in ("L0", "L1"):
                    act.wait_ge(s.route, b + 1)
                    nc.scalar.activation(rt[:], lg[:], ACT.Exp).then_inc(s.expd, 1)
                else:
                    act.wait_ge(s.route, b + 1)
                    nc.scalar.activation(rt[:], lg[:], ACT.Sigmoid).then_inc(s.expd, 1)
                gate(0)
                gate(1)
                act.wait_ge(s.wt_ps, b + 1)
                nc.scalar.activation(wT[:], route_ps[0:E, :], ACT.Copy).then_inc(s.wt, 1)
                for n in range(2, NT):
                    gate(n)

        @block.vector
        def _(dve):
            dve.sem_inc(s.hid1_ready, 2)
            dve.sem_inc(s.hid_ready, 2)
            dve.sem_inc(s.out_read, 1)
            dve.wait_ge(s.loads, 16 * len(loads))
            dve.wait_ge(s.consts, CONSTS)
            with dve.Fori(0, NTB) as b:
                CH = {"L0": 10, "L1": 9, "L2": 24, "L3": 7}[kind]
                links = [0]

                def link(ins):
                    links[0] += 1
                    ins.then_inc(s.chain, 1)
                    dve.wait_ge(s.chain, b * CH + links[0])

                tt, V = nc.vector.tensor_tensor, nc.vector
                wide = lambda a: a.unsqueeze(2).to_broadcast([128, SUB, E])

                def rank_of(value, n, out, last=False):
                    groups = value.shape[1]
                    v_e = value.unsqueeze(3).to_broadcast([128, groups, n, n])
                    v_f = value.unsqueeze(2).to_broadcast([128, groups, n, n])
                    c = cmp[:].rearrange("p a b c -> p (a b c)")[:, 0:groups * n * n].rearrange(
                        "p (a b c) -> p a b c", a=groups, b=n)
                    u = tie[:].rearrange("p a b c -> p (a b c)")[:, 0:groups * n * n].rearrange(
                        "p (a b c) -> p a b c", a=groups, b=n)
                    tt(c, v_f, v_e, ALU.is_gt)
                    link(tt(u, v_f, v_e, ALU.is_equal))
                    link(tt(u, u, later[:, 0:n, 0:n].unsqueeze(1).to_broadcast([128, groups, n, n]), ALU.mult))
                    link(tt(c, c, u, ALU.add))
                    link(V.tensor_reduce(out, c, AX.X, ALU.add))

                dve.wait_ge(s.logits, b + 1)
                product = route_ps[:, 0:SUB * E].rearrange("p (q e) -> p q e", q=SUB)
                if w.get("br") is not None and kind != "L2":
                    add = tt(lg[:], product, br[:].unsqueeze(1).to_broadcast([128, SUB, E]), ALU.add)
                else:
                    add = V.tensor_copy(lg[:], product)
                if kind in ("L0", "L1"):
                    link(add)
                    link(V.tensor_reduce(small[:, 0, :], lg[:], AX.X, ALU.max))
                    tt(lg[:], lg[:], wide(small[:, 0, :]), ALU.subtract).then_inc(s.route, 1)
                    dve.wait_ge(s.route, b + 1)
                    rank_of(lg[:], E, rank[:])
                    link(V.tensor_scalar(rw[:], rank[:], 2.0, None, ALU.is_lt))
                    dve.wait_ge(s.expd, b + 1)
                    if kind == "L0":
                        link(tt(rw[:], rw[:], rt[:], ALU.mult))
                        link(V.tensor_reduce(small[:, 1, :], rw[:], AX.X, ALU.add))
                        link(V.reciprocal(small[:, 2, :], small[:, 1, :]))
                    else:
                        V.tensor_reduce(small[:, 1, :], rt[:], AX.X, ALU.add)
                        link(tt(rw[:], rw[:], rt[:], ALU.mult))
                        link(V.reciprocal(small[:, 2, :], small[:, 1, :]))
                    tt(rw[:], rw[:], wide(small[:, 2, :]), ALU.mult).then_inc(s.weights, 1)
                elif kind == "L3":
                    add.then_inc(s.route, 1)
                    dve.wait_ge(s.expd, b + 1)
                    dve.nop(nofuse=True)
                    for q in range(SUB):
                        last = V.max(top8[:, q, :], rt[:, q, :])
                    link(last)
                    dve.nop(nofuse=True)
                    for q in range(SUB):
                        last = V.match_replace(rw[:, q, :], top8[:, q, :], rt[:, q, :], -1.0)
                    link(last)
                    link(V.tensor_scalar(rw[:], rw[:], 0.0, None, ALU.is_lt))
                    link(tt(rw[:], rw[:], rt[:], ALU.mult))
                    link(V.tensor_reduce(small[:, 0, :], top8[:], AX.X, ALU.add))
                    link(V.tensor_scalar(small[:, 1, :], small[:, 0, :], 1e-9, None, ALU.add))
                    link(V.reciprocal(small[:, 2, :], small[:, 1, :]))
                    tt(rw[:], rw[:], wide(small[:, 2, :]), ALU.mult).then_inc(s.weights, 1)
                else:
                    add.then_inc(s.route, 1)
                    dve.wait_ge(s.expd, b + 1)
                    link(tt(lg[:], rt[:], br[:].unsqueeze(1).to_broadcast([128, SUB, E]), ALU.add))
                    grouped = lg[:].rearrange("p q (g e) -> p (q g) e", g=4)
                    rank4 = rank[:].rearrange("p q (g e) -> p (q g) e", g=4)
                    rank_of(grouped, 4, rank4)
                    link(V.tensor_scalar(masked[:], rank[:], 2.0, None, ALU.is_lt))
                    link(tt(masked[:], masked[:], lg[:], ALU.mult))
                    link(V.tensor_reduce(gsc[:].rearrange("p q g -> p (q g)"),
                                         masked[:].rearrange("p q (g e) -> p (q g) e", g=4), AX.X, ALU.add))
                    rank_of(gsc[:], 4, grank[:])
                    link(V.tensor_scalar(grank[:], grank[:], 2.0, None, ALU.is_lt))
                    link(tt(masked[:].rearrange("p q (g e) -> p (q g) e", g=4), grouped,
                            grank[:].rearrange("p q g -> p (q g)").unsqueeze(2).to_broadcast([128, 4 * SUB, 4]),
                            ALU.mult))
                    rank_of(masked[:], E, rank[:])
                    link(V.tensor_scalar(rw[:], rank[:], 4.0, None, ALU.is_lt))
                    link(tt(rw[:], rw[:], rt[:], ALU.mult))
                    link(V.tensor_reduce(small[:, 0, :], rw[:], AX.X, ALU.add))
                    link(V.tensor_scalar(small[:, 1, :], small[:, 0, :], 1e-20, None, ALU.add))
                    link(V.reciprocal(small[:, 2, :], small[:, 1, :]))
                    link(tt(rw[:], rw[:], wide(small[:, 2, :]), ALU.mult))
                    V.tensor_scalar(rw[:], rw[:], 2.5, None, ALU.mult).then_inc(s.weights, 1)
                assert links[0] == CH, (kind, links[0])

                for n, t in enumerate(tiles):
                    rows = shared if t < 0 else 128
                    dve.wait_ge(s.gated_ready, b * NT + n + 3)
                    if glu:
                        dve.wait_ge(s.up, b * NT + n + 1)
                    bias = 0.0
                    if t < 0 and shared_bias:
                        bias = bsb[0:rows, :]
                    elif t >= 0 and has_bias and glu:
                        bias = bb[:, t:t + 1]
                    if t < 0:
                        V.scalar_tensor_tensor(out=hid[0:rows, n % 2, :], in0=up_ps[0:rows, n % 2, :], scalar=bias,
                                               in1=gated[0:rows, n % 2, :], op0=ALU.add,
                                               op1=ALU.mult).then_inc(s.hid1_ready, 1)
                        dve.wait_ge(s.hid1_ready, b * NT + n + 3)
                        dve.sem_inc(s.hid_ready, 1)
                        continue
                    if glu:
                        V.scalar_tensor_tensor(out=hid1[:, n % 2, :], in0=up_ps[:, n % 2, :], scalar=bias,
                                               in1=gated[:, n % 2, :], op0=ALU.add,
                                               op1=ALU.mult).then_inc(s.hid1_ready, 1)
                        dve.wait_ge(s.hid1_ready, b * NT + n + 3)
                    routed = n - (1 if shared else 0)
                    dve.wait_ge(s.wps, b * n_routed + routed + 1)
                    if glu:
                        V.tensor_tensor(hid[:, n % 2, :], hid1[:, n % 2, :], weight_ps[:, n % 2, :],
                                        ALU.mult).then_inc(s.hid_ready, 1)
                    else:
                        V.tensor_tensor(hid[:, n % 2, :], gated[:, n % 2, :], weight_ps[:, n % 2, :],
                                        ALU.mult).then_inc(s.hid_ready, 1)
                        dve.wait_ge(s.hid_ready, b * NT + n + 3)
                        dve.sem_inc(s.hid1_ready, 1)
                dve.wait_ge(s.out, b + 1)
                tok = bass.ds(b * TB, TB)
                if shared and w.get("bias_sd") is not None:
                    V.scalar_tensor_tensor(out=x[:, tok], in0=out_ps[:], scalar=bsd[:], in1=x[:, tok],
                                           op0=ALU.add, op1=ALU.add).then_inc(s.out_read, 1)
                else:
                    V.tensor_tensor(x[:, tok], x[:, tok], out_ps[:], ALU.add).then_inc(s.out_read, 1)
    release(nc, s)


HEADS, DH = 16, 8
PARTS = 3
STACK = PARTS * PARTS * DH
MAXROW = 96
NEG = -1.0e30


def attention_inputs(nc, name, h, scratch, v_all, w):
    inter, bias = w["interleaved"], w.get("bq") is not None
    with ExitStack() as ctx:
        def sb(n, shape, dt=F32):
            return ctx.enter_context(nc.sbuf_tensor(f"{name}_{n}", shape, dt))

        qk_ps = ctx.enter_context(nc.psum_tensor(f"{name}_qk_ps", [128, 2, TB], F32))
        v_ps = ctx.enter_context(nc.psum_tensor(f"{name}_v_ps", [128, TB], F32))
        wqk = sb("wqk", [128, 2, 128])
        wv = sb("wv", [128, 128])
        bqk = sb("bqk", [128, 2])
        bv = sb("bv", [128, 128])
        hb = sb("hb", [128, TB])
        full = sb("full", [128, 2, TB])
        rest = sb("rest", [128, 2, TB])
        rest2 = sb("rest2", [128, 2, TB])
        part = [sb(f"part{n}", [128, 2, TB], BF16) for n in range(PARTS)]
        s = semaphores(nc, name, "loads ones copied qk v full_ready part1 rest_ready part2 rest2_ready part3 "
                                 "v_read written")
        loads = [(wqk[:, 0, :], w["wq"]), (wqk[:, 1, :], w["wk"]), (wv[:], w["wv"])]
        if bias:
            loads += [(bqk[:, 0:1], column(w["bq"])), (bqk[:, 1:2], column(w["bk"]))]
            if inter:
                loads += [(bv[64 * r:64 * r + 64, 0:64], w["bv"][r].partition_broadcast(64)) for r in range(2)]
            else:
                loads.append((bv[:], w["bv"].partition_broadcast(128)))
        OUT = 16 * 2 * PARTS
        block = ctx.enter_context(nc.Block())

        @block.sync
        def _(sp):
            sp.sem_inc(s.written, 1)
            with nc.allow_non_contiguous_dma("biases, one value per partition"):
                for to, source in loads:
                    sp.dma_start(to, source).then_inc(s.loads, 16)
            with sp.Fori(0, BATCH) as b:
                for j in range(2):
                    for n, ready in enumerate((s.part1, s.part2, s.part3)):
                        sp.wait_ge(ready, b * 2 + j + 2)
                        for z in range(2):
                            if inter:
                                to = scratch[z, n, bass.ds(b * HEADS + j * 8, 8)].rearrange(
                                    "e d (u t) -> (d u) e t", u=16)
                                source = part[n][:, z, :].rearrange("p (e t) -> p e t", e=8)
                            else:
                                to = scratch[z, n, bass.ds(b * HEADS, HEADS)].rearrange(
                                    "e d p -> (e d) p")[:, j * TB:(j + 1) * TB]
                                source = part[n][:, z, :]
                            sp.dma_start(to, source).then_inc(s.written, 16)
            sp.wait_ge(s.written, OUT * NTB + 1)

        @block.gpsimd
        def _(pool):
            pool.memset(v_all[:, :, :, DH:DH + 1], 1.0).then_inc(s.ones, 1)
            pool.sem_inc(s.rest_ready, 1)
            pool.sem_inc(s.rest2_ready, 1)
            with pool.Fori(0, BATCH) as b:
                for j in range(2):
                    k = b * 2 + j
                    pool.wait_ge(s.part1, k + 2)
                    pool.wait_ge(s.rest2_ready, k + 1)
                    nc.gpsimd.tensor_tensor(rest[:], full[:], part[0][:], ALU.subtract).then_inc(s.rest_ready, 1)
                    pool.wait_ge(s.part2, k + 2)
                    pool.wait_ge(s.part3, k + 1)
                    pool.wait_ge(s.rest_ready, k + 2)
                    nc.gpsimd.tensor_tensor(rest2[:], rest[:], part[1][:], ALU.subtract).then_inc(s.rest2_ready, 1)

        @block.tensor
        def _(pe):
            pe.wait_ge(s.loads, 16 * len(loads))
            with pe.Fori(0, BATCH) as b:
                for j in range(2):
                    k = b * 2 + j
                    pe.wait_ge(s.copied, k + 2)
                    pe.wait_ge(s.full_ready, k + 1)
                    for z in range(2):
                        mm = nc.tensor.matmul(qk_ps[:, z, :], wqk[:, z, :], hb[:], start=True, stop=True)
                    mm.then_inc(s.qk, 1)
                    pe.wait_ge(s.v_read, k + 1)
                    if inter:
                        for e in range(8):
                            for r in range(2):
                                mm = nc.tensor.matmul(v_ps[64 * r:64 * r + 64, e * 64:(e + 1) * 64],
                                                      hb[:, e * 64:(e + 1) * 64], wv[:, r * 64:(r + 1) * 64],
                                                      start=True, stop=True)
                    else:
                        for q in range(4):
                            mm = nc.tensor.matmul(v_ps[:, q * 128:(q + 1) * 128], hb[:, q * 128:(q + 1) * 128],
                                                  wv[:], start=True, stop=True)
                    mm.then_inc(s.v, 1)

        @block.scalar
        def _(act):
            for sem in (s.copied, s.full_ready, s.part1):
                act.sem_inc(sem, 1)
            act.wait_ge(s.loads, 16 * len(loads))
            with act.Fori(0, BATCH) as b:
                for j in range(2):
                    k = b * 2 + j
                    act.wait_ge(s.v_read, k + 1)
                    nc.scalar.activation(hb[:], h[:, bass.ds(b * SEQ + j * TB, TB)], ACT.Copy).then_inc(s.copied, 1)
                    act.wait_ge(s.qk, k + 1)
                    act.wait_ge(s.rest_ready, k + 1)
                    act.wait_ge(s.part1, k + 1)
                    for z in range(2):
                        a = nc.scalar.activation(full[:, z, :], qk_ps[:, z, :], ACT.Identity,
                                                 bias=bqk[:, z:z + 1] if bias else 0.0)
                    a.then_inc(s.full_ready, 1)
                    act.wait_ge(s.full_ready, k + 2)
                    act.wait_ge(s.written, k * OUT + 1)
                    nc.scalar.activation(part[0][:], full[:], ACT.Copy).then_inc(s.part1, 1)

        @block.vector
        def _(dve):
            for sem in (s.v_read, s.part2, s.part3):
                dve.sem_inc(sem, 1)
            dve.wait_ge(s.loads, 16 * len(loads))
            dve.wait_ge(s.ones, 1)
            with dve.Fori(0, BATCH) as b:
                for j in range(2):
                    k = b * 2 + j
                    dve.wait_ge(s.v, k + 1)
                    if inter:
                        to = v_all[:, bass.ds(b * HEADS + j * 8, 8), :, 0:DH]
                        source = v_ps[:].rearrange("p (e k d) -> p e k d", e=8, k=8)
                        more = bv[:, 0:64].rearrange("p (k d) -> p k d", k=8).unsqueeze(1).to_broadcast([128, 8, 8, DH])
                        v = nc.vector.tensor_tensor(to, source, more, ALU.add)
                    else:
                        for q in range(4):
                            to = v_all[:, bass.ds(b * HEADS, HEADS), j * 4 + q, 0:DH]
                            source = v_ps[:, q * 128:(q + 1) * 128].rearrange("p (h d) -> p h d", d=DH)
                            if bias:
                                v = nc.vector.tensor_tensor(to, source, bv[:].rearrange("p (h d) -> p h d", d=DH),
                                                            ALU.add)
                            else:
                                v = nc.vector.tensor_copy(to, source)
                    v.then_inc(s.v_read, 1)
                    dve.wait_ge(s.rest_ready, k + 2)
                    dve.wait_ge(s.written, k * OUT + 1)
                    nc.vector.tensor_copy(part[1][:], rest[:]).then_inc(s.part2, 1)
                    dve.wait_ge(s.rest2_ready, k + 2)
                    nc.vector.tensor_copy(part[2][:], rest2[:]).then_inc(s.part3, 1)
    release(nc, s)


def attention(nc, name, scratch, v_all, target, w):
    causal, inter = w["causal"], w["interleaved"]
    GROUPS = BATCH * HEADS // 4
    SCALE = float(DH) ** -0.5
    with ExitStack() as ctx:
        def sb(n, shape, dt=F32):
            return ctx.enter_context(nc.sbuf_tensor(f"{name}_{n}", shape, dt))

        def ps(n, shape):
            return ctx.enter_context(nc.psum_tensor(f"{name}_{n}", shape, F32))

        s_ps = ps("s_ps", [128, 2, 2, TB])
        max_ps = ps("max_ps", [128, 2, TB])
        o_ps = ps("o_ps", [128, TB])
        y_ps = ps("y_ps", [128, TB])
        qs = sb("qs", [128, 2, 4, SEQ], BF16)
        ks = sb("ks", [128, 2, 4, SEQ], BF16)
        vg = sb("vg", [128, 2, 4, 8, DH + 1])
        prob = sb("prob", [128, 2, 2, TB])
        halves = sb("halves", [128, 2, 16, 2])
        nmax = sb("nmax", [128, 16])
        nrest = sb("nrest", [128, 16])
        nrest2 = sb("nrest2", [128, 16])
        nparts = sb("nparts", [128, 16, PARTS], BF16)
        wo = sb("wo", [128, 4, 128])
        bo = sb("bo", [128, 1])
        total = sb("total", [128, 128])
        ident_bf = sb("ident_bf", [128, 128], BF16)
        zero_bf = sb("zero_bf", [128, TB], BF16)
        o_sb = sb("o_sb", [128, TB])
        inv = sb("inv", [128, TB])
        on = sb("on", [128, TB])
        mask_k = sb("mask_k", [128, 896], BF16) if causal else None
        mask_q = sb("mask_q", [128, 896], BF16) if causal else None
        s = semaphores(nc, name, "loads consts ones stacks0 stacks1 stack_used mx mx_read chain rows_ps rows vg_ready "
                                 "sc prob_ready pv o_copied sums inv_ready on_ready y y_read zeroed")
        stacks = (s.stacks0, s.stacks1)
        bias = w.get("bo") is not None
        LOADS = 16 * (16 + bias)
        STACKS = 16 * 4 * 6

        def units(half):
            return [(j, p) for j in range(4) for p in range(4) if not (causal and half == 0 and p >= 2)]

        def maxima(half):
            return [(j, half * 4 + q, kh) for j in range(4) for q in range(4) for kh in range(2)
                    if not (causal and kh == 1 and half == 0)]

        def shared(half, n):
            nm = len(maxima(1 - half))
            return min(nm, -(-nm * (n + 1) // (len(units(half)) - 4)))

        SUMS_AT, PROJECT_AT = (1, 4)
        NU = len(units(0)) + len(units(1))
        NM = len(maxima(0)) + len(maxima(1))
        block = ctx.enter_context(nc.Block())

        @block.sync
        def _(sp):
            with nc.allow_non_contiguous_dma("rows of heads of 8"):
                for g in range(4):
                    for j in range(4):
                        r = (4 * g + j) * DH
                        if g == 0 and j == 0:
                            sp.wait_ge(s.zeroed, 3)
                        sp.dma_start(wo[32 * j:32 * j + DH, g, :], w["wo"][r:r + DH, :]).then_inc(s.loads, 16)
                if bias:
                    sp.dma_start(bo[:], column(w["bo"])).then_inc(s.loads, 16)
            sp.sem_inc(s.stack_used, 2)
            with sp.Fori(0, GROUPS // 2) as i:
                for z in range(2):
                    sp.wait_ge(s.stack_used, i * 2 + z + 1)
                    for j in range(4):
                        head = bass.ds(i * 8 + z * 4 + j, 1)
                        for n in range(PARTS):
                            r = n * PARTS * DH
                            sp.dma_start(qs[r:r + 24, z, j, :],
                                         scratch[0, n:n + 1, head].rearrange("n e d p -> (n e) d p").to_broadcast(
                                             [PARTS, DH, SEQ])).then_inc(stacks[z], 16)
                            sp.dma_start(ks[r:r + 24, z, j, :],
                                         scratch[1, :, head].rearrange("n e d p -> (n e) d p")).then_inc(stacks[z], 16)

        @block.gpsimd
        def _(pool):
            pool.memset(wo[:], 0.0).then_inc(s.zeroed, 1)
            pool.memset(qs[:], 0.0).then_inc(s.zeroed, 1)
            pool.memset(ks[:], 0.0).then_inc(s.zeroed, 1)
            pool.memset(total[:], 0.0).then_inc(s.consts, 1)
            pool.memset(zero_bf[:], 0.0).then_inc(s.consts, 1)
            pool.memset(ident_bf[:], 0.0).then_inc(s.consts, 1)
            n = 3
            if causal:
                pool.memset(mask_k[:], 0.0).then_inc(s.consts, 1)
                pool.memset(mask_q[:], 0.0).then_inc(s.consts, 1)
                n = 5
            pool.wait_ge(s.consts, n)
            pool.affine_select(out=total[:].rearrange("p (j d) -> p j d", j=4), in_=total[:].rearrange(
                "p (j d) -> p j d", j=4), compare_op=ALU.not_equal, fill=1.0, base=-DH,
                pattern=[[-32, 4], [0, 32]], channel_multiplier=1).then_inc(s.consts, 1)
            pool.affine_select(out=ident_bf[:], in_=ident_bf[:], compare_op=ALU.not_equal, fill=1.0, base=0,
                               pattern=[[-1, 128]], channel_multiplier=1).then_inc(s.consts, 1)
            if causal:
                pool.affine_select(out=mask_k[:], in_=mask_k[:], compare_op=ALU.is_ge, fill=NEG, base=-384,
                                   pattern=[[1, 896]], channel_multiplier=-1).then_inc(s.consts, 1)
                pool.affine_select(out=mask_q[:], in_=mask_q[:], compare_op=ALU.is_ge, fill=NEG, base=384,
                                   pattern=[[-1, 896]], channel_multiplier=1).then_inc(s.consts, 1)
            pool.sem_inc(s.vg_ready, 2)
            with pool.Fori(0, GROUPS // 2) as i:
                for z in range(2):
                    pool.wait_ge(s.stack_used, i * 2 + z + 1)
                    nc.gpsimd.tensor_copy(vg[:, z], v_all[:, bass.ds(i * 8 + z * 4, 4)]).then_inc(s.vg_ready, 1)

        CONSTS = 9 if causal else 5

        @block.tensor
        def _(pe):
            pe.wait_ge(s.consts, CONSTS)
            pe.wait_ge(s.ones, 1)
            pe.wait_ge(s.loads, LOADS)
            nc.tensor.matmul(o_ps[:], zero_bf[:, 0:128], zero_bf[:], start=True, stop=True).then_inc(
                s.pv, 1)

            def maximum(G, z, half, n):
                j, q, kh = maxima(half)[n]
                k = n + (len(maxima(0)) if half else 0)
                pe.wait_ge(s.mx_read, G * NM + k + 1)
                out = max_ps[:, n % 2, :]
                diagonal = causal and kh == q // 4
                if diagonal:
                    off = (q % 4) * 128
                    nc.tensor.matmul(out, ident_bf[:], mask_q[:, 384 - off:896 - off], start=True, stop=False)
                nc.tensor.matmul(out, qs[0:STACK, z, j, q * 128:(q + 1) * 128],
                                 ks[0:STACK, z, j, kh * TB:(kh + 1) * TB],
                                 start=not diagonal, stop=True).then_inc(s.mx, 1)

            def turn(G, half, j2):
                if j2 == 0:
                    pe.wait_ge(s.chain, (G * 2 + half) * 5 + 5)
                pe.wait_ge(s.rows, (G * 2 + half) * 2 + j2 + 1)
                for jj in range(2):
                    for q in range(4):
                        mm = nc.tensor.matmul(max_ps[MAXROW:MAXROW + PARTS, jj, q * 128:(q + 1) * 128],
                                              nparts[:, (j2 * 2 + jj) * 4 + q, :], ident_bf[:],
                                              start=True, stop=True)
                mm.then_inc(s.rows_ps, 1)

            def scores(G, z, half, n):
                j, p = units(half)[n]
                k = n + (len(units(0)) if half else 0)
                pe.wait_ge(s.prob_ready, G * NU + k + 1)
                for e in range(2):
                    kt = 2 * p + e
                    diagonal = causal and kt // 4 == half
                    if diagonal:
                        off = (kt % 4) * 128
                        nc.tensor.matmul(s_ps[:, n % 2, e, :], ident_bf[:], mask_k[:, 384 - off:896 - off],
                                         start=True, stop=False)
                    mm = nc.tensor.matmul(s_ps[:, n % 2, e, :], ks[0:MAXROW + PARTS, z, j, kt * 128:(kt + 1) * 128],
                                          qs[0:MAXROW + PARTS, z, j, half * TB:(half + 1) * TB],
                                          start=not diagonal, stop=True)
                mm.then_inc(s.sc, 1)

            def values(G, z, half, n):
                j, p = units(half)[n]
                k = n + (len(units(0)) if half else 0)
                pe.wait_ge(s.prob_ready, G * NU + k + 3)
                if n == 0:
                    pe.wait_ge(s.o_copied, G * 2 + half + 1)
                last_pair = max(pp for jj, pp in units(half) if jj == j)
                for e in range(2):
                    mm = nc.tensor.matmul(o_ps[32 * j:32 * j + DH + 1, :], vg[:, z, j, 2 * p + e, :],
                                          prob[:, n % 2, e, :], start=(p == 0 and e == 0),
                                          stop=(p == last_pair and e == 1), skip_group_check=True)
                mm.then_inc(s.pv, 1)

            def sums(it):
                pe.wait_ge(s.o_copied, it + 2)
                pe.wait_ge(s.y_read, it + 1)
                nc.tensor.matmul(y_ps[:], total[:], o_sb[:], start=True, stop=True).then_inc(s.sums, 1)

            def project(it, g):
                pe.wait_ge(s.on_ready, it + 2)
                nc.tensor.matmul(y_ps[:], wo[:, g, :], on[:], start=True, stop=True).then_inc(s.y, 1)

            def operands(b, g):
                pe.wait_ge(stacks[g % 2], (b * 2 + g // 2 + 1) * STACKS)
                pe.wait_ge(s.vg_ready, b * 4 + g + 3)

            def half_step(b, g, half, first, last):
                G, z = b * 4 + g, g % 2
                it = G * 2 + half
                nu = len(units(half))
                next_half, next_z, next_G = 1 - half, (z + half) % 2, G + half
                done = 0
                pe.wait_ge(s.rows, it * 2 + 2)
                for n in range(nu):
                    scores(G, z, half, n)
                    if n == 0:
                        pe.wait_ge(s.rows, it * 2 + 3)
                    if n >= 1:
                        values(G, z, half, n - 1)
                    if n == 0 and not last and half == 1:
                        operands(b, g + 1)
                    while not last and done < shared(half, n):
                        maximum(next_G, next_z, next_half, done)
                        done += 1
                    if n == SUMS_AT and not first:
                        sums(it - 1)
                    if n == PROJECT_AT and not first:
                        project(it - 1, g if half else (g + 3) % 4)
                    if n >= nu - 2 and not last:
                        turn(next_G, next_half, n - (nu - 2))
                values(G, z, half, nu - 1)

            operands(0, 0)
            for n in range(len(maxima(0))):
                maximum(0, 0, 0, n)
            for j2 in range(2):
                turn(0, 0, j2)
            for g in range(4):
                for half in range(2):
                    half_step(0, g, half, first=g + half == 0, last=False)
            with pe.Fori(1, BATCH - 1) as b:
                for g in range(4):
                    for half in range(2):
                        half_step(b, g, half, first=False, last=False)
            for g in range(4):
                for half in range(2):
                    half_step(BATCH - 1, g, half, first=False, last=g == 3 and half == 1)
            sums(GROUPS * 2 - 1)
            project(GROUPS * 2 - 1, 3)

        @block.scalar
        def _(act):
            act.sem_inc(s.rows, 1)
            act.sem_inc(s.prob_ready, 2)
            act.sem_inc(s.o_copied, 1)
            act.wait_ge(s.consts, CONSTS)
            def rows(G, z, half, j2):
                act.wait_ge(s.rows_ps, (G * 2 + half) * 2 + j2 + 1)
                nc.scalar.activation(qs[MAXROW:MAXROW + PARTS, z, 2 * j2:2 * j2 + 2, half * TB:(half + 1) * TB],
                                     max_ps[MAXROW:MAXROW + PARTS, :, :], ACT.Copy).then_inc(s.rows, 1)

            def half_step(G, z, half, last):
                nu = len(units(half))
                base = G * NU + (len(units(0)) if half else 0)
                for n in range(nu):
                    act.wait_ge(s.sc, base + n + 1)
                    act.wait_ge(s.pv, base + n)
                    nc.scalar.activation(prob[:, n % 2], s_ps[:, n % 2], ACT.Exp,
                                         scale=SCALE).then_inc(s.prob_ready, 1)
                    if n >= nu - 2 and not last:
                        rows(G + half, (z + half) % 2, 1 - half, n - (nu - 2))
                act.wait_ge(s.pv, base + nu + 1)
                if half == 1:
                    act.sem_inc(s.stack_used, 1)
                act.wait_ge(s.on_ready, G * 2 + half + 1)
                nc.scalar.activation(o_sb[:], o_ps[:], ACT.Copy).then_inc(s.o_copied, 1)

            for j2 in range(2):
                rows(0, 0, 0, j2)
            with act.Fori(0, GROUPS // 2 - 1) as i:
                for z in range(2):
                    for half in range(2):
                        half_step(i * 2 + z, z, half, last=False)
            for z in range(2):
                for half in range(2):
                    half_step(GROUPS - 2 + z, z, half, last=z == 1 and half == 1)

        @block.vector
        def _(dve):
            dve.sem_inc(s.mx_read, 2)
            dve.sem_inc(s.on_ready, 1)
            dve.sem_inc(s.y_read, 1)
            dve.wait_ge(s.loads, LOADS)
            V = nc.vector
            dve.wait_ge(s.zeroed, 3)
            V.memset(ks[MAXROW:MAXROW + PARTS], 1.0).then_inc(s.ones, 1)
            def maximum(G, half, n):
                j, q, kh = maxima(half)[n]
                k = G * NM + n + (len(maxima(0)) if half else 0)
                dve.wait_ge(s.mx, k + 1)
                V.reduce_max(halves[:, 0, j * 4 + q % 4, kh:kh + 1], max_ps[:, n % 2, :],
                             AX.X).then_inc(s.mx_read, 1)

            def split_maxima(G, half):
                it = G * 2 + half
                dve.wait_ge(s.mx_read, (G + half) * NM + (0 if half else len(maxima(0))) + 2)
                hs = halves[:, 0, :, 0:1 if causal and half == 0 else 2]
                V.tensor_reduce(nmax[:], hs, AX.X, ALU.max, negate=True).then_inc(s.chain, 1)
                dve.wait_ge(s.chain, it * 5 + 1)
                V.tensor_copy(nparts[:, :, 0], nmax[:]).then_inc(s.chain, 1)
                dve.wait_ge(s.chain, it * 5 + 2)
                V.tensor_tensor(nrest[:], nmax[:], nparts[:, :, 0], ALU.subtract).then_inc(s.chain, 1)
                dve.wait_ge(s.chain, it * 5 + 3)
                V.tensor_copy(nparts[:, :, 1], nrest[:]).then_inc(s.chain, 1)
                dve.wait_ge(s.chain, it * 5 + 4)
                V.tensor_tensor(nparts[:, :, 2], nrest[:], nparts[:, :, 1], ALU.subtract).then_inc(s.chain, 1)

            def normalise(it):
                dve.wait_ge(s.sums, it + 1)
                V.reciprocal(inv[:], y_ps[:]).then_inc(s.inv_ready, 1)
                dve.wait_ge(s.inv_ready, it + 1)
                V.tensor_tensor(on[:], o_sb[:], inv[:], ALU.mult).then_inc(s.on_ready, 1)

            def add_output(b, g, half):
                it = (b * 4 + g) * 2 + half
                dve.wait_ge(s.y, it + 1)
                if inter:
                    to = target[:, bass.ds(b * SEQ, SEQ)].rearrange("p (t u) -> p u t", u=16)[
                        :, 8 * half:8 * half + 8, :]
                    source = y_ps[:].rearrange("p (u t) -> p u t", u=8)
                else:
                    to = target[:, bass.ds(b * SEQ + half * TB, TB)]
                    source = y_ps[:]
                if bias and g == 0:
                    V.scalar_tensor_tensor(out=to, in0=source, scalar=bo[:], in1=to, op0=ALU.add,
                                           op1=ALU.add).then_inc(s.y_read, 1)
                else:
                    V.tensor_tensor(to, to, source, ALU.add).then_inc(s.y_read, 1)

            def half_step(b, g, half, first, last):
                G = b * 4 + g
                it = G * 2 + half
                done = 0
                for n in range(len(units(half))):
                    while not last and done < shared(half, n):
                        maximum(G + half, 1 - half, done)
                        done += 1
                    if n == SUMS_AT and not first:
                        normalise(it - 1)
                    if n == PROJECT_AT and not first:
                        if half:
                            add_output(b, g, 0)
                        elif g:
                            add_output(b, g - 1, 1)
                        else:
                            add_output(b - 1, 3, 1)
                if not last:
                    split_maxima(G + half, 1 - half)

            for n in range(len(maxima(0))):
                maximum(0, 0, n)
            split_maxima(0, 0)
            for g in range(4):
                for half in range(2):
                    half_step(0, g, half, first=g + half == 0, last=False)
            with dve.Fori(1, BATCH - 1) as b:
                for g in range(4):
                    for half in range(2):
                        half_step(b, g, half, first=False, last=False)
            for g in range(4):
                for half in range(2):
                    half_step(BATCH - 1, g, half, first=False, last=g == 3 and half == 1)
            normalise(GROUPS * 2 - 1)
            add_output(BATCH - 1, 3, 1)
    release(nc, s)


def project(nc, name, src, outs):
    n_out, nk = len(outs), len(src)
    add = outs[0].get("add", False)
    slots = 4 if n_out % 2 == 0 else 2
    with ExitStack() as ctx:
        def sb(n, shape):
            return ctx.enter_context(nc.sbuf_tensor(f"{name}_{n}", shape, F32))

        out_ps = ctx.enter_context(nc.psum_tensor(f"{name}_ps", [128, slots, TB], F32))
        weights = sb("weights", [128, n_out, nk, 128])
        bias = sb("bias", [128, n_out])
        s = semaphores(nc, name, "loads product taken")
        loads = []
        for n, o in enumerate(outs):
            o["rows"] = o["w"][0].shape[-1]
            for k in range(nk):
                kr = o["w"][k].shape[0]
                loads.append((weights[0:kr, n, k, 0:o["rows"]], o["w"][k]))
            if o.get("bias") is not None:
                loads.append((bias[0:o["rows"], n:n + 1], column(o["bias"])))
        block = ctx.enter_context(nc.Block())

        @block.sync
        def _(sp):
            with nc.allow_non_contiguous_dma("biases, one value per partition"):
                for to, source in loads:
                    sp.dma_start(to, source).then_inc(s.loads, 16)

        @block.tensor
        def _(pe):
            pe.wait_ge(s.loads, 16 * len(loads))
            with pe.Fori(0, BATCH) as b:
                for j in range(2):
                    tok = bass.ds(b * SEQ + j * TB, TB)
                    for n, o in enumerate(outs):
                        m = j * n_out + n
                        pe.wait_ge(s.taken, b * (2 * n_out) + m + 1)
                        pe.nop(nofuse=True)
                        for k in range(nk):
                            kr = o["w"][k].shape[0]
                            mm = nc.tensor.matmul(out_ps[0:o["rows"], m % slots, :],
                                                  weights[0:kr, n, k, 0:o["rows"]], src[k][0:kr, tok],
                                                  start=(k == 0), stop=(k == nk - 1))
                        mm.then_inc(s.product, 1)

        def take(engine, compute):
            engine.sem_inc(s.taken, slots)
            engine.wait_ge(s.loads, 16 * len(loads))
            with engine.Fori(0, BATCH) as b:
                for j in range(2):
                    tok = bass.ds(b * SEQ + j * TB, TB)
                    for n, o in enumerate(outs):
                        m = j * n_out + n
                        engine.wait_ge(s.product, b * (2 * n_out) + m + 1)
                        engine.nop(nofuse=True)
                        compute(n, o, o["dst"][0:o["rows"], tok], out_ps[0:o["rows"], m % slots, :]).then_inc(
                            s.taken, 1)

        if add:
            @block.vector
            def _(dve):
                def compute(n, o, dst, ps):
                    if o.get("bias") is None:
                        return nc.vector.tensor_tensor(dst, dst, ps, ALU.add)
                    return nc.vector.scalar_tensor_tensor(out=dst, in0=ps, scalar=bias[0:o["rows"], n:n + 1],
                                                          in1=dst, op0=ALU.add, op1=ALU.add)
                take(dve, compute)
        else:
            @block.scalar
            def _(act):
                def compute(n, o, dst, ps):
                    return nc.scalar.activation(
                        dst, ps, o.get("func", ACT.Identity),
                        bias=bias[0:o["rows"], n:n + 1] if o.get("bias") is not None else 0.0)
                take(act, compute)
    release(nc, s)


def causal_conv(nc, name, tiles, weight, shift):
    nt, taps = len(tiles), 4
    with ExitStack() as ctx:
        def sb(n, shape):
            return ctx.enter_context(nc.sbuf_tensor(f"{name}_{n}", shape, F32))

        wt = sb("wt", [128, nt, taps])
        bt = sb("bt", [128, nt])
        acc = sb("acc", [128, 2, SEQ])
        s = semaphores(nc, name, "loads first chain summed done")
        block = ctx.enter_context(nc.Block())

        @block.sync
        def _(sp):
            with nc.allow_non_contiguous_dma("taps, one row per partition"):
                sp.dma_start(wt[:], weight.rearrange("(t p) k -> p t k", p=128)).then_inc(s.loads, 16)
                sp.dma_start(bt[:], shift.rearrange("(t p) -> p t", p=128)).then_inc(s.loads, 16)

        @block.scalar
        def _(act):
            act.wait_ge(s.loads, 32)
            with act.Fori(0, BATCH) as b:
                tok = bass.ds(b * SEQ, SEQ)
                for t in range(nt):
                    nc.scalar.activation(acc[:, t % 2], tiles[t][:, tok], ACT.Identity, bias=bt[:, t:t + 1],
                                         scale=wt[:, t, taps - 1:taps]).then_inc(s.first, 1)
                for t in range(nt):
                    act.wait_ge(s.summed, b * nt + t + 1)
                    act.nop(nofuse=True)
                    nc.scalar.activation(tiles[t][:, tok], acc[:, t % 2], ACT.Silu).then_inc(s.done, 1)
                    act.wait_ge(s.done, b * nt + t + 1)

        @block.vector
        def _(dve):
            dve.wait_ge(s.loads, 32)
            with dve.Fori(0, BATCH) as b:
                for t in range(nt):
                    dve.wait_ge(s.first, b * nt + t + 1)
                    for k in range(1, taps):
                        v = nc.vector.scalar_tensor_tensor(
                            out=acc[:, t % 2, k:SEQ], in0=tiles[t][:, bass.ds(b * SEQ, SEQ - k)],
                            scalar=wt[:, t, taps - 1 - k:taps - k], in1=acc[:, t % 2, k:SEQ],
                            op0=ALU.mult, op1=ALU.add)
                        if k < taps - 1:
                            v.then_inc(s.chain, 1)
                            dve.wait_ge(s.chain, b * (nt * 2) + t * 2 + k)
                    v.then_inc(s.summed, 1)
    release(nc, s)


def pointwise(nc, name, steps):
    s = semaphores(nc, name, "loads step")
    with ExitStack() as ctx:
        scalars, loads = {}, []
        for n, st in enumerate(steps):
            if len(st) == 6 and not isinstance(st[2], float):
                scalars[n] = ctx.enter_context(nc.sbuf_tensor(f"{name}_s{n}", [128, 1], F32))
                loads.append((scalars[n][:], column(st[2])))
        block = ctx.enter_context(nc.Block())

        @block.sync
        def _(sp):
            with nc.allow_non_contiguous_dma("one value per partition"):
                for to, source in loads:
                    sp.dma_start(to, source).then_inc(s.loads, 16)

        @block.vector
        def _(dve):
            if loads:
                dve.wait_ge(s.loads, 16 * len(loads))
            with dve.Fori(0, BATCH) as b:
                tok = bass.ds(b * SEQ, SEQ)
                for n, st in enumerate(steps):
                    if len(st) == 4:
                        v = nc.vector.tensor_tensor(st[0][:, tok], st[1][:, tok], st[2][:, tok], st[3])
                    else:
                        v = nc.vector.scalar_tensor_tensor(
                            out=st[0][:, tok], in0=st[1][:, tok], scalar=scalars[n][:] if n in scalars else st[2],
                            in1=st[3][:, tok], op0=st[4], op1=st[5])
                    v.then_inc(s.step, 1)
                    dve.wait_ge(s.step, b * len(steps) + n + 1)
    release(nc, s)


def grouped_conv(nc, name, h, target, weight, shift):
    with ExitStack() as ctx:
        def sb(n, shape):
            return ctx.enter_context(nc.sbuf_tensor(f"{name}_{n}", shape, F32))

        ps = ctx.enter_context(nc.psum_tensor(f"{name}_ps", [128, 2, TB], F32))
        wt = sb("wt", [128, 4, 128])
        bt = sb("bt", [128, 1])
        s = semaphores(nc, name, "zeroed loads product taken")
        block = ctx.enter_context(nc.Block())

        @block.sync
        def _(sp):
            sp.wait_ge(s.zeroed, 1)
            with nc.allow_non_contiguous_dma("blocks of 32"):
                for g in range(4):
                    r = slice(32 * g, 32 * g + 32)
                    sp.dma_start(wt[r, :, r], weight[:, :, r].rearrange("k i o -> i k o")).then_inc(s.loads, 16)
                sp.dma_start(bt[:], column(shift)).then_inc(s.loads, 16)

        @block.gpsimd
        def _(pool):
            pool.memset(wt[:], 0.0).then_inc(s.zeroed, 1)

        @block.tensor
        def _(pe):
            pe.wait_ge(s.loads, 80)
            with pe.Fori(0, BATCH) as b:
                for j in range(2):
                    pe.wait_ge(s.taken, b * 2 + j + 1)
                    for k in range(4):
                        skip = k if j == 0 else 0
                        mm = nc.tensor.matmul(ps[:, j, skip:TB], wt[:, 3 - k, :],
                                              h[:, bass.ds(b * SEQ + j * TB - k + skip, TB - skip)],
                                              start=(k == 0), stop=(k == 3), skip_group_check=True)
                    mm.then_inc(s.product, 1)

        @block.vector
        def _(dve):
            dve.sem_inc(s.taken, 2)
            dve.wait_ge(s.loads, 80)
            with dve.Fori(0, BATCH) as b:
                for j in range(2):
                    tok = bass.ds(b * SEQ + j * TB, TB)
                    dve.wait_ge(s.product, b * 2 + j + 1)
                    nc.vector.scalar_tensor_tensor(out=target[:, tok], in0=ps[:, j, :], scalar=bt[:],
                                                   in1=target[:, tok], op0=ALU.add, op1=ALU.add).then_inc(s.taken, 1)
    release(nc, s)


def pooled_mix(nc, name, q, k, v, target):
    with ExitStack() as ctx:
        def sb(n, shape, dt=F32):
            return ctx.enter_context(nc.sbuf_tensor(f"{name}_{n}", shape, dt))

        count = sb("count", [128, SEQ], I32)
        inv = sb("inv", [128, SEQ])
        one = sb("one", [128, SEQ])
        t1, t2 = sb("t1", [128, SEQ]), sb("t2", [128, SEQ])
        s = semaphores(nc, name, "consts setup step")
        block = ctx.enter_context(nc.Block())

        @block.gpsimd
        def _(pool):
            pool.iota(count[:], pattern=[[1, SEQ]], base=1, channel_multiplier=0).then_inc(s.consts, 1)
            pool.memset(one[:], 1.0).then_inc(s.consts, 1)

        @block.vector
        def _(dve):
            V = nc.vector
            dve.wait_ge(s.consts, 2)
            V.tensor_copy(t1[:], count[:]).then_inc(s.setup, 1)
            dve.wait_ge(s.setup, 1)
            V.reciprocal(inv[:], t1[:]).then_inc(s.setup, 1)
            dve.wait_ge(s.setup, 2)
            with dve.Fori(0, BATCH) as b:
                tok = bass.ds(b * SEQ, SEQ)
                steps = (
                    lambda: V.tensor_tensor_scan(t1[:], one[:], q[:, tok], 0.0, ALU.mult, ALU.add),
                    lambda: V.tensor_tensor(t1[:], t1[:], inv[:], ALU.mult),
                    lambda: V.tensor_tensor(t1[:], t1[:], k[:, tok], ALU.mult),
                    lambda: V.tensor_tensor_scan(t2[:], one[:], t1[:], 0.0, ALU.mult, ALU.add),
                    lambda: V.tensor_tensor(t2[:], t2[:], inv[:], ALU.mult),
                    lambda: V.tensor_tensor(t2[:], t2[:], v[:, tok], ALU.mult),
                    lambda: V.tensor_tensor(target[:, tok], target[:, tok], t2[:], ALU.add),
                )
                for n, step in enumerate(steps):
                    step().then_inc(s.step, 1)
                    dve.wait_ge(s.step, b * len(steps) + n + 1)
    release(nc, s)


def mean_gate(nc, name, xc, gate, w_c):
    with ExitStack() as ctx:
        def sb(n, shape):
            return ctx.enter_context(nc.sbuf_tensor(f"{name}_{n}", shape, F32))

        c_ps = ctx.enter_context(nc.psum_tensor(f"{name}_c_ps", [16, 2, TB], F32))
        g_ps = ctx.enter_context(nc.psum_tensor(f"{name}_g_ps", [128, 2, TB], F32))
        wc = sb("wc", [128, 2, 16])
        mean = sb("mean", [16, 128])
        c = sb("c", [16, 2, TB])
        s = semaphores(nc, name, "loads consts c_product c_ready g_product g_ready")
        block = ctx.enter_context(nc.Block())

        @block.sync
        def _(sp):
            sp.dma_start(wc[:], w_c.rearrange("(t p) n -> p t n", p=128)).then_inc(s.loads, 16)

        @block.gpsimd
        def _(pool):
            pool.memset(mean[:], 1.0 / 16).then_inc(s.consts, 1)

        @block.tensor
        def _(pe):
            pe.wait_ge(s.loads, 16)
            pe.wait_ge(s.consts, 1)
            with pe.Fori(0, BATCH) as b:
                for j in range(2):
                    tok = bass.ds(b * SEQ + j * TB, TB)
                    pe.wait_ge(s.c_ready, b * 2 + j + 1)
                    pe.nop(nofuse=True)
                    for t in range(2):
                        mm = nc.tensor.matmul(c_ps[:, j, :], wc[:, t, :], xc[t][:, tok], start=(t == 0), stop=(t == 1))
                    mm.then_inc(s.c_product, 1)
                    pe.wait_ge(s.c_ready, b * 2 + j + 3)
                    pe.wait_ge(s.g_ready, b * 2 + j + 1)
                    nc.tensor.matmul(g_ps[:, j, :], mean[:], c[:, j, :], start=True, stop=True).then_inc(s.g_product, 1)

        @block.scalar
        def _(act):
            act.sem_inc(s.c_ready, 2)
            act.sem_inc(s.g_ready, 2)
            with act.Fori(0, BATCH) as b:
                for j in range(2):
                    act.wait_ge(s.c_product, b * 2 + j + 1)
                    nc.scalar.activation(c[:, j, :], c_ps[:, j, :], ACT.Copy).then_inc(s.c_ready, 1)
                    act.wait_ge(s.g_product, b * 2 + j + 1)
                    act.nop(nofuse=True)
                    nc.scalar.activation(gate[:, bass.ds(b * SEQ + j * TB, TB)], g_ps[:, j, :],
                                         ACT.Sigmoid).then_inc(s.g_ready, 1)
    release(nc, s)


def selective_scan(nc, name, u, b_rows, c_rows, y, delta=None, a_log=None, decay_rows=None):
    N, NT = 16, 2
    shared_decay = decay_rows is not None
    with ExitStack() as ctx:
        def sb(n, shape, dt=F32):
            return ctx.enter_context(nc.sbuf_tensor(f"{name}_{n}", shape, dt))

        row_ps = ctx.enter_context(nc.psum_tensor(f"{name}_row_ps", [128, 2, 2, TB], F32))
        y_ps = ctx.enter_context(nc.psum_tensor(f"{name}_y_ps", [128, NT, 2, TB], F32))
        ident = sb("ident", [128, 128])
        a_col = sb("a_col", [128, NT, N])
        bn = sb("bn", [128, 2, SEQ])
        cn = sb("cn", [128, 2, SEQ])
        decay = sb("decay", [128, 2, SEQ])
        bu = sb("bu", [128, 2, SEQ])
        hs = sb("hs", [128, SEQ])
        hc = sb("hc", [128, 2, SEQ])
        s = semaphores(nc, name, "loads consts a_step rows rows_read decay_ready bu_ready state hc_ready summed y_read")
        R = 3 if shared_decay else 2
        K = N * NT
        block = ctx.enter_context(nc.Block())

        @block.sync
        def _(sp):
            if a_log is not None:
                sp.dma_start(a_col[:], a_log.rearrange("(t p) n -> p t n", p=128)).then_inc(s.loads, 16)

        @block.gpsimd
        def _(pool):
            pool.memset(ident[:], 0.0).then_inc(s.consts, 1)
            pool.wait_ge(s.consts, 1)
            pool.affine_select(out=ident[:], in_=ident[:], compare_op=ALU.not_equal, fill=1.0, base=0,
                               pattern=[[-1, 128]], channel_multiplier=1).then_inc(s.consts, 1)
            with pool.Fori(0, BATCH) as b:
                for n in range(N):
                    for t in range(NT):
                        k = n * NT + t
                        if t == 0:
                            pool.wait_ge(s.rows_read, b * (N * R) + n * R + 3)
                        pool.wait_ge(s.state, b * K + k + 1)
                        pool.nop(nofuse=True)
                        nc.gpsimd.tensor_tensor(bu[:, k % 2], u[t][:, bass.ds(b * SEQ, SEQ)], bn[:, n % 2],
                                                ALU.mult).then_inc(s.bu_ready, 1)

        @block.tensor
        def _(pe):
            pe.wait_ge(s.consts, 2)

            def repeat(b, n):
                sources = [b_rows, c_rows] + ([decay_rows] if shared_decay else [])
                for r, rows in enumerate(sources):
                    m = n * R + r
                    pe.wait_ge(s.rows_read, b * (N * R) + m + 1)
                    pe.nop(nofuse=True)
                    for j in range(2):
                        mm = nc.tensor.matmul(row_ps[:, m % 2, j, :],
                                              ident[0:N, n:n + 1].to_broadcast([N, 128]),
                                              rows[:, bass.ds(b * SEQ + j * TB, TB)], start=True, stop=True)
                    mm.then_inc(s.rows, 1)

            with pe.Fori(0, BATCH) as b:
                repeat(b, 0)
                for n in range(N):
                    if n + 1 < N:
                        repeat(b, n + 1)
                    for t in range(NT):
                        k = n * NT + t
                        pe.wait_ge(s.hc_ready, b * K + k + 3)
                        if n == 0:
                            pe.wait_ge(s.y_read, b * NT + t + 1)
                        for j in range(2):
                            mm = nc.tensor.matmul(y_ps[:, t, j, :], ident[:], hc[:, k % 2, j * TB:(j + 1) * TB],
                                                  start=(n == 0), stop=(n == N - 1))
                        mm.then_inc(s.summed, 1)

        @block.scalar
        def _(act):
            act.sem_inc(s.rows_read, 2)
            act.sem_inc(s.y_read, NT)
            if a_log is not None:
                act.wait_ge(s.loads, 16)
                nc.scalar.activation(a_col[:], a_col[:], ACT.Exp).then_inc(s.a_step, 1)
                act.wait_ge(s.a_step, 1)
                nc.scalar.activation(a_col[:], a_col[:], ACT.Copy, scale=-1.0).then_inc(s.a_step, 1)
                act.wait_ge(s.a_step, 2)
            with act.Fori(0, BATCH) as b:
                for n in range(N):
                    targets = [bn, cn] + ([decay] if shared_decay else [])
                    for r, to in enumerate(targets):
                        m = n * R + r
                        act.wait_ge(s.rows, b * (N * R) + m + 1)
                        if r == 0:
                            act.wait_ge(s.hc_ready, b * K + max(n * NT, 1))
                        nc.scalar.activation(to[:, n % 2], row_ps[:, m % 2].rearrange("p j t -> p (j t)"),
                                                 ACT.Copy).then_inc(s.rows_read, 1)
                    if not shared_decay:
                        for t in range(NT):
                            k = n * NT + t
                            act.wait_ge(s.state, b * K + k + 1)
                            act.nop(nofuse=True)
                            nc.scalar.activation(decay[:, k % 2], delta[t][:, bass.ds(b * SEQ, SEQ)], ACT.Exp,
                                                 scale=a_col[:, t, n:n + 1]).then_inc(s.decay_ready, 1)
                for t in range(NT):
                    act.wait_ge(s.summed, b * K + K - NT + t + 3)
                    act.nop(nofuse=True)
                    nc.scalar.activation(y[t][:, bass.ds(b * SEQ, SEQ)], y_ps[:, t].rearrange("p j t -> p (j t)"),
                                         ACT.Copy).then_inc(s.y_read, 1)

        @block.vector
        def _(dve):
            dve.sem_inc(s.state, 2)
            dve.sem_inc(s.hc_ready, 2)
            dve.sem_inc(s.summed, 2)
            with dve.Fori(0, BATCH) as b:
                for n in range(N):
                    for t in range(NT):
                        k = n * NT + t
                        dve.wait_ge(s.bu_ready, b * K + k + 1)
                        if shared_decay:
                            dve.wait_ge(s.rows_read, b * (N * R) + n * R + 5)
                        else:
                            dve.wait_ge(s.rows_read, b * (N * R) + n * R + 4)
                            dve.wait_ge(s.decay_ready, b * K + k + 1)
                        dve.wait_ge(s.hc_ready, b * K + k + 2)
                        nc.vector.tensor_tensor_scan(hs[:], decay[:, n % 2 if shared_decay else k % 2], bu[:, k % 2],
                                                     0.0, ALU.mult, ALU.add).then_inc(s.state, 1)
                        dve.wait_ge(s.state, b * K + k + 3)
                        dve.wait_ge(s.summed, b * K + k + 1)
                        nc.vector.tensor_tensor(hc[:, k % 2], hs[:], cn[:, n % 2], ALU.mult).then_inc(s.hc_ready, 1)
    release(nc, s)


def softplus(nc, name, tiles):
    nt = len(tiles)
    with ExitStack() as ctx:
        a = ctx.enter_context(nc.sbuf_tensor(f"{name}_a", [128, 2, SEQ], F32))
        s = semaphores(nc, name, "a_step done")
        block = ctx.enter_context(nc.Block())

        @block.scalar
        def _(act):
            act.sem_inc(s.done, 2)
            with act.Fori(0, BATCH) as b:
                for t in range(nt):
                    act.wait_ge(s.done, b * nt + t + 1)
                    act.nop(nofuse=True)
                    steps = (
                        lambda: nc.scalar.activation(a[:, t % 2], tiles[t][:, bass.ds(b * SEQ, SEQ)], ACT.Abs),
                        lambda: nc.scalar.activation(a[:, t % 2], a[:, t % 2], ACT.Exp, scale=-1.0),
                        lambda: nc.scalar.activation(a[:, t % 2], a[:, t % 2], ACT.Ln, bias=1.0),
                    )
                    for n, step in enumerate(steps):
                        step().then_inc(s.a_step, 1)
                        act.wait_ge(s.a_step, b * (3 * nt) + 3 * t + n + 1)

        @block.vector
        def _(dve):
            with dve.Fori(0, BATCH) as b:
                for t in range(nt):
                    tok = bass.ds(b * SEQ, SEQ)
                    dve.wait_ge(s.a_step, b * (3 * nt) + 3 * t + 3)
                    nc.vector.scalar_tensor_tensor(out=tiles[t][:, tok], in0=tiles[t][:, tok], scalar=0.0,
                                                   in1=a[:, t % 2], op0=ALU.max, op1=ALU.add).then_inc(s.done, 1)
    release(nc, s)


def clipped_decay(nc, name, rows):
    s = semaphores(nc, name, "clipped step")
    with nc.Block() as block:
        @block.vector
        def _(dve):
            with dve.Fori(0, BATCH) as b:
                r = rows[:, bass.ds(b * SEQ, SEQ)]
                nc.vector.tensor_scalar(r, r, -5.0, 0.0, ALU.max, ALU.min).then_inc(s.clipped, 1)

        @block.scalar
        def _(act):
            with act.Fori(0, BATCH) as b:
                r = rows[:, bass.ds(b * SEQ, SEQ)]
                act.wait_ge(s.clipped, b + 1)
                act.nop(nofuse=True)
                nc.scalar.activation(r, r, ACT.Exp).then_inc(s.step, 1)
                act.wait_ge(s.step, b * 2 + 1)
                act.nop(nofuse=True)
                nc.scalar.activation(r, r, ACT.Exp, scale=-1.0).then_inc(s.step, 1)
    release(nc, s)


def feature_map(nc, name, q, k, scale):
    with ExitStack() as ctx:
        low = ctx.enter_context(nc.sbuf_tensor(f"{name}_low", [128, 2, SEQ], F32))
        s = semaphores(nc, name, "low_ready expd done")
        block = ctx.enter_context(nc.Block())

        @block.vector
        def _(dve):
            dve.sem_inc(s.done, 2)
            with dve.Fori(0, BATCH) as b:
                tok = bass.ds(b * SEQ, SEQ)
                for z, t in enumerate((q, k)):
                    dve.wait_ge(s.done, b * 2 + z + 1)
                    nc.vector.tensor_scalar(low[:, z], t[:, tok], scale if z == 0 else 1.0, 0.0, ALU.mult,
                                            ALU.min).then_inc(s.low_ready, 1)
                for z, t in enumerate((q, k)):
                    dve.wait_ge(s.expd, b * 2 + z + 1)
                    nc.vector.tensor_scalar(t[:, tok], t[:, tok], 0.0, scale if z == 0 else 1.0, ALU.max,
                                            ALU.mult).then_inc(s.low_ready, 1)
                    dve.wait_ge(s.low_ready, b * 4 + z + 3)
                    nc.vector.tensor_tensor(t[:, tok], t[:, tok], low[:, z], ALU.add).then_inc(s.done, 1)

        @block.scalar
        def _(act):
            with act.Fori(0, BATCH) as b:
                for z in range(2):
                    act.wait_ge(s.low_ready, b * 4 + z + 1)
                    nc.scalar.activation(low[:, z], low[:, z], ACT.Exp).then_inc(s.expd, 1)
    release(nc, s)


def gated_linear_attention(nc, name, q, k, v, gate, y):
    NT = 8
    with ExitStack() as ctx:
        def sb(n, shape):
            return ctx.enter_context(nc.sbuf_tensor(f"{name}_{n}", shape, F32))

        rep_ps = ctx.enter_context(nc.psum_tensor(f"{name}_rep_ps", [128, 3, 2, TB], F32))
        y_ps = ctx.enter_context(nc.psum_tensor(f"{name}_y_ps", [128, 2, TB], F32))
        sel_i = sb("sel_i", [128, NT, 128])
        sel_j = sb("sel_j", [128, NT, 128])
        sel_g = sb("sel_g", [HEADS, NT, 128])
        sum_j = sb("sum_j", [128, NT, 128])
        ks = sb("ks", [128, SEQ])
        gs = sb("gs", [128, 2, SEQ])
        kv = sb("kv", [128, 2, SEQ])
        st = sb("st", [128, SEQ])
        qst = sb("qst", [128, 2, SEQ])
        s = semaphores(nc, name, "consts rep ks_ready gs_ready kv_ready state qs_ready summed y_read")
        K = NT
        block = ctx.enter_context(nc.Block())

        @block.gpsimd
        def _(pool):
            def view(t):
                return t[:].rearrange("p t (h i j) -> p t h i j", h=2, i=8)

            pool.memset(sel_i[:], 1.0).then_inc(s.consts, 1)
            pool.memset(sel_j[:], 0.0).then_inc(s.consts, 1)
            pool.memset(sel_g[:], 1.0).then_inc(s.consts, 1)
            pool.memset(sum_j[:], 0.0).then_inc(s.consts, 1)
            pool.wait_ge(s.consts, 4)
            pool.affine_select(out=sel_i[:], in_=sel_i[:], compare_op=ALU.is_ge, fill=0.0, base=0,
                               pattern=[[128, NT], [1, 128]], channel_multiplier=-8).then_inc(s.consts, 1)
            pool.wait_ge(s.consts, 5)
            pool.affine_select(out=sel_i[:], in_=sel_i[:], compare_op=ALU.is_ge, fill=0.0, base=7,
                               pattern=[[-128, NT], [-1, 128]], channel_multiplier=8).then_inc(s.consts, 1)
            pool.affine_select(out=sel_g[:], in_=sel_g[:], compare_op=ALU.is_ge, fill=0.0, base=0,
                               pattern=[[128, NT], [1, 128]], channel_multiplier=-64).then_inc(s.consts, 1)
            pool.wait_ge(s.consts, 7)
            pool.affine_select(out=sel_g[:], in_=sel_g[:], compare_op=ALU.is_ge, fill=0.0, base=63,
                               pattern=[[-128, NT], [-1, 128]], channel_multiplier=64).then_inc(s.consts, 1)
            n = 8
            for h in range(2):
                part = sel_j[:, :, 64 * h:64 * h + 64].rearrange("p t (i j) -> p t i j", i=8)
                pool.affine_select(out=part, in_=part, compare_op=ALU.not_equal, fill=1.0, base=-8 * h,
                                   pattern=[[-16, NT], [0, 8], [-1, 8]], channel_multiplier=1).then_inc(s.consts, 1)
                n += 1
                pool.wait_ge(s.consts, n)
            for i in range(8):
                for t in range(NT):
                    part = sum_j[:, t, 16 * t:16 * t + 16].rearrange("p (h j) -> p h j", h=2)
                    pool.affine_select(out=part, in_=part, compare_op=ALU.not_equal, fill=1.0, base=-8 * i,
                                       pattern=[[-64, 2], [-1, 8]], channel_multiplier=1).then_inc(s.consts, 1)
                n += NT
                pool.wait_ge(s.consts, n)

        CONSTS = 10 + 8 * NT

        @block.tensor
        def _(pe):
            pe.wait_ge(s.consts, CONSTS)
            with pe.Fori(0, BATCH) as b:
                for t in range(NT):
                    g = b * K + t
                    for r, (sel, rows) in enumerate(((sel_i, k), (sel_j, v), (sel_g, gate), (sel_i, q))):
                        if r == 0:
                            pe.wait_ge(s.qs_ready, g + 2)
                        if r == 1:
                            pe.wait_ge(s.kv_ready, g + 1)
                        if r == 2:
                            pe.wait_ge(s.gs_ready, g + 1)
                        if r == 3:
                            pe.wait_ge(s.ks_ready, g + 2)
                        pe.nop(nofuse=True)
                        for j in range(2):
                            mm = nc.tensor.matmul(rep_ps[:, r % 3, j, :], sel[:, t, :],
                                                  rows[:, bass.ds(b * SEQ + j * TB, TB)], start=True, stop=True)
                        mm.then_inc(s.rep, 1)
                    pe.wait_ge(s.qs_ready, g + 3)
                    if t == 0:
                        pe.wait_ge(s.y_read, b + 1)
                    for j in range(2):
                        mm = nc.tensor.matmul(y_ps[:, j, :], sum_j[:, t, :], qst[:, t % 2, j * TB:(j + 1) * TB],
                                              start=(t == 0), stop=(t == NT - 1))
                    mm.then_inc(s.summed, 1)

        @block.scalar
        def _(act):
            act.sem_inc(s.ks_ready, 1)
            act.sem_inc(s.gs_ready, 1)
            act.sem_inc(s.y_read, 1)
            with act.Fori(0, BATCH) as b:
                for t in range(NT):
                    g = b * K + t
                    act.wait_ge(s.rep, g * 4 + 1)
                    act.wait_ge(s.kv_ready, g + 1)
                    nc.scalar.activation(ks[:], rep_ps[:, 0].rearrange("p j t -> p (j t)"), ACT.Copy).then_inc(
                        s.ks_ready, 1)
                    act.wait_ge(s.rep, g * 4 + 3)
                    act.wait_ge(s.state, g + 1)
                    nc.scalar.activation(gs[:, t % 2], rep_ps[:, 2].rearrange("p j t -> p (j t)"), ACT.Copy).then_inc(
                        s.gs_ready, 1)
                act.wait_ge(s.summed, b * K + K + 2)
                act.nop(nofuse=True)
                nc.scalar.activation(y[:, bass.ds(b * SEQ, SEQ)], y_ps[:].rearrange("p j t -> p (j t)"),
                                     ACT.Copy).then_inc(s.y_read, 1)

        @block.vector
        def _(dve):
            dve.sem_inc(s.kv_ready, 1)
            dve.sem_inc(s.state, 2)
            dve.sem_inc(s.qs_ready, 2)
            dve.sem_inc(s.summed, 2)
            with dve.Fori(0, BATCH) as b:
                for t in range(NT):
                    g = b * K + t
                    dve.wait_ge(s.ks_ready, g + 2)
                    dve.wait_ge(s.rep, g * 4 + 2)
                    dve.wait_ge(s.state, g + 1)
                    nc.vector.tensor_tensor(kv[:, t % 2], ks[:], rep_ps[:, 1].rearrange("p j t -> p (j t)"),
                                            ALU.mult).then_inc(s.kv_ready, 1)
                    dve.wait_ge(s.kv_ready, g + 2)
                    dve.wait_ge(s.gs_ready, g + 2)
                    dve.wait_ge(s.qs_ready, g + 2)
                    nc.vector.tensor_tensor_scan(st[:], gs[:, t % 2], kv[:, t % 2], 0.0, ALU.mult,
                                                 ALU.add).then_inc(s.state, 1)
                    dve.wait_ge(s.rep, g * 4 + 4)
                    dve.wait_ge(s.state, g + 3)
                    dve.wait_ge(s.summed, g + 1)
                    nc.vector.tensor_tensor(qst[:, t % 2], st[:], rep_ps[:, 0].rearrange("p j t -> p (j t)"),
                                            ALU.mult).then_inc(s.qs_ready, 1)
    release(nc, s)


WAVE_HEADS, POS, SAMPLES = 8, 16, 33
SUBS = TB // 128


def wave_attention_weights(nc, name, h, rows, attn, index, p):
    WH, H, S = 3 * WAVE_HEADS, WAVE_HEADS, SAMPLES
    with ExitStack() as ctx:
        def sb(n, shape, dt=F32):
            return ctx.enter_context(nc.sbuf_tensor(f"{name}_{n}", shape, dt))

        tok_ps = ctx.enter_context(nc.psum_tensor(f"{name}_tok_ps", [128, SUBS, 128], F32))
        query_ps = ctx.enter_context(nc.psum_tensor(f"{name}_query_ps", [128, SUBS, 128], F32))
        wave_ps = ctx.enter_context(nc.psum_tensor(f"{name}_wave_ps", [128, SUBS, WH], F32))
        ident = sb("ident", [128, 128])
        w_wave, w_query = sb("w_wave", [128, WH]), sb("w_query", [128, H * POS])
        b_wave, b_query, key = sb("b_wave", [128, WH]), sb("b_query", [128, H * POS]), sb("key", [128, POS])
        grid_i, grid, grid_abs = sb("grid_i", [128, S], I32), sb("grid", [128, S]), sb("grid_abs", [128, S])
        centre_i, centre = sb("centre_i", [128, SUBS], I32), sb("centre", [128, SUBS])
        hb = sb("hb", [128, TB])
        tok = sb("tok", [128, SUBS, 128])
        wave = sb("wave", [128, SUBS, WH])
        wave_f = sb("wave_f", [128, 3, SUBS, H])
        query = sb("query", [128, SUBS, H * POS])
        avg = sb("avg", [128, 3, SUBS])
        qk = sb("qk", [128, SUBS, H])
        pos, cell, mask, rel, env, t33 = (sb(m, [128, SUBS, S]) for m in ("pos", "cell", "mask", "rel", "env", "t33"))
        cell_i = sb("cell_i", [128, SUBS, S], I32)
        sc = sb("sc", [128, SUBS * H, S])
        first = sb("first", [128, 1])
        zero33 = sb("zero33", [128, SUBS, S])
        big = sb("big", [128, SUBS * H])
        big2 = sb("big2", [128, SUBS * H])
        s = semaphores(nc, name, "loads consts setup copied products tok_ready written wave_in wave_silu query_in "
                                 "query_silu wave_done env_in env_done exp_in exp_done chain done next_first")
        loads = [(w_wave[:], p["w_wave"]), (w_query[:], p["w_query"]),
                 (b_wave[:], p["b_wave"].partition_broadcast(128)), (b_query[:], p["b_query"].partition_broadcast(128)),
                 (key[:], p["key_weight"].partition_broadcast(128))]
        block = ctx.enter_context(nc.Block())

        @block.sync
        def _(sp):
            for to, source in loads:
                sp.dma_start(to, source).then_inc(s.loads, 16)
            sp.sem_inc(s.written, 1)
            with sp.Fori(0, NTB) as b:
                sp.wait_ge(s.tok_ready, b + 1)
                sp.dma_start(rows[bass.ds(b * TB, TB), :].rearrange("(q p) c -> p q c", p=128), tok[:]).then_inc(
                    s.written, 16)
            sp.wait_ge(s.written, 16 * NTB + 1)

        @block.gpsimd
        def _(pool):
            pool.memset(ident[:], 0.0).then_inc(s.consts, 1)
            pool.iota(grid_i[:], pattern=[[1, S]], base=-(S // 2), channel_multiplier=0).then_inc(s.consts, 1)
            pool.iota(centre_i[:], pattern=[[128, SUBS]], base=0, channel_multiplier=1).then_inc(s.consts, 1)
            pool.wait_ge(s.consts, 3)
            pool.affine_select(out=ident[:], in_=ident[:], compare_op=ALU.not_equal, fill=1.0, base=0,
                               pattern=[[-1, 128]], channel_multiplier=1).then_inc(s.consts, 1)

        @block.tensor
        def _(pe):
            pe.wait_ge(s.loads, 16 * len(loads))
            pe.wait_ge(s.consts, 4)
            with pe.Fori(0, NTB) as b:
                pe.wait_ge(s.copied, b + 1)
                pe.wait_ge(s.done, b + 1)
                for q in range(SUBS):
                    nc.tensor.transpose(tok_ps[:, q, :], hb[:, q * 128:(q + 1) * 128], ident[:])
                    nc.tensor.matmul(wave_ps[:, q, :], hb[:, q * 128:(q + 1) * 128], w_wave[:], start=True, stop=True)
                    mm = nc.tensor.matmul(query_ps[:, q, :], hb[:, q * 128:(q + 1) * 128], w_query[:],
                                          start=True, stop=True)
                mm.then_inc(s.products, 1)

        @block.scalar
        def _(act):
            with act.Fori(0, NTB) as b:
                act.wait_ge(s.done, b + 1)
                act.nop(nofuse=True)
                nc.scalar.activation(hb[:], h[:, bass.ds(b * TB, TB)], ACT.Copy).then_inc(s.copied, 1)
                act.wait_ge(s.products, b + 1)
                act.wait_ge(s.written, b * 16 + 1)
                nc.scalar.activation(tok[:], tok_ps[:], ACT.Copy).then_inc(s.tok_ready, 1)
                act.wait_ge(s.query_in, b + 1)
                nc.scalar.activation(query[:], query[:], ACT.Silu).then_inc(s.query_silu, 1)
                nc.scalar.activation(wave[:], wave[:], ACT.Silu).then_inc(s.wave_silu, 1)
                act.wait_ge(s.wave_silu, b + 1)
                w = wave[:].rearrange("p q (f h) -> p f q h", f=3)
                nc.scalar.activation(wave_f[:, 0], w[:, 0], ACT.Sigmoid)
                nc.scalar.activation(wave_f[:, 2], w[:, 2], ACT.Sigmoid)
                nc.scalar.activation(wave_f[:, 1], w[:, 1], ACT.Tanh).then_inc(s.wave_done, 1)
                act.wait_ge(s.env_in, b + 1)
                nc.scalar.activation(env[:], env[:], ACT.Exp).then_inc(s.env_done, 1)
                act.wait_ge(s.exp_in, b + 1)
                nc.scalar.activation(sc[:], sc[:], ACT.Exp).then_inc(s.exp_done, 1)

        @block.vector
        def _(dve):
            V, tt = nc.vector, nc.vector.tensor_tensor
            dve.sem_inc(s.done, 1)
            dve.wait_ge(s.loads, 16 * len(loads))
            dve.wait_ge(s.consts, 4)
            V.tensor_copy(grid[:], grid_i[:]).then_inc(s.setup, 1)
            V.tensor_copy(centre[:], centre_i[:]).then_inc(s.setup, 1)
            dve.wait_ge(s.setup, 2)
            V.scalar_tensor_tensor(out=grid_abs[:], in0=grid[:], scalar=-1.0, in1=grid[:], op0=ALU.mult,
                                   op1=ALU.max).then_inc(s.setup, 1)
            V.memset(first[:], 0.0).then_inc(s.setup, 1)
            V.memset(zero33[:], 0.0).then_inc(s.setup, 1)
            dve.wait_ge(s.setup, 5)
            LINKS = 33
            with dve.Fori(0, BATCH) as b:
                for j in range(2):
                    k = b * 2 + j
                    links = [0]

                    def link(ins):
                        links[0] += 1
                        ins.then_inc(s.chain, 1)
                        dve.wait_ge(s.chain, k * LINKS + links[0])

                    def over_samples(a):
                        return a.unsqueeze(2).to_broadcast([128, SUBS, S])

                    def over_tiles(a, n=S):
                        return a.unsqueeze(1).to_broadcast([128, SUBS, n])

                    dve.wait_ge(s.products, k + 1)
                    link(tt(wave[:], wave_ps[:], over_tiles(b_wave[:], WH), ALU.add))
                    tt(query[:], query_ps[:], over_tiles(b_query[:], H * POS), ALU.add).then_inc(s.query_in, 1)
                    dve.wait_ge(s.query_silu, k + 1)
                    q4 = query[:].rearrange("p q (h d) -> p (q h) d", d=POS)
                    link(tt(q4, q4, key[:].unsqueeze(1).to_broadcast([128, SUBS * H, POS]), ALU.mult))
                    link(V.tensor_reduce(qk[:].rearrange("p q h -> p (q h)"), q4, AX.X, ALU.add))
                    link(V.tensor_scalar(qk[:], qk[:], float(POS) ** -0.5, None, ALU.mult))
                    dve.wait_ge(s.wave_done, k + 1)
                    for f, (scale, shift) in enumerate(((15.0, 1.0), (16.0, 0.0), (9.5, 0.5))):
                        last = V.tensor_scalar(wave_f[:, f], wave_f[:, f], scale, shift, ALU.mult, ALU.add)
                    link(last)
                    link(V.tensor_reduce(avg[:], wave_f[:], AX.X, ALU.add))
                    link(V.tensor_scalar(avg[:], avg[:], 1.0 / H, None, ALU.mult))
                    link(tt(pos[:], over_tiles(grid[:]), over_samples(avg[:, 0]), ALU.mult))
                    link(V.scalar_tensor_tensor(out=pos[:], in0=over_samples(centre[:]), scalar=float(j * TB),
                                                in1=pos[:], op0=ALU.add, op1=ALU.add))
                    link(tt(pos[:], pos[:], over_samples(avg[:, 1]), ALU.add))
                    V.tensor_scalar(mask[:], pos[:], 0.0, None, ALU.is_ge)
                    link(V.tensor_scalar(t33[:], pos[:], float(SEQ), None, ALU.is_lt))
                    link(tt(mask[:], mask[:], t33[:], ALU.mult))
                    link(V.tensor_scalar(pos[:], pos[:], 0.0, float(SEQ - 1), ALU.max, ALU.min))
                    link(V.tensor_copy(cell_i[:], pos[:]))
                    link(V.tensor_copy(cell[:], cell_i[:]))
                    link(tt(t33[:], cell[:], pos[:], ALU.is_gt))
                    link(tt(cell[:], cell[:], t33[:], ALU.subtract))
                    V.scalar_tensor_tensor(out=index[:, bass.ds(k * SUBS, SUBS), :], in0=cell[:], scalar=first[:],
                                           in1=zero33[:], op0=ALU.add, op1=ALU.add)
                    tt(rel[:], over_tiles(grid_abs[:]), over_samples(avg[:, 0]), ALU.mult)
                    link(V.tensor_scalar(big[:, 0:SUBS], avg[:, 2], 0.1, None, ALU.max))
                    link(V.reciprocal(big2[:, 0:SUBS], big[:, 0:SUBS]))
                    link(V.tensor_scalar(big2[:, 0:SUBS], big2[:, 0:SUBS], -1.0, None, ALU.mult))
                    tt(env[:], rel[:], over_samples(big2[:, 0:SUBS]), ALU.mult).then_inc(s.env_in, 1)
                    link(tt(rel[:], rel[:], mask[:], ALU.mult))
                    link(V.tensor_scalar(t33[:], mask[:], 1.0e30, -1.0e30, ALU.mult, ALU.add))
                    for q in range(SUBS):
                        last = tt(sc[:, q * H:(q + 1) * H, :], rel[:, q].unsqueeze(1).to_broadcast([128, H, S]),
                                  qk[:, q].unsqueeze(2).to_broadcast([128, H, S]), ALU.mult)
                    link(last)
                    for q in range(SUBS):
                        last = tt(sc[:, q * H:(q + 1) * H, :], sc[:, q * H:(q + 1) * H, :],
                                  t33[:, q].unsqueeze(1).to_broadcast([128, H, S]), ALU.add)
                    link(last)
                    link(V.tensor_reduce(big[:], sc[:], AX.X, ALU.max))
                    wide = lambda a: a.unsqueeze(2).to_broadcast([128, SUBS * H, S])
                    tt(sc[:], sc[:], wide(big[:]), ALU.subtract).then_inc(s.exp_in, 1)
                    dve.wait_ge(s.exp_done, k + 1)
                    dve.wait_ge(s.env_done, k + 1)
                    link(V.tensor_reduce(big[:], sc[:], AX.X, ALU.add))
                    link(V.reciprocal(big2[:], big[:]))
                    link(tt(sc[:], sc[:], wide(big2[:]), ALU.mult))
                    link(tt(env[:], env[:], mask[:], ALU.mult))
                    for q in range(SUBS):
                        last = tt(sc[:, q * H:(q + 1) * H, :], sc[:, q * H:(q + 1) * H, :],
                                  env[:, q].unsqueeze(1).to_broadcast([128, H, S]), ALU.mult)
                    link(last)
                    link(V.tensor_reduce(big[:], sc[:], AX.X, ALU.add))
                    link(V.tensor_scalar(big[:], big[:], 1e-8, None, ALU.add))
                    link(V.reciprocal(big2[:], big[:]))
                    tt(attn[:, bass.ds(k * SUBS, SUBS)].rearrange("p q h s -> p (q h) s"), sc[:], wide(big2[:]),
                       ALU.mult).then_inc(s.done, 1)
                    assert links[0] == LINKS, links[0]
                dve.wait_ge(s.done, b * 2 + 3)
                V.tensor_scalar(first[:], first[:], float(SEQ), None, ALU.add).then_inc(s.next_first, 1)
                dve.wait_ge(s.next_first, b + 1)
    release(nc, s)


def wave_gather(nc, name, rows, attn, index, out):
    NT, H, S = TOKENS // 128, WAVE_HEADS, SAMPLES
    with ExitStack() as ctx:
        def sb(n, shape, dt=F32):
            return ctx.enter_context(nc.sbuf_tensor(f"{name}_{n}", shape, dt))

        turn_ps = ctx.enter_context(nc.psum_tensor(f"{name}_turn_ps", [128, 2, 512], F32))
        ident = sb("ident", [128, 128])
        vals = sb("vals", [128, 2, S, 128])
        idx = sb("idx", [128, 2, S], I32)
        acc = sb("acc", [128, 2, 128])
        s = semaphores(nc, name, "consts idx_ready gathered0 gathered1 weighted summed turned out_ready")
        gathered = (s.gathered0, s.gathered1)
        block = ctx.enter_context(nc.Block())

        @block.gpsimd
        def _(pool):
            pool.memset(ident[:], 0.0).then_inc(s.consts, 1)
            pool.wait_ge(s.consts, 1)
            pool.affine_select(out=ident[:], in_=ident[:], compare_op=ALU.not_equal, fill=1.0, base=0,
                               pattern=[[-1, 128]], channel_multiplier=1).then_inc(s.consts, 1)
            with pool.Fori(0, NT // 2) as i:
                for j in range(2):
                    pool.wait_ge(s.idx_ready, i * 2 + j + 3)
                    pool.wait_ge(s.summed, i * 2 + j + 1)
                    pool.nop(nofuse=True)
                    for n in range(S):
                        pool.indirect_dma_start(
                            out=vals[:, j, n, :], out_offset=None, in_=rows,
                            in_offset=bass.IndirectOffsetOnAxis(ap=idx[:, j, n:n + 1], axis=0)).then_inc(
                                gathered[j], 16)

        @block.scalar
        def _(act):
            act.sem_inc(s.idx_ready, 2)
            act.sem_inc(s.out_ready, 2)
            with act.Fori(0, NT // 2) as i:
                for j in range(2):
                    act.wait_ge(s.summed, i * 2 + j + 1)
                    act.nop(nofuse=True)
                    nc.scalar.copy(idx[:, j], index[:, bass.ds(i * 2 + j, 1), :].rearrange(
                        "p a s -> p (a s)")).then_inc(s.idx_ready, 1)
                for j in range(2):
                    act.wait_ge(s.turned, i * 2 + j + 1)
                    act.nop(nofuse=True)
                    nc.scalar.activation(out[:, bass.ds(i * 256 + j * 128, 128)], turn_ps[:, j, 0:128],
                                         ACT.Copy).then_inc(s.out_ready, 1)

        @block.vector
        def _(dve):
            dve.sem_inc(s.summed, 2)
            with dve.Fori(0, NT // 2) as i:
                for j in range(2):
                    k = i * 2 + j
                    dve.wait_ge(gathered[j], (i + 1) * (16 * S))
                    for n in range(H):
                        view = vals[:, j, :, 16 * n:16 * n + 16]
                        w = attn[:, bass.ds(k, 1), n, :].rearrange("p a s -> p (a s)").unsqueeze(2).to_broadcast(
                            [128, S, 16])
                        last = nc.vector.tensor_tensor(view, view, w, ALU.mult)
                    last.then_inc(s.weighted, 1)
                    dve.wait_ge(s.weighted, k + 1)
                    dve.wait_ge(s.out_ready, k + 1)
                    nc.vector.tensor_reduce(acc[:, j, :], vals[:, j].rearrange("p s c -> p c s"), AX.X,
                                            ALU.add).then_inc(s.summed, 1)

        @block.tensor
        def _(pe):
            pe.wait_ge(s.consts, 2)
            with pe.Fori(0, NT // 2) as i:
                for j in range(2):
                    pe.wait_ge(s.summed, i * 2 + j + 3)
                    pe.wait_ge(s.out_ready, i * 2 + j + 1)
                    nc.tensor.transpose(turn_ps[:, j, 0:128], acc[:, j, :], ident[:]).then_inc(s.turned, 1)
    release(nc, s)


def add_tile(nc, name, dst, src):
    s = semaphores(nc, name, "done")
    with nc.Block() as block:
        @block.vector
        def _(dve):
            with dve.Fori(0, 4) as i:
                tok = bass.ds(i * 1024, 1024)
                nc.vector.tensor_tensor(dst[:, tok], dst[:, tok], src[:, tok], ALU.add).then_inc(s.done, 1)

        @block.gpsimd
        def _(pool):
            pool.wait_ge(s.done, 4)
    release(nc, s)


def moe_weights(kind, w):
    col = column
    if kind == "L0":
        return dict(wr=w["gate_w"], br=w["gate_b"], wa=w["W1"], wd=w["W2"], bias_a=w["b1"],
                    down_bias=w["b2"])
    if kind == "L1":
        return dict(wr=w["gate_w"], br=w["gate_b"],
                    wa=w["rw1"][:, :, 0:128].rearrange("e d f -> d e f"),
                    wb=w["rw1"][:, :, 128:256].rearrange("e d f -> d e f"),
                    wd=w["rw2"].rearrange("e f d -> f e d"),
                    bias_a=w["rb1"][:, 0:128].rearrange("e f -> f e"),
                    bias_b=w["rb1"][:, 128:256].rearrange("e f -> f e"), down_bias=w["rb2"],
                    sa=w["sw1"][0, :, 0:128], sb=w["sw1"][0, :, 128:256], sd=w["sw2"][0],
                    bias_sa=col(w["sb1"][0, 0:128]), bias_sb=col(w["sb1"][0, 128:256]), bias_sd=col(w["sb2"][0]))
    if kind == "L2":
        return dict(wr=w["router_weight"], br=w["e_bias"],
                    wa=w["gate_w"],
                    wb=w["up_w"], wd=w["down_w"], sa=w["sh_gate_w"], sb=w["sh_up_w"], sd=w["sh_down_w"])
    return dict(wr=w["Wr"], br=w["br"], wa=w["Wg"], wb=w["Wu"],
                wd=w["Wd"].rearrange("(t e) i h -> (e i) t h", e=2),
                bias_a=w["bg"].rearrange("(t e) i -> (e i) t", e=2),
                bias_b=w["bu"].rearrange("(t e) i -> (e i) t", e=2), down_bias=w["bd"],
                sa=w["Wg_s"], sb=w["Wu_s"], sd=w["Wd_s"],
                bias_sa=col(w["bg_s"]), bias_sb=col(w["bu_s"]), bias_sd=col(w["bd_s"]))


def sub_params(a, prefix):
    return {k[len(prefix):]: v for k, v in a.items() if k.startswith(prefix)}


def program(nc, a, x_dram, out_dram, stages):
    with ExitStack() as ctx:
        x = ctx.enter_context(nc.sbuf_tensor("x", [128, TOKENS], F32))
        xn = ctx.enter_context(nc.sbuf_tensor("xn", [128, TOKENS], F32))
        s = semaphores(nc, "io", "loaded stored")
        with nc.Block() as block:
            @block.sync
            def _(sp):
                sp.dma_start(x[:], x_dram).then_inc(s.loaded, 16)
                sp.wait_ge(s.loaded, 16)
        scratch = nc.dram_tensor("heads", (2, PARTS, BATCH * HEADS, DH, SEQ), BF16, kind="Internal").ap()
        for n in stages:
            if n in (1, 3):
                p = sub_params(a, "L0_ffn_")
                norm(nc, f"n{n}", [x], [xn], 1e-5)
                with ExitStack() as inner:
                    h = inner.enter_context(nc.sbuf_tensor(f"h{n}", [128, TOKENS], F32))
                    v_all = inner.enter_context(nc.sbuf_tensor(f"v{n}", [128, BATCH * HEADS, 8, DH + 1], F32))
                    norm(nc, f"na{n}", [xn], [h], 1e-5, gain=p["ln1_g"], shift=p["ln1_b"])
                    q = dict(interleaved=False, causal=False, wq=p["w_qkv"][:, 0:128], wk=p["w_qkv"][:, 128:256],
                             wv=p["w_qkv"][:, 256:384], bq=p["b_qkv"][0:128], bk=p["b_qkv"][128:256],
                             bv=p["b_qkv"][256:384], wo=p["w_o"], bo=p["b_o"])
                    attention_inputs(nc, f"i{n}", h, scratch, v_all, q)
                    attention(nc, f"a{n}", scratch, v_all, xn, q)
                with ExitStack() as inner:
                    h = inner.enter_context(nc.sbuf_tensor(f"hm{n}", [128, TOKENS], F32))
                    add_tile(nc, f"r{n}", x, xn)
                    norm(nc, f"nb{n}", [xn], [h], 1e-5, gain=p["ln2_g"], shift=p["ln2_b"])
                    moe(nc, f"m{n}", "L0", h, x, moe_weights("L0", p))
            if n == 0:
                p = sub_params(a, "L0_attn_a_")
                norm(nc, f"n{n}", [x], [xn], 1e-5)
                with ExitStack() as inner:
                    tile = lambda m, r=128: inner.enter_context(nc.sbuf_tensor(f"{m}{n}", [r, TOKENS], F32))
                    o = tile("o")
                    rows = nc.dram_tensor("rows", (TOKENS, C), F32, kind="Internal").ap()
                    with ExitStack() as weights:
                        attn = weights.enter_context(nc.sbuf_tensor(
                            "wave_attn", [128, TOKENS // 128, WAVE_HEADS, SAMPLES], F32))
                        index = weights.enter_context(nc.sbuf_tensor(
                            "wave_index", [128, TOKENS // 128, SAMPLES], I32))
                        wave_attention_weights(nc, f"w{n}", xn, rows, attn, index, p)
                        wave_gather(nc, f"g{n}", rows, attn, index, o)
                    se1, se = tile("se1", 32), tile("se")
                    project(nc, f"p1{n}", [o], [dict(dst=se1, func=ACT.Silu, w=[p["w_se1"]], bias=p["b_se1"])])
                    project(nc, f"p2{n}", [se1], [dict(dst=se, func=ACT.Sigmoid, w=[p["w_se2"]], bias=p["b_se2"])])
                    pointwise(nc, f"e{n}", [(o, o, se, ALU.mult)])
                    project(nc, f"po{n}", [o], [dict(dst=se, func=ACT.Silu, w=[p["w_out"]])])
                    add_tile(nc, f"r{n}", x, se)
            if n == 2:
                p = sub_params(a, "L0_attn_b_")
                norm(nc, f"n{n}", [x], [xn], 1e-5)
                with ExitStack() as inner:
                    tile = lambda m, r=128: inner.enter_context(nc.sbuf_tensor(f"{m}{n}", [r, TOKENS], F32))
                    u, z = [tile("u0"), tile("u1")], [tile("z0"), tile("z1")]
                    cut = lambda m: [p["W_in"][:, 128 * m:128 * m + 128]]
                    project(nc, f"p{n}", [xn], [dict(dst=u[m], func=ACT.Silu, w=cut(m)) for m in range(2)])
                    project(nc, f"pz{n}", [xn], [dict(dst=z[m], func=ACT.Sigmoid, w=cut(2 + m)) for m in range(2)])
                    pointwise(nc, f"e{n}", [(u[m], u[m], z[m], ALU.mult) for m in range(2)])
                    rows = dict(A=z[0], B=z[1], C=xn)
                    project(nc, f"pr{n}", u, [dict(dst=rows[c], w=[p["W_" + c][0:128, :], p["W_" + c][128:256, :]])
                                              for c in "ABC"])
                    clipped_decay(nc, f"d{n}", rows["A"][0:16])
                    selective_scan(nc, f"s{n}", u, rows["B"][0:16], rows["C"][0:16], u, decay_rows=rows["A"][0:16])
                    norm(nc, f"nb{n}", u, u, 1.1920929e-07, center=False, gain=p["norm_w"])
                    project(nc, f"po{n}", u, [dict(dst=x, add=True, w=[p["W_out"][128 * m:128 * m + 128, :]
                                                                        for m in range(2)])])
            if n == 4:
                p = sub_params(a, "L1_attn_a_")
                norm(nc, f"n{n}", [x], [xn], 1e-5)
                with ExitStack() as inner:
                    tile = lambda m, r=128: inner.enter_context(nc.sbuf_tensor(f"{m}{n}", [r, TOKENS], F32))
                    xc, dl, u = ([tile(f"{m}{r}") for r in range(2)] for m in ("xc", "dl", "u"))
                    norm(nc, f"na{n}", [xn], [u[0]], 1e-5, center=False, gain=p["norm_w"])
                    half = lambda m: slice(128 * m, 128 * m + 128)
                    project(nc, f"p{n}", [u[0]], [dict(dst=xc[m], w=[p["in_w"][:, half(m)]]) for m in range(2)])
                    causal_conv(nc, f"c{n}", xc, p["conv_w"], p["conv_b"])
                    project(nc, f"pd{n}", xc, [dict(dst=u[0], w=[p["wd1"][half(m), :] for m in range(2)])])
                    project(nc, f"pe{n}", [u[0]], [dict(dst=dl[m], w=[p["wd2"][:, half(m)]], bias=p["wd2_b"][half(m)])
                                                  for m in range(2)])
                    softplus(nc, f"sp{n}", dl)
                    pointwise(nc, f"e{n}", [(u[m], dl[m], xc[m], ALU.mult) for m in range(2)])
                    with ExitStack() as rows_ctx:
                        rows = {c: rows_ctx.enter_context(nc.sbuf_tensor(f"rows_{c}{n}", [16, TOKENS], F32))
                                for c in "bc"}
                        project(nc, f"pr{n}", xc, [dict(dst=rows[c], w=[p["w" + c][half(m), :] for m in range(2)])
                                                  for c in "bc"])
                        selective_scan(nc, f"s{n}", u, rows["b"], rows["c"], u, delta=dl, a_log=p["A_log"])
                    pointwise(nc, f"f{n}", [(u[m], xc[m], p["W_D"][half(m)], u[m], ALU.mult, ALU.add)
                                           for m in range(2)])
                    norm(nc, f"nb{n}", [xn], [dl[0]], 1e-5, center=False, gain=p["norm_w"])
                    project(nc, f"ps{n}", [dl[0]], [dict(dst=xc[m], func=ACT.Silu, w=[p["skip_w"][:, half(m)]])
                                                    for m in range(2)])
                    pointwise(nc, f"g{n}", [(u[m], u[m], xc[m], ALU.mult) for m in range(2)] + [(x, x, xn, ALU.add)])
                    project(nc, f"po{n}", u, [dict(dst=x, add=True, w=[p["out_w"][half(m), :] for m in range(2)])])
            if n == 14:
                p = sub_params(a, "L3_attn_b_")
                norm(nc, f"n{n}", [x], [xn], 1e-5)
                with ExitStack() as inner:
                    tile = lambda m, r=128: inner.enter_context(nc.sbuf_tensor(f"{m}{n}", [r, TOKENS], F32))
                    q, k, v, gate = tile("q"), tile("k"), tile("v"), tile("gate", 16)
                    project(nc, f"p{n}", [xn], [dict(dst=q, w=[p["Wq"]]), dict(dst=k, w=[p["Wk"]]),
                                                dict(dst=v, w=[p["Wv"]])])
                    project(nc, f"pg{n}", [xn], [dict(dst=gate, func=ACT.Sigmoid, w=[p["Wg"]], bias=p["bg"])])
                    feature_map(nc, f"f{n}", q, k, float(DH) ** -0.5)
                    gated_linear_attention(nc, f"l{n}", q, k, v, gate, q)
                    project(nc, f"po{n}", [q], [dict(dst=x, add=True, w=[p["Wo"]])])
            if n == 6:
                p = sub_params(a, "L1_attn_b_")
                norm(nc, f"n{n}", [x], [xn], 1e-5)
                with ExitStack() as inner:
                    tile = lambda m: inner.enter_context(nc.sbuf_tensor(f"{m}{n}", [128, TOKENS], F32))
                    h, xc, z = tile("h"), [tile("xc0"), tile("xc1")], [tile("z0"), tile("z1")]
                    norm(nc, f"na{n}", [xn], [h], 1e-5, gain=p["norm_w"], shift=p["norm_b"])
                    cut = lambda m: dict(w=[p["in_w"][:, 128 * m:128 * m + 128]], bias=p["in_b"][128 * m:128 * m + 128])
                    project(nc, f"p{n}", [h], [dict(dst=xc[m], **cut(m)) for m in range(2)])
                    project(nc, f"pz{n}", [h], [dict(dst=z[m], func=ACT.Silu, **cut(2 + m)) for m in range(2)])
                    causal_conv(nc, f"c{n}", xc, p["conv_w"], p["conv_b"])
                    mean_gate(nc, f"g{n}", xc, h, p["xproj_w"][:, 17:33])
                    pointwise(nc, f"e{n}", [st for m in range(2) for st in (
                        (xc[m], h, p["D"][128 * m:128 * m + 128], xc[m], ALU.add, ALU.mult),
                        (xc[m], xc[m], z[m], ALU.mult))] + [(x, x, xn, ALU.add)])
                    project(nc, f"po{n}", xc, [dict(dst=x, add=True, bias=p["out_b"],
                                                    w=[p["out_w"][128 * m:128 * m + 128, :] for m in range(2)])])
            if n == 8:
                p = sub_params(a, "L2_attn_a_")
                norm(nc, f"n{n}", [x], [xn], 1e-5)
                with ExitStack() as inner:
                    tile = lambda m: inner.enter_context(nc.sbuf_tensor(f"{m}{n}", [128, TOKENS], F32))
                    h, u = tile("h"), [tile(f"u{m}") for m in range(4)]
                    norm(nc, f"na{n}", [xn], [h], 1e-5, gain=p["ln_conv_g"], shift=p["ln_conv_b"])
                    grouped_conv(nc, f"c{n}", h, xn, p["conv_w"], p["conv_b"])
                    norm(nc, f"nb{n}", [xn], [h], 1e-5, gain=p["ln_attn_g"], shift=p["ln_attn_b"])
                    project(nc, f"p{n}", [h], [dict(dst=u[m], w=[p["W" + c]], bias=p["b" + c])
                                               for m, c in enumerate("qkv")])
                    pooled_mix(nc, f"m{n}", u[0], u[1], u[2], xn)
                    norm(nc, f"nc{n}", [xn], [h], 1e-5, gain=p["ln_boom_g"], shift=p["ln_boom_b"])
                    project(nc, f"pb{n}", [h], [dict(dst=u[m], func=ACT.Gelu, w=[p["Wb"][:, 128 * m:128 * m + 128]],
                                                     bias=p["bb"][128 * m:128 * m + 128]) for m in range(4)])
                    add_tile(nc, f"r{n}", x, xn)
                    project(nc, f"pu{n}", u, [dict(dst=x, add=True, bias=p["bu"],
                                                   w=[p["Wu"][128 * m:128 * m + 128, :] for m in range(4)])])
            if n == 10:
                p = sub_params(a, "L2_attn_b_")
                norm(nc, f"n{n}", [x], [xn], 1e-5)
                with ExitStack() as inner:
                    v_all = inner.enter_context(nc.sbuf_tensor(f"v{n}", [128, BATCH * HEADS, 8, DH + 1], F32))
                    q = dict(interleaved=True, causal=False, wq=p["W_qkv"][0], wk=p["W_qkv"][1], wv=p["W_qkv"][2],
                             bq=p["b_qkv"][0], bk=p["b_qkv"][1],
                             bv=p["b_qkv"][2].rearrange("(r n) -> r n", r=2), wo=p["W_out"], bo=p["b_out"])
                    attention_inputs(nc, f"i{n}", xn, scratch, v_all, q)
                    attention(nc, f"a{n}", scratch, v_all, x, q)
            if n == 12:
                p = sub_params(a, "L3_attn_a_")
                norm(nc, f"n{n}", [x], [xn], 1e-5)
                norm(nc, f"na{n}", [xn], [xn], 1e-5, gain=p["g_ln"])
                with ExitStack() as inner:
                    v_all = inner.enter_context(nc.sbuf_tensor(f"v{n}", [128, BATCH * HEADS, 8, DH + 1], F32))
                    q = dict(interleaved=False, causal=True, wq=p["Wq"], wk=p["Wkv"][:, 0:128],
                             wv=p["Wkv"][:, 128:256], wo=p["Wo"])
                    attention_inputs(nc, f"i{n}", xn, scratch, v_all, q)
                    attention(nc, f"a{n}", scratch, v_all, x, q)
            if n in (5, 7, 9, 11, 13, 15):
                kind = "L" + str(n // 4)
                norm(nc, f"n{n}", [x], [xn], 1e-5)
                moe(nc, f"m{n}", kind, xn, x, moe_weights(kind, sub_params(a, kind + "_ffn_")))
        with nc.Block() as block:
            @block.sync
            def _(sp):
                sp.dma_start(out_dram, x[:]).then_inc(s.stored, 16)
                sp.wait_ge(s.stored, 16)


def layouts(inputs):
    import numpy as np

    t = {k: np.asarray(v) for k, v in inputs.items()}
    out = dict(t)
    T = lambda name, *axes: out.__setitem__(name, np.ascontiguousarray(t[name].transpose(*axes)))
    out["L0_ffn_W1"] = np.ascontiguousarray(t["L0_ffn_W1"].transpose(1, 0, 2)).reshape(128, 32, 128)
    out["L0_ffn_W2"] = np.ascontiguousarray(t["L0_ffn_W2"].reshape(32, 128, 128).transpose(1, 0, 2))
    out["L0_ffn_b1"] = np.ascontiguousarray(t["L0_ffn_b1"].reshape(32, 128).T)
    T("L2_ffn_router_weight", 1, 0)
    for n in ("L1_attn_b_in_w", "L1_attn_b_xproj_w", "L1_attn_b_out_w", "L2_attn_a_Wq", "L2_attn_a_Wk",
              "L2_attn_a_Wv", "L2_attn_a_Wb", "L2_attn_a_Wu", "L1_attn_a_skip_w", "L1_attn_a_in_w",
              "L1_attn_a_wd1", "L1_attn_a_wd2", "L1_attn_a_wb", "L1_attn_a_wc", "L1_attn_a_out_w",
              "L3_attn_b_Wq", "L3_attn_b_Wk", "L3_attn_b_Wv", "L3_attn_b_Wo", "L3_attn_b_Wg"):
        T(n, 1, 0)
    out["L1_attn_b_conv_w"] = t["L1_attn_b_conv_w"].reshape(256, 4)
    T("L2_attn_a_conv_w", 2, 1, 0)
    for n in ("gate_w", "up_w"):
        out["L2_ffn_" + n] = np.ascontiguousarray(t["L2_ffn_" + n].transpose(2, 0, 1)).reshape(128, 8, 128)
    out["L2_ffn_down_w"] = np.ascontiguousarray(
        t["L2_ffn_down_w"].reshape(8, 2, 128, 64).transpose(1, 3, 0, 2)).reshape(128, 8, 128)
    for n in ("sh_gate_w", "sh_up_w", "sh_down_w"):
        T("L2_ffn_" + n, 1, 0)
    f = t["L2_attn_b_W_qkv"].reshape(16, 3, 8, 128)
    fb = t["L2_attn_b_b_qkv"].reshape(16, 3, 8)
    qk, qkb = f[:, 0:2].transpose(1, 3, 2, 0).reshape(2, 128, 128), fb[:, 0:2].transpose(1, 2, 0).reshape(2, 128)
    v = f[:, 2].reshape(8, 2, 8, 128).transpose(3, 1, 0, 2).reshape(1, 128, 128)
    vb = fb[:, 2].reshape(8, 2, 8).transpose(1, 0, 2).reshape(1, 128)
    out["L2_attn_b_W_qkv"] = np.ascontiguousarray(np.concatenate([qk, v]))
    out["L2_attn_b_b_qkv"] = np.ascontiguousarray(np.concatenate([qkb, vb]))
    T("L2_attn_b_W_out", 1, 0)
    for n in ("Wg", "Wu"):
        out["L3_ffn_" + n] = np.ascontiguousarray(t["L3_ffn_" + n].transpose(1, 0, 2)).reshape(128, 16, 128)
    return out


def kernel(**inputs):
    import numpy as np
    import concourse.bacc as bacc
    from concourse.bass_utils import run_bass_kernel_spmd

    nc = bacc.Bacc("TRN2", target_bir_lowering=False, num_devices=1)
    arrays, a = {}, {}
    for name, value in layouts(inputs).items():
        if value.dtype.kind in "iu":
            continue
        if name == "L0_attn_a_x":
            value = np.ascontiguousarray(value.reshape(TOKENS, C).T)
        arrays[f"in_{name}"] = value
        a[name] = nc.dram_tensor(f"in_{name}", value.shape, mybir.dt.from_np(value.dtype), kind="ExternalInput").ap()
    out = nc.dram_tensor("out", (C, TOKENS), F32, kind="ExternalOutput").ap()
    program(nc, a, a["L0_attn_a_x"], out, range(16))
    result = run_bass_kernel_spmd(nc, [arrays], core_ids=[0])
    return np.ascontiguousarray(result.results[0]["out"].T).reshape(BATCH, SEQ, C)
```

```python
from collections import namedtuple
from contextlib import ExitStack

import concourse.bass as bass
from concourse import mybir

F32 = mybir.dt.float32
BF16 = mybir.dt.bfloat16
I32 = mybir.dt.int32
U32 = mybir.dt.uint32
ALU = mybir.AluOpType
ACT = mybir.ActivationFunctionType
AX = mybir.AxisListType

BATCH, SEQ, C = 4, 1024, 128
TOKENS = BATCH * SEQ
TB = 512
NTB = TOKENS // TB


def semaphores(nc, stage, names):
    return namedtuple("Semaphores", names)(*(nc.alloc_semaphore(f"{stage}_{n}") for n in names.split()))


def release(nc, sems):
    nc.clear_and_free_semaphores(list(sems))
    nc.all_engine_barrier()


def column(vector):
    return vector.rearrange("(p a) -> p a", a=1)


def norm(nc, name, src, dst, eps, center=True, gain=None, shift=None):
    nt = len(src)
    SUB = TB // 128
    with ExitStack() as ctx:
        def sb(n, shape):
            return ctx.enter_context(nc.sbuf_tensor(f"{name}_{n}", shape, F32))

        wide_ps = ctx.enter_context(nc.psum_tensor(f"{name}_wide", [128, 2, TB], F32))
        var_ps = ctx.enter_context(nc.psum_tensor(f"{name}_var", [128, TB], F32))
        average = sb("average", [128, 128])
        ident = sb("ident", [128, 128])
        eps_col = sb("eps", [128, 1])
        sq = sb("sq", [128, 2, nt, TB])
        std = sb("std", [128, NTB * SUB])
        rstd = sb("rstd", [128, NTB * SUB])
        par = sb("par", [128, 2, nt])
        s = semaphores(nc, name, "consts params mean centered squared var std_ready rstd_ready spread scaled shifted")
        n_par = (gain is not None) + (shift is not None)
        block = ctx.enter_context(nc.Block())

        def tokens(i, j):
            return bass.ds(i * (2 * TB) + j * TB, TB)

        @block.sync
        def _(sp):
            for n, vector in enumerate((gain, shift)):
                if vector is not None:
                    with nc.allow_non_contiguous_dma("one value per partition"):
                        sp.dma_start(par[:, n, :], vector.rearrange("(t p) -> p t", p=128)).then_inc(s.params, 16)

        @block.gpsimd
        def _(pool):
            pool.memset(average[:], 1.0 / (128 * nt)).then_inc(s.consts, 1)
            pool.memset(eps_col[:], eps).then_inc(s.consts, 1)
            pool.memset(ident[:], 0.0).then_inc(s.consts, 1)
            pool.wait_ge(s.consts, 3)
            pool.affine_select(out=ident[:], in_=ident[:], compare_op=ALU.not_equal, fill=1.0, base=0,
                               pattern=[[-1, 128]], channel_multiplier=1).then_inc(s.consts, 1)

        @block.tensor
        def _(pe):
            pe.wait_ge(s.consts, 4)

            def mean(k):
                pe.wait_ge(s.centered, k + 1)
                pe.nop(nofuse=True)
                nc.tensor.matmul(wide_ps[:, k % 2, :], average[:], src[0][:, k * TB:(k + 1) * TB],
                                 start=True, stop=True).then_inc(s.mean, 1)

            if center:
                mean(0)
                mean(1)
            for k in range(NTB):
                pe.wait_ge(s.squared, k + 1)
                for q in range(SUB):
                    for t in range(nt):
                        mm = nc.tensor.matmul(var_ps[:, k * SUB + q:k * SUB + q + 1],
                                              sq[:, k % 2, t, q * 128:(q + 1) * 128], average[:, 0:1],
                                              start=(t == 0), stop=(t == nt - 1))
                mm.then_inc(s.var, 1)
                if center and k + 2 < NTB:
                    mean(k + 2)
            pe.wait_ge(s.rstd_ready, 1)
            for k in range(NTB):
                pe.wait_ge(s.scaled, k + 1)
                for q in range(SUB):
                    c = k * SUB + q
                    mm = nc.tensor.matmul(wide_ps[:, k % 2, q * 128:(q + 1) * 128],
                                          rstd[:, c:c + 1].to_broadcast([128, 128]), ident[:],
                                          start=True, stop=True)
                mm.then_inc(s.spread, 1)

        @block.scalar
        def _(act):
            act.wait_ge(s.consts, 4)
            with act.Fori(0, NTB // 2) as i:
                for j in range(2):
                    if center:
                        act.wait_ge(s.centered, i * 2 + j + 3)
                    act.wait_ge(s.var, i * 2 + j + 1)
                    act.nop(nofuse=True)
                    for t in range(nt):
                        a = nc.scalar.activation(sq[:, j, t, :], (dst if center else src)[t][:, tokens(i, j)],
                                                 ACT.Square)
                    a.then_inc(s.squared, 1)
            act.wait_ge(s.var, NTB + 2)
            nc.scalar.activation(std[:], var_ps[:, 0:NTB * SUB], ACT.Sqrt, bias=eps_col[:]).then_inc(s.std_ready, 1)
            if shift is not None:
                act.wait_ge(s.params, 16 * n_par)
                with act.Fori(0, NTB // 2) as i:
                    for j in range(2):
                        act.wait_ge(s.scaled, i * 2 + j + 3)
                        act.nop(nofuse=True)
                        for t in range(nt):
                            d = dst[t][:, tokens(i, j)]
                            a = nc.scalar.activation(d, d, ACT.Identity, bias=par[:, 1, t:t + 1])
                        a.then_inc(s.shifted, 1)

        @block.vector
        def _(dve):
            dve.sem_inc(s.centered, 2)
            dve.sem_inc(s.var, 2)
            dve.sem_inc(s.scaled, 2)
            if center:
                with dve.Fori(0, NTB // 2) as i:
                    for j in range(2):
                        dve.wait_ge(s.mean, i * 2 + j + 1)
                        nc.vector.tensor_tensor(dst[0][:, tokens(i, j)], src[0][:, tokens(i, j)],
                                                wide_ps[:, j, :], ALU.subtract).then_inc(s.centered, 1)
            if n_par:
                dve.wait_ge(s.params, 16 * n_par)
            dve.wait_ge(s.squared, NTB)
            dve.wait_ge(s.std_ready, 1)
            nc.vector.reciprocal(rstd[:], std[:]).then_inc(s.rstd_ready, 1)
            with dve.Fori(0, NTB // 2) as i:
                for j in range(2):
                    dve.wait_ge(s.spread, i * 2 + j + 1)
                    for t in range(nt):
                        d, value = dst[t][:, tokens(i, j)], (dst if center else src)[t][:, tokens(i, j)]
                        if gain is not None:
                            v = nc.vector.scalar_tensor_tensor(out=d, in0=value, scalar=par[:, 0, t:t + 1],
                                                               in1=wide_ps[:, j, :], op0=ALU.mult, op1=ALU.mult)
                        else:
                            v = nc.vector.tensor_tensor(d, value, wide_ps[:, j, :], ALU.mult)
                    v.then_inc(s.scaled, 1)
    release(nc, s)


MOE = {
    "L0": dict(E=8, F=512, shared=0, glu=False),
    "L1": dict(E=8, F=128, shared=128, glu=True),
    "L2": dict(E=16, F=64, shared=128, glu=True),
    "L3": dict(E=32, F=64, shared=64, glu=True),
}


def moe(nc, name, kind, h, x, w):
    cfg = MOE[kind]
    E, F, shared, glu = cfg["E"], cfg["F"], cfg["shared"], cfg["glu"]
    n_routed = E * F // 128
    tiles = ([-1] if shared else []) + list(range(n_routed))
    NT = len(tiles)
    SUB = TB // 128
    has_bias = w.get("bias_a") is not None
    has_down_bias = w.get("down_bias") is not None
    with ExitStack() as ctx:
        def sb(n, shape, dt=F32):
            return ctx.enter_context(nc.sbuf_tensor(f"{name}_{n}", shape, dt))

        def ps(n, shape):
            return ctx.enter_context(nc.psum_tensor(f"{name}_{n}", shape, F32))

        gate_ps = ps("gate_ps", [128, 2, TB])
        up_ps = ps("up_ps", [128, 2, TB]) if glu else None
        weight_ps = ps("weight_ps", [128, 2, TB])
        out_ps = ps("out_ps", [128, TB])
        route_ps = ps("route_ps", [128, TB])

        wa = sb("wa", [128, n_routed, 128])
        wb = sb("wb", [128, n_routed, 128]) if glu else None
        wd = sb("wd", [128, n_routed, 128])
        sa, sbb, sd = (sb("sa", [128, shared]), sb("sbb", [128, shared]), sb("sd", [shared, 128])) if shared else (None,) * 3
        ba, bb = sb("ba", [128, n_routed]), sb("bb", [128, n_routed])
        bsa, bsb, bsd = sb("bsa", [128, 1]), sb("bsb", [128, 1]), sb("bsd", [128, 1])
        bd = sb("bd", [96, 128])
        wr = sb("wr", [128, E])
        br = sb("br", [128, E])
        sel = sb("sel", [96, n_routed, 128], BF16)
        ident_bf = sb("ident_bf", [128, 128], BF16)
        hb = sb("hb", [128, TB])
        gated = sb("gated", [128, 2, TB])
        hid1 = sb("hid1", [128, 2, TB])
        hid = sb("hid", [128, 2, TB])
        wT = sb("wT", [96, TB], BF16)
        wT32 = sb("wT32", [96, TB]) if has_down_bias else None
        lg = sb("lg", [128, SUB, E])
        rt = sb("rt", [128, SUB, E])
        rw = sb("rw", [128, SUB, E])
        rest = sb("rest", [128, SUB, E])
        parts = sb("parts", [128, SUB, 3, 32], BF16)
        small = sb("small", [128, 4, SUB])
        if kind != "L3":
            later = sb("later", [128, E, E])
            cmp = sb("cmp", [128, SUB, E, E])
            tie = sb("tie", [128, SUB, E, E])
            rank = sb("rank", [128, SUB, E])
        if kind == "L2":
            grank = sb("grank", [128, SUB, 4])
            gsc = sb("gsc", [128, SUB, 4])
            masked = sb("masked", [128, SUB, E])
        top8 = sb("top8", [128, SUB, 8])
        s = semaphores(nc, name, "loads consts copied logits route expd weights wt_ps wt gate up gated_ready "
                                 "hid1_ready hid_ready wps out out_read chain cleared")

        loads = []
        for tile, key in ((wa, "wa"), (wb, "wb"), (wd, "wd"), (sa, "sa"), (sbb, "sb"), (sd, "sd"), (wr, "wr")):
            if w.get(key) is not None:
                loads.append((tile[:], w[key]))
        if has_bias:
            loads.append((ba[:], w["bias_a"]))
            if glu:
                loads.append((bb[:], w["bias_b"]))
        if shared and w.get("bias_sa") is not None:
            loads += [(bsa[0:shared, :], w["bias_sa"]), (bsb[0:shared, :], w["bias_sb"])]
        if shared and w.get("bias_sd") is not None:
            loads.append((bsd[:], w["bias_sd"]))
        if has_down_bias:
            loads += [(bd[32 * n:32 * n + E, :], w["down_bias"]) for n in range(3)]
        if w.get("br") is not None:
            loads.append((br[:], w["br"].partition_broadcast(128)))
        shared_bias = shared and w.get("bias_sa") is not None

        block = ctx.enter_context(nc.Block())

        @block.sync
        def _(sp):
            if has_down_bias:
                sp.wait_ge(s.cleared, 1)
            with nc.allow_non_contiguous_dma("parameters, one value per partition"):
                for to, source in loads:
                    sp.dma_start(to, source).then_inc(s.loads, 16)

        @block.gpsimd
        def _(pool):
            if has_down_bias:
                pool.memset(bd[:], 0.0).then_inc(s.cleared, 1)
            pool.memset(ident_bf[:], 0.0).then_inc(s.consts, 1)
            pool.memset(sel[:], 1.0).then_inc(s.consts, 1)
            pool.memset(parts[:], 0.0).then_inc(s.consts, 1)
            n = 3
            if kind != "L3":
                pool.memset(later[:], 1.0).then_inc(s.consts, 1)
                n += 1
            pool.wait_ge(s.consts, n)
            pool.affine_select(out=ident_bf[:], in_=ident_bf[:], compare_op=ALU.not_equal, fill=1.0, base=0,
                               pattern=[[-1, 128]], channel_multiplier=1).then_inc(s.consts, 1)
            for part in range(3):
                rows = sel[32 * part:32 * part + 32]
                pool.affine_select(out=rows, in_=rows, compare_op=ALU.is_ge, fill=0.0, base=0,
                                   pattern=[[128, n_routed], [1, 128]], channel_multiplier=-F).then_inc(s.consts, 1)
                pool.wait_ge(s.consts, n + 2 + 2 * part)
                pool.affine_select(out=rows, in_=rows, compare_op=ALU.is_ge, fill=0.0, base=F - 1,
                                   pattern=[[-128, n_routed], [-1, 128]], channel_multiplier=F).then_inc(s.consts, 1)
                pool.wait_ge(s.consts, n + 3 + 2 * part)
            if kind != "L3":
                pool.affine_select(out=later[:], in_=later[:], compare_op=ALU.is_gt, fill=0.0, base=0,
                                   pattern=[[1, E], [-1, E]], channel_multiplier=0).then_inc(s.consts, 1)

        CONSTS = 10 if kind == "L3" else 12

        @block.tensor
        def _(pe):
            pe.wait_ge(s.consts, CONSTS)
            pe.wait_ge(s.loads, 16 * len(loads))

            def logits(b):
                pe.wait_ge(s.copied, b + 1)
                pe.wait_ge(s.wt, b + 1)
                for q in range(SUB):
                    mm = nc.tensor.matmul(route_ps[:, q * E:(q + 1) * E], hb[:, q * 128:(q + 1) * 128], wr[:],
                                          start=True, stop=True)
                mm.then_inc(s.logits, 1)

            def experts(b, last_block):
                tok = bass.ds(b * TB, TB)

                def project(n):
                    t = tiles[n]
                    rows = shared if t < 0 else 128
                    pe.wait_ge(s.gated_ready, b * NT + n + 1)
                    pe.nop(nofuse=True)
                    nc.tensor.matmul(gate_ps[0:rows, n % 2, :], sa[:] if t < 0 else wa[:, t, :], h[:, tok],
                                     start=True, stop=True).then_inc(s.gate, 1)
                    if glu:
                        pe.wait_ge(s.hid1_ready, b * NT + n + 1)
                        pe.nop(nofuse=True)
                        nc.tensor.matmul(up_ps[0:rows, n % 2, :], sbb[:] if t < 0 else wb[:, t, :], h[:, tok],
                                         start=True, stop=True).then_inc(s.up, 1)

                def spread(n):
                    t = tiles[n]
                    if t >= 0:
                        pe.wait_ge(s.hid_ready, b * NT + n + 1)
                        nc.tensor.matmul(weight_ps[:, n % 2, :], sel[:, t, :], wT[:],
                                         start=True, stop=True).then_inc(s.wps, 1)

                def down(n):
                    t = tiles[n]
                    rows = shared if t < 0 else 128
                    pe.wait_ge(s.hid_ready, b * NT + n + 3)
                    last = n == NT - 1
                    mm = nc.tensor.matmul(out_ps[:], sd[:] if t < 0 else wd[:, t, :], hid[0:rows, n % 2, :],
                                          start=(n == 0 and not has_down_bias), stop=last)
                    return mm

                project(0)
                project(1)
                pe.wait_ge(s.weights, b + 1)
                for q in range(SUB):
                    mm = nc.tensor.matmul(route_ps[0:96, q * 128:(q + 1) * 128],
                                          parts[:, q].rearrange("p n e -> p (n e)"), ident_bf[:],
                                          start=True, stop=True)
                mm.then_inc(s.wt_ps, 1)
                pe.wait_ge(s.wt, b + 2)
                spread(0)
                pe.wait_ge(s.out_read, b + 1)
                if has_down_bias:
                    nc.tensor.matmul(out_ps[:], bd[:], wT32[:], start=True, stop=False)
                spread(1)
                for n in range(2, NT):
                    if n == 2 and not last_block:
                        logits(b + 1)
                    project(n)
                    down(n - 2)
                    spread(n)
                down(NT - 2)
                down(NT - 1).then_inc(s.out, 1)

            logits(0)
            with pe.Fori(0, NTB - 1) as b:
                experts(b, last_block=False)
            experts(NTB - 1, last_block=True)

        @block.scalar
        def _(act):
            act.sem_inc(s.wt, 1)
            act.sem_inc(s.gated_ready, 2)
            act.wait_ge(s.loads, 16 * len(loads))

            def tokens(b):
                nc.scalar.activation(hb[:], h[:, bass.ds(b * TB, TB)], ACT.Copy).then_inc(s.copied, 1)

            def route(b):
                act.wait_ge(s.route, b + 1)
                nc.scalar.activation(rt[:], lg[:], ACT.Exp if kind in ("L0", "L1") else ACT.Sigmoid).then_inc(
                    s.expd, 1)

            def experts(b, last_block):
                for n, t in enumerate(tiles):
                    rows = shared if t < 0 else 128
                    act.wait_ge(s.gate, b * NT + n + 1)
                    act.wait_ge(s.hid1_ready, b * NT + n + 1)
                    bias = 0.0
                    if t < 0 and shared_bias:
                        bias = bsa[0:rows, :]
                    elif t >= 0 and has_bias:
                        bias = ba[:, t:t + 1]
                    nc.scalar.activation(gated[0:rows, n % 2, :], gate_ps[0:rows, n % 2, :],
                                         ACT.Silu if glu else ACT.Relu, bias=bias).then_inc(s.gated_ready, 1)
                    if n == 1:
                        act.wait_ge(s.wt_ps, b + 1)
                        if has_down_bias:
                            nc.scalar.activation(wT32[:], route_ps[0:96, :], ACT.Copy)
                        nc.scalar.activation(wT[:], route_ps[0:96, :], ACT.Copy).then_inc(s.wt, 1)
                        if not last_block:
                            act.wait_ge(s.logits, b + 1)
                            act.nop(nofuse=True)
                            tokens(b + 1)
                    if n == 2 and not last_block:
                        route(b + 1)

            tokens(0)
            route(0)
            with act.Fori(0, NTB - 1) as b:
                experts(b, last_block=False)
            experts(NTB - 1, last_block=True)

        @block.vector
        def _(dve):
            dve.sem_inc(s.hid1_ready, 2)
            dve.sem_inc(s.hid_ready, 2)
            dve.sem_inc(s.out_read, 1)
            dve.wait_ge(s.loads, 16 * len(loads))
            dve.wait_ge(s.consts, CONSTS)

            tt, V = nc.vector.tensor_tensor, nc.vector
            STEPS = {"L0": 7, "L1": 7, "L2": 13, "L3": 5}[kind]

            def routing(b):
                CH = {"L0": 14, "L1": 13, "L2": 28, "L3": 11}[kind]
                links = [0]

                def link(ins):
                    links[0] += 1
                    ins.then_inc(s.chain, 1)
                    dve.wait_ge(s.chain, b * CH + links[0])

                wide = lambda a: a.unsqueeze(2).to_broadcast([128, SUB, E])

                def rank_of(value, n, out, last=False):
                    groups = value.shape[1]
                    v_e = value.unsqueeze(3).to_broadcast([128, groups, n, n])
                    v_f = value.unsqueeze(2).to_broadcast([128, groups, n, n])
                    c = cmp[:].rearrange("p a b c -> p (a b c)")[:, 0:groups * n * n].rearrange(
                        "p (a b c) -> p a b c", a=groups, b=n)
                    u = tie[:].rearrange("p a b c -> p (a b c)")[:, 0:groups * n * n].rearrange(
                        "p (a b c) -> p a b c", a=groups, b=n)
                    tt(c, v_f, v_e, ALU.is_gt)
                    link(tt(u, v_f, v_e, ALU.is_equal))
                    yield
                    link(tt(u, u, later[:, 0:n, 0:n].unsqueeze(1).to_broadcast([128, groups, n, n]), ALU.mult))
                    link(tt(c, c, u, ALU.add))
                    yield
                    link(V.tensor_reduce(out, c, AX.X, ALU.add))
                    yield

                dve.wait_ge(s.logits, b + 1)
                product = route_ps[:, 0:SUB * E].rearrange("p (q e) -> p q e", q=SUB)
                if w.get("br") is not None and kind != "L2":
                    add = tt(lg[:], product, br[:].unsqueeze(1).to_broadcast([128, SUB, E]), ALU.add)
                else:
                    add = V.tensor_copy(lg[:], product)
                if kind in ("L0", "L1"):
                    link(add)
                    link(V.tensor_reduce(small[:, 0, :], lg[:], AX.X, ALU.max))
                    tt(lg[:], lg[:], wide(small[:, 0, :]), ALU.subtract).then_inc(s.route, 1)
                    yield
                    dve.wait_ge(s.route, b + 1)
                    yield from rank_of(lg[:], E, rank[:])
                    link(V.tensor_scalar(rw[:], rank[:], 2.0, None, ALU.is_lt))
                    yield
                    dve.wait_ge(s.expd, b + 1)
                    if kind == "L0":
                        link(tt(rw[:], rw[:], rt[:], ALU.mult))
                        link(V.tensor_reduce(small[:, 1, :], rw[:], AX.X, ALU.add))
                        link(V.reciprocal(small[:, 2, :], small[:, 1, :]))
                    else:
                        V.tensor_reduce(small[:, 1, :], rt[:], AX.X, ALU.add)
                        link(tt(rw[:], rw[:], rt[:], ALU.mult))
                        link(V.reciprocal(small[:, 2, :], small[:, 1, :]))
                    link(tt(rw[:], rw[:], wide(small[:, 2, :]), ALU.mult))
                elif kind == "L3":
                    add.then_inc(s.route, 1)
                    yield
                    dve.wait_ge(s.expd, b + 1)
                    dve.nop(nofuse=True)
                    for q in range(SUB):
                        last = V.max(top8[:, q, :], rt[:, q, :])
                    link(last)
                    yield
                    dve.nop(nofuse=True)
                    for q in range(SUB):
                        last = V.match_replace(rw[:, q, :], top8[:, q, :], rt[:, q, :], -1.0)
                    link(last)
                    yield
                    link(V.tensor_scalar(rw[:], rw[:], 0.0, None, ALU.is_lt))
                    link(tt(rw[:], rw[:], rt[:], ALU.mult))
                    link(V.tensor_reduce(small[:, 0, :], top8[:], AX.X, ALU.add))
                    link(V.tensor_scalar(small[:, 1, :], small[:, 0, :], 1e-9, None, ALU.add))
                    link(V.reciprocal(small[:, 2, :], small[:, 1, :]))
                    link(tt(rw[:], rw[:], wide(small[:, 2, :]), ALU.mult))
                else:
                    add.then_inc(s.route, 1)
                    yield
                    dve.wait_ge(s.expd, b + 1)
                    link(tt(lg[:], rt[:], br[:].unsqueeze(1).to_broadcast([128, SUB, E]), ALU.add))
                    grouped = lg[:].rearrange("p q (g e) -> p (q g) e", g=4)
                    rank4 = rank[:].rearrange("p q (g e) -> p (q g) e", g=4)
                    yield from rank_of(grouped, 4, rank4)
                    link(V.tensor_scalar(masked[:], rank[:], 2.0, None, ALU.is_lt))
                    link(tt(masked[:], masked[:], lg[:], ALU.mult))
                    link(V.tensor_reduce(gsc[:].rearrange("p q g -> p (q g)"),
                                         masked[:].rearrange("p q (g e) -> p (q g) e", g=4), AX.X, ALU.add))
                    yield from rank_of(gsc[:], 4, grank[:])
                    link(V.tensor_scalar(grank[:], grank[:], 2.0, None, ALU.is_lt))
                    link(tt(masked[:].rearrange("p q (g e) -> p (q g) e", g=4), grouped,
                            grank[:].rearrange("p q g -> p (q g)").unsqueeze(2).to_broadcast([128, 4 * SUB, 4]),
                            ALU.mult))
                    yield from rank_of(masked[:], E, rank[:])
                    link(V.tensor_scalar(rw[:], rank[:], 4.0, None, ALU.is_lt))
                    yield
                    link(tt(rw[:], rw[:], rt[:], ALU.mult))
                    link(V.tensor_reduce(small[:, 0, :], rw[:], AX.X, ALU.add))
                    link(V.tensor_scalar(small[:, 1, :], small[:, 0, :], 1e-20, None, ALU.add))
                    link(V.reciprocal(small[:, 2, :], small[:, 1, :]))
                    link(tt(rw[:], rw[:], wide(small[:, 2, :]), ALU.mult))
                    link(V.tensor_scalar(rw[:], rw[:], 2.5, None, ALU.mult))
                yield
                link(V.tensor_copy(parts[:, :, 0, 0:E], rw[:]))
                link(tt(rest[:], rw[:], parts[:, :, 0, 0:E], ALU.subtract))
                link(V.tensor_copy(parts[:, :, 1, 0:E], rest[:]))
                tt(parts[:, :, 2, 0:E], rest[:], parts[:, :, 1, 0:E], ALU.subtract).then_inc(s.weights, 1)
                assert links[0] == CH, (kind, links[0])

            def experts(b, last_block):
                steps = iter(()) if last_block else routing(b + 1)
                for n, t in enumerate(tiles):
                    rows = shared if t < 0 else 128
                    if n >= 2:
                        for _ in range(1 if NT - 3 >= STEPS else -(-STEPS // (NT - 3))):
                            next(steps, None)
                    dve.wait_ge(s.gated_ready, b * NT + n + 3)
                    if glu:
                        dve.wait_ge(s.up, b * NT + n + 1)
                    bias = 0.0
                    if t < 0 and shared_bias:
                        bias = bsb[0:rows, :]
                    elif t >= 0 and has_bias and glu:
                        bias = bb[:, t:t + 1]
                    if t < 0:
                        V.scalar_tensor_tensor(out=hid[0:rows, n % 2, :], in0=up_ps[0:rows, n % 2, :], scalar=bias,
                                               in1=gated[0:rows, n % 2, :], op0=ALU.add,
                                               op1=ALU.mult).then_inc(s.hid1_ready, 1)
                        dve.wait_ge(s.hid1_ready, b * NT + n + 3)
                        dve.sem_inc(s.hid_ready, 1)
                        continue
                    if glu:
                        V.scalar_tensor_tensor(out=hid1[:, n % 2, :], in0=up_ps[:, n % 2, :], scalar=bias,
                                               in1=gated[:, n % 2, :], op0=ALU.add,
                                               op1=ALU.mult).then_inc(s.hid1_ready, 1)
                        dve.wait_ge(s.hid1_ready, b * NT + n + 3)
                    routed = n - (1 if shared else 0)
                    dve.wait_ge(s.wps, b * n_routed + routed + 1)
                    if glu:
                        V.tensor_tensor(hid[:, n % 2, :], hid1[:, n % 2, :], weight_ps[:, n % 2, :],
                                        ALU.mult).then_inc(s.hid_ready, 1)
                    else:
                        V.tensor_tensor(hid[:, n % 2, :], gated[:, n % 2, :], weight_ps[:, n % 2, :],
                                        ALU.mult).then_inc(s.hid_ready, 1)
                        dve.wait_ge(s.hid_ready, b * NT + n + 3)
                        dve.sem_inc(s.hid1_ready, 1)
                for _ in steps:
                    pass
                dve.wait_ge(s.out, b + 1)
                tok = bass.ds(b * TB, TB)
                if shared and w.get("bias_sd") is not None:
                    V.scalar_tensor_tensor(out=x[:, tok], in0=out_ps[:], scalar=bsd[:], in1=x[:, tok],
                                           op0=ALU.add, op1=ALU.add).then_inc(s.out_read, 1)
                else:
                    V.tensor_tensor(x[:, tok], x[:, tok], out_ps[:], ALU.add).then_inc(s.out_read, 1)

            for _ in routing(0):
                pass
            with dve.Fori(0, NTB - 1) as b:
                experts(b, last_block=False)
            experts(NTB - 1, last_block=True)
    release(nc, s)


HEADS, DH = 16, 8
PARTS = 3
STACK = PARTS * PARTS * DH
MAXROW = 96
NEG = -1.0e30


def attention_inputs(nc, name, h, scratch, v_all, w):
    inter, bias = w["interleaved"], w.get("bq") is not None
    with ExitStack() as ctx:
        def sb(n, shape, dt=F32):
            return ctx.enter_context(nc.sbuf_tensor(f"{name}_{n}", shape, dt))

        qk_ps = ctx.enter_context(nc.psum_tensor(f"{name}_qk_ps", [128, 2, TB], F32))
        v_ps = ctx.enter_context(nc.psum_tensor(f"{name}_v_ps", [128, TB], F32))
        wqk = sb("wqk", [128, 2, 128])
        wv = sb("wv", [128, 128])
        bqk = sb("bqk", [128, 2])
        bv = sb("bv", [128, 128])
        hb = sb("hb", [128, TB])
        full = sb("full", [128, 2, TB])
        rest = sb("rest", [128, 2, TB])
        part = [sb(f"part{n}", [128, 2, 2, TB], BF16) for n in range(PARTS)]
        s = semaphores(nc, name, "loads ones copied qk v full_ready part1 rest_ready part2 part3 "
                                 "v_read written0 written1")
        written = (s.written0, s.written1)
        loads = [(wqk[:, 0, :], w["wq"]), (wqk[:, 1, :], w["wk"]), (wv[:], w["wv"])]
        if bias:
            loads += [(bqk[:, 0:1], column(w["bq"])), (bqk[:, 1:2], column(w["bk"]))]
            if inter:
                loads += [(bv[64 * r:64 * r + 64, 0:64], w["bv"][r].partition_broadcast(64)) for r in range(2)]
            else:
                loads.append((bv[:], w["bv"].partition_broadcast(128)))
        OUT = 16 * 2 * PARTS
        block = ctx.enter_context(nc.Block())

        @block.sync
        def _(sp):
            for sem in written:
                sp.sem_inc(sem, 1)
            with nc.allow_non_contiguous_dma("biases, one value per partition"):
                for to, source in loads:
                    sp.dma_start(to, source).then_inc(s.loads, 16)
            with sp.Fori(0, BATCH) as b:
                for j in range(2):
                    for n, ready in enumerate((s.part1, s.part2, s.part3)):
                        sp.wait_ge(ready, b * 2 + j + 2)
                        for z in range(2):
                            if inter:
                                to = scratch[z, n, bass.ds(b * HEADS + j * 8, 8)].rearrange(
                                    "e d (u t) -> (d u) e t", u=16)
                                source = part[n][:, j, z, :].rearrange("p (e t) -> p e t", e=8)
                            else:
                                to = scratch[z, n, bass.ds(b * HEADS, HEADS)].rearrange(
                                    "e d p -> (e d) p")[:, j * TB:(j + 1) * TB]
                                source = part[n][:, j, z, :]
                            sp.dma_start(to, source).then_inc(written[j], 16)
            for sem in written:
                sp.wait_ge(sem, OUT * BATCH + 1)

        @block.gpsimd
        def _(pool):
            pool.memset(v_all[:, :, :, DH:DH + 1], 1.0).then_inc(s.ones, 1)
            pool.sem_inc(s.rest_ready, 1)
            with pool.Fori(0, BATCH) as b:
                for j in range(2):
                    k = b * 2 + j
                    pool.wait_ge(s.part1, k + 2)
                    pool.wait_ge(s.part3, k + 1)
                    nc.gpsimd.tensor_tensor(rest[:], full[:], part[0][:, j], ALU.subtract).then_inc(s.rest_ready, 1)

        @block.tensor
        def _(pe):
            pe.wait_ge(s.loads, 16 * len(loads))
            with pe.Fori(0, BATCH) as b:
                for j in range(2):
                    k = b * 2 + j
                    pe.wait_ge(s.copied, k + 2)
                    pe.wait_ge(s.full_ready, k + 1)
                    for z in range(2):
                        mm = nc.tensor.matmul(qk_ps[:, z, :], wqk[:, z, :], hb[:], start=True, stop=True)
                    mm.then_inc(s.qk, 1)
                    pe.wait_ge(s.v_read, k + 1)
                    if inter:
                        for e in range(8):
                            for r in range(2):
                                mm = nc.tensor.matmul(v_ps[64 * r:64 * r + 64, e * 64:(e + 1) * 64],
                                                      hb[:, e * 64:(e + 1) * 64], wv[:, r * 64:(r + 1) * 64],
                                                      start=True, stop=True)
                    else:
                        for q in range(4):
                            mm = nc.tensor.matmul(v_ps[:, q * 128:(q + 1) * 128], hb[:, q * 128:(q + 1) * 128],
                                                  wv[:], start=True, stop=True)
                    mm.then_inc(s.v, 1)

        @block.scalar
        def _(act):
            for sem in (s.copied, s.full_ready, s.part1):
                act.sem_inc(sem, 1)
            act.wait_ge(s.loads, 16 * len(loads))
            with act.Fori(0, BATCH) as b:
                for j in range(2):
                    k = b * 2 + j
                    act.wait_ge(s.v_read, k + 1)
                    nc.scalar.activation(hb[:], h[:, bass.ds(b * SEQ + j * TB, TB)], ACT.Copy).then_inc(s.copied, 1)
                    act.wait_ge(s.qk, k + 1)
                    act.wait_ge(s.rest_ready, k + 1)
                    act.wait_ge(s.part1, k + 1)
                    for z in range(2):
                        a = nc.scalar.activation(full[:, z, :], qk_ps[:, z, :], ACT.Identity,
                                                 bias=bqk[:, z:z + 1] if bias else 0.0)
                    a.then_inc(s.full_ready, 1)
                    act.wait_ge(s.full_ready, k + 2)
                    act.wait_ge(written[j], b * OUT + 1)
                    nc.scalar.activation(part[0][:, j], full[:], ACT.Copy).then_inc(s.part1, 1)

        @block.vector
        def _(dve):
            for sem in (s.v_read, s.part2, s.part3):
                dve.sem_inc(sem, 1)
            dve.wait_ge(s.loads, 16 * len(loads))
            dve.wait_ge(s.ones, 1)
            with dve.Fori(0, BATCH) as b:
                for j in range(2):
                    k = b * 2 + j
                    dve.wait_ge(s.v, k + 1)
                    if inter:
                        to = v_all[:, bass.ds(b * HEADS + j * 8, 8), :, 0:DH]
                        source = v_ps[:].rearrange("p (e k d) -> p e k d", e=8, k=8)
                        more = bv[:, 0:64].rearrange("p (k d) -> p k d", k=8).unsqueeze(1).to_broadcast([128, 8, 8, DH])
                        v = nc.vector.tensor_tensor(to, source, more, ALU.add)
                    else:
                        for q in range(4):
                            to = v_all[:, bass.ds(b * HEADS, HEADS), j * 4 + q, 0:DH]
                            source = v_ps[:, q * 128:(q + 1) * 128].rearrange("p (h d) -> p h d", d=DH)
                            if bias:
                                v = nc.vector.tensor_tensor(to, source, bv[:].rearrange("p (h d) -> p h d", d=DH),
                                                            ALU.add)
                            else:
                                v = nc.vector.tensor_copy(to, source)
                    v.then_inc(s.v_read, 1)
                    dve.wait_ge(s.rest_ready, k + 2)
                    dve.wait_ge(written[j], b * OUT + 1)
                    nc.vector.tensor_copy(part[1][:, j], rest[:]).then_inc(s.part2, 1)
                    dve.wait_ge(s.part2, k + 2)
                    nc.vector.tensor_tensor(part[2][:, j], rest[:], part[1][:, j], ALU.subtract).then_inc(s.part3, 1)
    release(nc, s)


def attention(nc, name, scratch, v_all, target, w):
    causal, inter = w["causal"], w["interleaved"]
    GROUPS = BATCH * HEADS // 4
    SCALE = float(DH) ** -0.5
    with ExitStack() as ctx:
        def sb(n, shape, dt=F32):
            return ctx.enter_context(nc.sbuf_tensor(f"{name}_{n}", shape, dt))

        def ps(n, shape):
            return ctx.enter_context(nc.psum_tensor(f"{name}_{n}", shape, F32))

        s_ps = ps("s_ps", [128, 2, 2, TB])
        max_ps = ps("max_ps", [128, 2, TB])
        o_ps = ps("o_ps", [128, TB])
        y_ps = ps("y_ps", [128, TB])
        qs = sb("qs", [128, 2, 4, SEQ], BF16)
        ks = sb("ks", [128, 2, 4, SEQ], BF16)
        vg = sb("vg", [128, 2, 4, 8, DH + 1])
        prob = sb("prob", [128, 2, 2, TB])
        halves = sb("halves", [128, 2, 16, 2])
        nmax = sb("nmax", [128, 16])
        nrest = sb("nrest", [128, 16])
        nrest2 = sb("nrest2", [128, 16])
        nparts = sb("nparts", [128, 16, PARTS], BF16)
        wo = sb("wo", [128, 4, 128])
        bo = sb("bo", [128, 1])
        total = sb("total", [128, 4])
        ident = sb("ident", [128, 128])
        ident_bf = sb("ident_bf", [128, 128], BF16)
        zero_bf = sb("zero_bf", [128, TB], BF16)
        o_sb = sb("o_sb", [128, TB])
        inv = sb("inv", [128, 16])
        inv_rows = sb("inv_rows", [128, TB])
        on = sb("on", [128, TB])
        mask_k = sb("mask_k", [128, 896], BF16) if causal else None
        mask_q = sb("mask_q", [128, 896], BF16) if causal else None
        s = semaphores(nc, name, "loads consts ones stacks0 stacks1 stack_used mx mx_read chain rows_ps rows vg_ready "
                                 "sc prob_ready pv o_copied sums spread inv_ready inv_rows_ready on_ready y y_read zeroed")
        stacks = (s.stacks0, s.stacks1)
        bias = w.get("bo") is not None
        LOADS = 16 * (16 + bias)
        STACKS = 16 * 4 * 6

        def units(half):
            return [(j, p) for p in range(4) for j in range(4) if not (causal and half == 0 and p >= 2)]

        def maxima(half):
            return [(j, half * 4 + q, kh) for j in range(4) for q in range(4) for kh in range(2)
                    if not (causal and kh == 1 and half == 0)]

        def shared(half, n):
            nm = len(maxima(1 - half))
            return min(nm, -(-nm * (n + 1) // (len(units(half)) - 2)))

        SUMS_AT, SPREAD_AT, PROJECT_AT = 1, 3, 5
        NU = len(units(0)) + len(units(1))
        NM = len(maxima(0)) + len(maxima(1))
        block = ctx.enter_context(nc.Block())

        @block.sync
        def _(sp):
            with nc.allow_non_contiguous_dma("rows of heads of 8"):
                for g in range(4):
                    for j in range(4):
                        r = (4 * g + j) * DH
                        if g == 0 and j == 0:
                            sp.wait_ge(s.zeroed, 3)
                        sp.dma_start(wo[32 * j:32 * j + DH, g, :], w["wo"][r:r + DH, :]).then_inc(s.loads, 16)
                if bias:
                    sp.dma_start(bo[:], column(w["bo"])).then_inc(s.loads, 16)
            sp.sem_inc(s.stack_used, 2)
            with sp.Fori(0, GROUPS // 2) as i:
                for z in range(2):
                    sp.wait_ge(s.stack_used, i * 2 + z + 1)
                    for j in range(4):
                        head = bass.ds(i * 8 + z * 4 + j, 1)
                        for n in range(PARTS):
                            r = n * PARTS * DH
                            sp.dma_start(qs[r:r + 24, z, j, :],
                                         scratch[0, n:n + 1, head].rearrange("n e d p -> (n e) d p").to_broadcast(
                                             [PARTS, DH, SEQ])).then_inc(stacks[z], 16)
                            sp.dma_start(ks[r:r + 24, z, j, :],
                                         scratch[1, :, head].rearrange("n e d p -> (n e) d p")).then_inc(stacks[z], 16)

        @block.gpsimd
        def _(pool):
            pool.memset(wo[:], 0.0).then_inc(s.zeroed, 1)
            pool.memset(qs[:], 0.0).then_inc(s.zeroed, 1)
            pool.memset(ks[:], 0.0).then_inc(s.zeroed, 1)
            pool.memset(total[:], 0.0).then_inc(s.consts, 1)
            pool.memset(zero_bf[:], 0.0).then_inc(s.consts, 1)
            pool.memset(ident_bf[:], 0.0).then_inc(s.consts, 1)
            pool.memset(ident[:], 0.0).then_inc(s.consts, 1)
            n = 4
            if causal:
                pool.memset(mask_k[:], 0.0).then_inc(s.consts, 1)
                pool.memset(mask_q[:], 0.0).then_inc(s.consts, 1)
                n = 6
            pool.wait_ge(s.consts, n)
            pool.affine_select(out=total[:], in_=total[:], compare_op=ALU.not_equal, fill=1.0, base=-DH,
                               pattern=[[-32, 4]], channel_multiplier=1).then_inc(s.consts, 1)
            pool.affine_select(out=ident[:], in_=ident[:], compare_op=ALU.not_equal, fill=1.0, base=0,
                               pattern=[[-1, 128]], channel_multiplier=1).then_inc(s.consts, 1)
            pool.affine_select(out=ident_bf[:], in_=ident_bf[:], compare_op=ALU.not_equal, fill=1.0, base=0,
                               pattern=[[-1, 128]], channel_multiplier=1).then_inc(s.consts, 1)
            if causal:
                pool.affine_select(out=mask_k[:], in_=mask_k[:], compare_op=ALU.is_ge, fill=NEG, base=-384,
                                   pattern=[[1, 896]], channel_multiplier=-1).then_inc(s.consts, 1)
                pool.affine_select(out=mask_q[:], in_=mask_q[:], compare_op=ALU.is_ge, fill=NEG, base=384,
                                   pattern=[[-1, 896]], channel_multiplier=1).then_inc(s.consts, 1)
            pool.sem_inc(s.vg_ready, 2)

            def stage_values(i, z):
                pool.wait_ge(s.stack_used, i * 2 + z + 1)
                nc.gpsimd.tensor_copy(vg[:, z], v_all[:, bass.ds(i * 8 + z * 4, 4)]).then_inc(s.vg_ready, 1)

            def expand(i, z):
                for half in range(2):
                    it = (i * 2 + z) * 2 + half
                    pool.wait_ge(s.inv_ready, it + 1)
                    pool.nop(nofuse=True)
                    nc.gpsimd.tensor_copy(inv_rows[:].rearrange("p (c r) -> p c r", r=32),
                                          inv[:].unsqueeze(2).to_broadcast([128, 16, 32])).then_inc(
                                              s.inv_rows_ready, 1)

            stage_values(0, 0)
            with pool.Fori(0, GROUPS // 2 - 1) as i:
                stage_values(i, 1)
                expand(i, 0)
                stage_values(i + 1, 0)
                expand(i, 1)
            stage_values(GROUPS // 2 - 1, 1)
            for z in range(2):
                expand(GROUPS // 2 - 1, z)

        CONSTS = 11 if causal else 7

        @block.tensor
        def _(pe):
            pe.wait_ge(s.consts, CONSTS)
            pe.wait_ge(s.ones, 1)
            pe.wait_ge(s.loads, LOADS)
            nc.tensor.matmul(o_ps[:], zero_bf[:, 0:128], zero_bf[:], start=True, stop=True).then_inc(s.pv, 1)
            pe.sem_inc(s.pv, 1)

            def maximum(G, z, half, n):
                j, q, kh = maxima(half)[n]
                k = n + (len(maxima(0)) if half else 0)
                pe.wait_ge(s.mx_read, G * NM + k + 1)
                out = max_ps[:, n % 2, :]
                diagonal = causal and kh == q // 4
                if diagonal:
                    off = (q % 4) * 128
                    nc.tensor.matmul(out, ident_bf[:], mask_q[:, 384 - off:896 - off], start=True, stop=False)
                nc.tensor.matmul(out, qs[0:STACK, z, j, q * 128:(q + 1) * 128],
                                 ks[0:STACK, z, j, kh * TB:(kh + 1) * TB],
                                 start=not diagonal, stop=True).then_inc(s.mx, 1)

            def turn(G, half, j2):
                if j2 == 0:
                    pe.wait_ge(s.chain, (G * 2 + half) * 5 + 5)
                pe.wait_ge(s.rows, (G * 2 + half) * 2 + j2 + 1)
                for jj in range(2):
                    for q in range(4):
                        mm = nc.tensor.matmul(max_ps[MAXROW:MAXROW + PARTS, jj, q * 128:(q + 1) * 128],
                                              nparts[:, (j2 * 2 + jj) * 4 + q, :], ident_bf[:],
                                              start=True, stop=True)
                mm.then_inc(s.rows_ps, 1)

            def scores(G, z, half, n, e):
                j, p = units(half)[n]
                k = n + (len(units(0)) if half else 0)
                if e == 0:
                    pe.wait_ge(s.prob_ready, G * NU + k + 1)
                kt = 2 * p + e
                diagonal = causal and kt // 4 == half
                if diagonal:
                    off = (kt % 4) * 128
                    nc.tensor.matmul(s_ps[:, n % 2, e, :], ident_bf[:], mask_k[:, 384 - off:896 - off],
                                     start=True, stop=False)
                mm = nc.tensor.matmul(s_ps[:, n % 2, e, :], ks[0:MAXROW + PARTS, z, j, kt * 128:(kt + 1) * 128],
                                      qs[0:MAXROW + PARTS, z, j, half * TB:(half + 1) * TB],
                                      start=not diagonal, stop=True)
                if e == 1:
                    mm.then_inc(s.sc, 1)

            def values(G, z, half, n, e):
                j, p = units(half)[n]
                k = n + (len(units(0)) if half else 0)
                if e == 0:
                    pe.wait_ge(s.prob_ready, G * NU + k + 3)
                if n == 0:
                    pe.wait_ge(s.o_copied, G * 2 + half + 1)
                last_pair = max(pp for jj, pp in units(half) if jj == j)
                mm = nc.tensor.matmul(o_ps[32 * j:32 * j + DH + 1, :], vg[:, z, j, 2 * p + e, :],
                                      prob[:, n % 2, e, :], start=(p == 0 and e == 0),
                                      stop=(p == last_pair and e == 1), skip_group_check=True)
                if e == 1:
                    mm.then_inc(s.pv, 1)

            def sums(it):
                pe.wait_ge(s.o_copied, it + 2)
                pe.wait_ge(s.y_read, it + 1)
                for q in range(4):
                    mm = nc.tensor.matmul(y_ps[:, 4 * q:4 * q + 4], o_sb[:, q * 128:(q + 1) * 128], total[:],
                                          start=True, stop=True)
                mm.then_inc(s.sums, 1)

            def spread(it):
                pe.wait_ge(s.inv_rows_ready, it + 1)
                for q in range(4):
                    mm = nc.tensor.matmul(y_ps[:, q * 128:(q + 1) * 128],
                                          inv_rows[:, q * 128:(q + 1) * 128],
                                          ident[:], start=True, stop=True)
                mm.then_inc(s.spread, 1)

            def project(it, g):
                pe.wait_ge(s.on_ready, it + 2)
                nc.tensor.matmul(y_ps[:], wo[:, g, :], on[:], start=True, stop=True).then_inc(s.y, 1)

            def operands(b, g):
                pe.wait_ge(stacks[g % 2], (b * 2 + g // 2 + 1) * STACKS)
                pe.wait_ge(s.vg_ready, b * 4 + g + 3)

            def half_step(b, g, half, first, last):
                G, z = b * 4 + g, g % 2
                it = G * 2 + half
                nu = len(units(half))
                next_half, next_z, next_G = 1 - half, (z + half) % 2, G + half
                done = 0
                pe.wait_ge(s.rows, it * 2 + 2)
                for n in range(nu):
                    todo = 0 if last else shared(half, n)
                    scores(G, z, half, n, 0)
                    if n == 0:
                        pe.wait_ge(s.rows, it * 2 + 3)
                        if not last and half == 1:
                            operands(b, g + 1)
                    if done < todo:
                        maximum(next_G, next_z, next_half, done)
                        done += 1
                    scores(G, z, half, n, 1)
                    for e in range(2):
                        if done < todo:
                            maximum(next_G, next_z, next_half, done)
                            done += 1
                        if n >= 1:
                            values(G, z, half, n - 1, e)
                    while done < todo:
                        maximum(next_G, next_z, next_half, done)
                        done += 1
                    if n == SUMS_AT and not first:
                        sums(it - 1)
                    if n == SPREAD_AT and not first:
                        spread(it - 1)
                    if n == PROJECT_AT and not first:
                        project(it - 1, g if half else (g + 3) % 4)
                    if n >= nu - 2 and not last:
                        turn(next_G, next_half, n - (nu - 2))
                for e in range(2):
                    values(G, z, half, nu - 1, e)

            operands(0, 0)
            for n in range(len(maxima(0))):
                maximum(0, 0, 0, n)
            for j2 in range(2):
                turn(0, 0, j2)
            for g in range(4):
                for half in range(2):
                    half_step(0, g, half, first=g + half == 0, last=False)
            with pe.Fori(1, BATCH - 1) as b:
                for g in range(4):
                    for half in range(2):
                        half_step(b, g, half, first=False, last=False)
            for g in range(4):
                for half in range(2):
                    half_step(BATCH - 1, g, half, first=False, last=g == 3 and half == 1)
            sums(GROUPS * 2 - 1)
            spread(GROUPS * 2 - 1)
            project(GROUPS * 2 - 1, 3)

        @block.scalar
        def _(act):
            act.sem_inc(s.rows, 1)
            act.sem_inc(s.prob_ready, 2)
            act.sem_inc(s.o_copied, 1)
            act.wait_ge(s.consts, CONSTS)
            def rows(G, z, half, j2):
                act.wait_ge(s.rows_ps, (G * 2 + half) * 2 + j2 + 1)
                nc.scalar.activation(qs[MAXROW:MAXROW + PARTS, z, 2 * j2:2 * j2 + 2, half * TB:(half + 1) * TB],
                                     max_ps[MAXROW:MAXROW + PARTS, :, :], ACT.Copy).then_inc(s.rows, 1)

            def half_step(G, z, half, last):
                nu = len(units(half))
                base = G * NU + (len(units(0)) if half else 0)
                for n in range(nu):
                    act.wait_ge(s.sc, base + n + 1)
                    act.wait_ge(s.pv, base + n + 1)
                    nc.scalar.activation(prob[:, n % 2], s_ps[:, n % 2], ACT.Exp,
                                         scale=SCALE).then_inc(s.prob_ready, 1)
                    if n >= nu - 2 and not last:
                        rows(G + half, (z + half) % 2, 1 - half, n - (nu - 2))
                act.wait_ge(s.pv, base + nu + 2)
                if half == 1:
                    act.sem_inc(s.stack_used, 1)
                act.wait_ge(s.on_ready, G * 2 + half + 1)
                nc.scalar.activation(o_sb[:], o_ps[:], ACT.Copy).then_inc(s.o_copied, 1)

            for j2 in range(2):
                rows(0, 0, 0, j2)
            with act.Fori(0, GROUPS // 2 - 1) as i:
                for z in range(2):
                    for half in range(2):
                        half_step(i * 2 + z, z, half, last=False)
            for z in range(2):
                for half in range(2):
                    half_step(GROUPS - 2 + z, z, half, last=z == 1 and half == 1)

        @block.vector
        def _(dve):
            dve.sem_inc(s.mx_read, 2)
            dve.sem_inc(s.on_ready, 1)
            dve.sem_inc(s.y_read, 1)
            dve.wait_ge(s.loads, LOADS)
            V = nc.vector
            dve.wait_ge(s.zeroed, 3)
            V.memset(ks[MAXROW:MAXROW + PARTS], 1.0).then_inc(s.ones, 1)
            def maximum(G, half, n):
                j, q, kh = maxima(half)[n]
                k = G * NM + n + (len(maxima(0)) if half else 0)
                dve.wait_ge(s.mx, k + 1)
                V.reduce_max(halves[:, 0, j * 4 + q % 4, kh:kh + 1], max_ps[:, n % 2, :],
                             AX.X).then_inc(s.mx_read, 1)

            def split_maxima(G, half):
                it = G * 2 + half
                dve.wait_ge(s.mx_read, (G + half) * NM + (0 if half else len(maxima(0))) + 2)
                hs = halves[:, 0, :, 0:1 if causal and half == 0 else 2]
                V.tensor_reduce(nmax[:], hs, AX.X, ALU.max, negate=True).then_inc(s.chain, 1)
                dve.wait_ge(s.chain, it * 5 + 1)
                V.tensor_copy(nparts[:, :, 0], nmax[:]).then_inc(s.chain, 1)
                dve.wait_ge(s.chain, it * 5 + 2)
                V.tensor_tensor(nrest[:], nmax[:], nparts[:, :, 0], ALU.subtract).then_inc(s.chain, 1)
                dve.wait_ge(s.chain, it * 5 + 3)
                V.tensor_copy(nparts[:, :, 1], nrest[:]).then_inc(s.chain, 1)
                dve.wait_ge(s.chain, it * 5 + 4)
                V.tensor_tensor(nparts[:, :, 2], nrest[:], nparts[:, :, 1], ALU.subtract).then_inc(s.chain, 1)

            def invert(it):
                dve.wait_ge(s.sums, it + 1)
                V.reciprocal(inv[:], y_ps[:, 0:16]).then_inc(s.inv_ready, 1)

            def weigh(it):
                dve.wait_ge(s.spread, it + 1)
                V.tensor_tensor(on[:], o_sb[:], y_ps[:], ALU.mult).then_inc(s.on_ready, 1)

            def add_output(b, g, half):
                it = (b * 4 + g) * 2 + half
                dve.wait_ge(s.y, it + 1)
                if inter:
                    to = target[:, bass.ds(b * SEQ, SEQ)].rearrange("p (t u) -> p u t", u=16)[
                        :, 8 * half:8 * half + 8, :]
                    source = y_ps[:].rearrange("p (u t) -> p u t", u=8)
                else:
                    to = target[:, bass.ds(b * SEQ + half * TB, TB)]
                    source = y_ps[:]
                if bias and g == 0:
                    V.scalar_tensor_tensor(out=to, in0=source, scalar=bo[:], in1=to, op0=ALU.add,
                                           op1=ALU.add).then_inc(s.y_read, 1)
                else:
                    V.tensor_tensor(to, to, source, ALU.add).then_inc(s.y_read, 1)

            def half_step(b, g, half, first, last):
                G = b * 4 + g
                it = G * 2 + half
                done = 0
                for n in range(len(units(half))):
                    while not last and done < shared(half, n):
                        maximum(G + half, 1 - half, done)
                        done += 1
                    if n == SUMS_AT and not first:
                        invert(it - 1)
                    if n == SPREAD_AT and not first:
                        weigh(it - 1)
                    if n == PROJECT_AT and not first:
                        if half:
                            add_output(b, g, 0)
                        elif g:
                            add_output(b, g - 1, 1)
                        else:
                            add_output(b - 1, 3, 1)
                if not last:
                    split_maxima(G + half, 1 - half)

            for n in range(len(maxima(0))):
                maximum(0, 0, n)
            split_maxima(0, 0)
            for g in range(4):
                for half in range(2):
                    half_step(0, g, half, first=g + half == 0, last=False)
            with dve.Fori(1, BATCH - 1) as b:
                for g in range(4):
                    for half in range(2):
                        half_step(b, g, half, first=False, last=False)
            for g in range(4):
                for half in range(2):
                    half_step(BATCH - 1, g, half, first=False, last=g == 3 and half == 1)
            invert(GROUPS * 2 - 1)
            weigh(GROUPS * 2 - 1)
            add_output(BATCH - 1, 3, 1)
    release(nc, s)


def project(nc, name, src, outs):
    n_out, nk = len(outs), len(src)
    add = outs[0].get("add", False)
    slots = 4 if n_out % 2 == 0 else 2
    with ExitStack() as ctx:
        def sb(n, shape):
            return ctx.enter_context(nc.sbuf_tensor(f"{name}_{n}", shape, F32))

        out_ps = ctx.enter_context(nc.psum_tensor(f"{name}_ps", [128, slots, TB], F32))
        weights = sb("weights", [128, n_out, nk, 128])
        bias = sb("bias", [128, n_out])
        s = semaphores(nc, name, "loads product taken")
        loads = []
        for n, o in enumerate(outs):
            o["rows"] = o["w"][0].shape[-1]
            for k in range(nk):
                kr = o["w"][k].shape[0]
                loads.append((weights[0:kr, n, k, 0:o["rows"]], o["w"][k]))
            if o.get("bias") is not None:
                loads.append((bias[0:o["rows"], n:n + 1], column(o["bias"])))
        block = ctx.enter_context(nc.Block())

        @block.sync
        def _(sp):
            with nc.allow_non_contiguous_dma("biases, one value per partition"):
                for to, source in loads:
                    sp.dma_start(to, source).then_inc(s.loads, 16)

        @block.tensor
        def _(pe):
            pe.wait_ge(s.loads, 16 * len(loads))
            with pe.Fori(0, BATCH) as b:
                for j in range(2):
                    tok = bass.ds(b * SEQ + j * TB, TB)
                    for n, o in enumerate(outs):
                        m = j * n_out + n
                        pe.wait_ge(s.taken, b * (2 * n_out) + m + 1)
                        pe.nop(nofuse=True)
                        for k in range(nk):
                            kr = o["w"][k].shape[0]
                            mm = nc.tensor.matmul(out_ps[0:o["rows"], m % slots, :],
                                                  weights[0:kr, n, k, 0:o["rows"]], src[k][0:kr, tok],
                                                  start=(k == 0), stop=(k == nk - 1))
                        mm.then_inc(s.product, 1)

        def take(engine, compute):
            engine.sem_inc(s.taken, slots)
            engine.wait_ge(s.loads, 16 * len(loads))
            with engine.Fori(0, BATCH) as b:
                for j in range(2):
                    tok = bass.ds(b * SEQ + j * TB, TB)
                    for n, o in enumerate(outs):
                        m = j * n_out + n
                        engine.wait_ge(s.product, b * (2 * n_out) + m + 1)
                        engine.nop(nofuse=True)
                        compute(n, o, o["dst"][0:o["rows"], tok], out_ps[0:o["rows"], m % slots, :]).then_inc(
                            s.taken, 1)

        if add:
            @block.vector
            def _(dve):
                def compute(n, o, dst, ps):
                    if o.get("bias") is None:
                        return nc.vector.tensor_tensor(dst, dst, ps, ALU.add)
                    return nc.vector.scalar_tensor_tensor(out=dst, in0=ps, scalar=bias[0:o["rows"], n:n + 1],
                                                          in1=dst, op0=ALU.add, op1=ALU.add)
                take(dve, compute)
        else:
            @block.scalar
            def _(act):
                def compute(n, o, dst, ps):
                    return nc.scalar.activation(
                        dst, ps, o.get("func", ACT.Identity),
                        bias=bias[0:o["rows"], n:n + 1] if o.get("bias") is not None else 0.0)
                take(act, compute)
    release(nc, s)


def causal_conv(nc, name, tiles, weight, shift):
    nt, taps = len(tiles), 4
    with ExitStack() as ctx:
        def sb(n, shape):
            return ctx.enter_context(nc.sbuf_tensor(f"{name}_{n}", shape, F32))

        wt = sb("wt", [128, nt, taps])
        bt = sb("bt", [128, nt])
        acc = sb("acc", [128, 2, SEQ])
        s = semaphores(nc, name, "loads first chain summed done")
        block = ctx.enter_context(nc.Block())

        @block.sync
        def _(sp):
            with nc.allow_non_contiguous_dma("taps, one row per partition"):
                sp.dma_start(wt[:], weight.rearrange("(t p) k -> p t k", p=128)).then_inc(s.loads, 16)
                sp.dma_start(bt[:], shift.rearrange("(t p) -> p t", p=128)).then_inc(s.loads, 16)

        @block.scalar
        def _(act):
            act.wait_ge(s.loads, 32)
            with act.Fori(0, BATCH) as b:
                tok = bass.ds(b * SEQ, SEQ)
                for t in range(nt):
                    nc.scalar.activation(acc[:, t % 2], tiles[t][:, tok], ACT.Identity, bias=bt[:, t:t + 1],
                                         scale=wt[:, t, taps - 1:taps]).then_inc(s.first, 1)
                for t in range(nt):
                    act.wait_ge(s.summed, b * nt + t + 1)
                    act.nop(nofuse=True)
                    nc.scalar.activation(tiles[t][:, tok], acc[:, t % 2], ACT.Silu).then_inc(s.done, 1)
                    act.wait_ge(s.done, b * nt + t + 1)

        @block.vector
        def _(dve):
            dve.wait_ge(s.loads, 32)
            with dve.Fori(0, BATCH) as b:
                for t in range(nt):
                    dve.wait_ge(s.first, b * nt + t + 1)
                    for k in range(1, taps):
                        v = nc.vector.scalar_tensor_tensor(
                            out=acc[:, t % 2, k:SEQ], in0=tiles[t][:, bass.ds(b * SEQ, SEQ - k)],
                            scalar=wt[:, t, taps - 1 - k:taps - k], in1=acc[:, t % 2, k:SEQ],
                            op0=ALU.mult, op1=ALU.add)
                        if k < taps - 1:
                            v.then_inc(s.chain, 1)
                            dve.wait_ge(s.chain, b * (nt * 2) + t * 2 + k)
                    v.then_inc(s.summed, 1)
    release(nc, s)


def pointwise(nc, name, steps):
    s = semaphores(nc, name, "loads step")
    with ExitStack() as ctx:
        scalars, loads = {}, []
        for n, st in enumerate(steps):
            if len(st) == 6 and not isinstance(st[2], float):
                scalars[n] = ctx.enter_context(nc.sbuf_tensor(f"{name}_s{n}", [128, 1], F32))
                loads.append((scalars[n][:], column(st[2])))
        block = ctx.enter_context(nc.Block())

        @block.sync
        def _(sp):
            with nc.allow_non_contiguous_dma("one value per partition"):
                for to, source in loads:
                    sp.dma_start(to, source).then_inc(s.loads, 16)

        @block.vector
        def _(dve):
            if loads:
                dve.wait_ge(s.loads, 16 * len(loads))
            with dve.Fori(0, BATCH) as b:
                tok = bass.ds(b * SEQ, SEQ)
                for n, st in enumerate(steps):
                    if len(st) == 4:
                        v = nc.vector.tensor_tensor(st[0][:, tok], st[1][:, tok], st[2][:, tok], st[3])
                    else:
                        v = nc.vector.scalar_tensor_tensor(
                            out=st[0][:, tok], in0=st[1][:, tok], scalar=scalars[n][:] if n in scalars else st[2],
                            in1=st[3][:, tok], op0=st[4], op1=st[5])
                    v.then_inc(s.step, 1)
                    dve.wait_ge(s.step, b * len(steps) + n + 1)
    release(nc, s)


def grouped_conv(nc, name, h, target, weight, shift):
    with ExitStack() as ctx:
        def sb(n, shape):
            return ctx.enter_context(nc.sbuf_tensor(f"{name}_{n}", shape, F32))

        ps = ctx.enter_context(nc.psum_tensor(f"{name}_ps", [128, 2, TB], F32))
        wt = sb("wt", [128, 4, 128])
        bt = sb("bt", [128, 1])
        s = semaphores(nc, name, "zeroed loads product taken")
        block = ctx.enter_context(nc.Block())

        @block.sync
        def _(sp):
            sp.wait_ge(s.zeroed, 1)
            with nc.allow_non_contiguous_dma("blocks of 32"):
                for g in range(4):
                    r = slice(32 * g, 32 * g + 32)
                    sp.dma_start(wt[r, :, r], weight[:, :, r].rearrange("k i o -> i k o")).then_inc(s.loads, 16)
                sp.dma_start(bt[:], column(shift)).then_inc(s.loads, 16)

        @block.gpsimd
        def _(pool):
            pool.memset(wt[:], 0.0).then_inc(s.zeroed, 1)

        @block.tensor
        def _(pe):
            pe.wait_ge(s.loads, 80)
            with pe.Fori(0, BATCH) as b:
                for j in range(2):
                    pe.wait_ge(s.taken, b * 2 + j + 1)
                    for k in range(4):
                        skip = k if j == 0 else 0
                        mm = nc.tensor.matmul(ps[:, j, skip:TB], wt[:, 3 - k, :],
                                              h[:, bass.ds(b * SEQ + j * TB - k + skip, TB - skip)],
                                              start=(k == 0), stop=(k == 3), skip_group_check=True)
                    mm.then_inc(s.product, 1)

        @block.vector
        def _(dve):
            dve.sem_inc(s.taken, 2)
            dve.wait_ge(s.loads, 80)
            with dve.Fori(0, BATCH) as b:
                for j in range(2):
                    tok = bass.ds(b * SEQ + j * TB, TB)
                    dve.wait_ge(s.product, b * 2 + j + 1)
                    nc.vector.scalar_tensor_tensor(out=target[:, tok], in0=ps[:, j, :], scalar=bt[:],
                                                   in1=target[:, tok], op0=ALU.add, op1=ALU.add).then_inc(s.taken, 1)
    release(nc, s)


def pooled_mix(nc, name, q, k, v, target):
    with ExitStack() as ctx:
        def sb(n, shape, dt=F32):
            return ctx.enter_context(nc.sbuf_tensor(f"{name}_{n}", shape, dt))

        count = sb("count", [128, SEQ], I32)
        inv = sb("inv", [128, SEQ])
        one = sb("one", [128, SEQ])
        t1, t2 = sb("t1", [128, SEQ]), sb("t2", [128, SEQ])
        s = semaphores(nc, name, "consts setup step")
        block = ctx.enter_context(nc.Block())

        @block.gpsimd
        def _(pool):
            pool.iota(count[:], pattern=[[1, SEQ]], base=1, channel_multiplier=0).then_inc(s.consts, 1)
            pool.memset(one[:], 1.0).then_inc(s.consts, 1)

        @block.vector
        def _(dve):
            V = nc.vector
            dve.wait_ge(s.consts, 2)
            V.tensor_copy(t1[:], count[:]).then_inc(s.setup, 1)
            dve.wait_ge(s.setup, 1)
            V.reciprocal(inv[:], t1[:]).then_inc(s.setup, 1)
            dve.wait_ge(s.setup, 2)
            with dve.Fori(0, BATCH) as b:
                tok = bass.ds(b * SEQ, SEQ)
                steps = (
                    lambda: V.tensor_tensor_scan(t1[:], one[:], q[:, tok], 0.0, ALU.mult, ALU.add),
                    lambda: V.tensor_tensor(t1[:], t1[:], inv[:], ALU.mult),
                    lambda: V.tensor_tensor(t1[:], t1[:], k[:, tok], ALU.mult),
                    lambda: V.tensor_tensor_scan(t2[:], one[:], t1[:], 0.0, ALU.mult, ALU.add),
                    lambda: V.tensor_tensor(t2[:], t2[:], inv[:], ALU.mult),
                    lambda: V.tensor_tensor(t2[:], t2[:], v[:, tok], ALU.mult),
                    lambda: V.tensor_tensor(target[:, tok], target[:, tok], t2[:], ALU.add),
                )
                for n, step in enumerate(steps):
                    step().then_inc(s.step, 1)
                    dve.wait_ge(s.step, b * len(steps) + n + 1)
    release(nc, s)


def mean_gate(nc, name, xc, gate, w_c):
    with ExitStack() as ctx:
        def sb(n, shape):
            return ctx.enter_context(nc.sbuf_tensor(f"{name}_{n}", shape, F32))

        c_ps = ctx.enter_context(nc.psum_tensor(f"{name}_c_ps", [16, 2, TB], F32))
        g_ps = ctx.enter_context(nc.psum_tensor(f"{name}_g_ps", [128, 2, TB], F32))
        wc = sb("wc", [128, 2, 16])
        mean = sb("mean", [16, 128])
        c = sb("c", [16, 2, TB])
        s = semaphores(nc, name, "loads consts c_product c_ready g_product g_ready")
        block = ctx.enter_context(nc.Block())

        @block.sync
        def _(sp):
            sp.dma_start(wc[:], w_c.rearrange("(t p) n -> p t n", p=128)).then_inc(s.loads, 16)

        @block.gpsimd
        def _(pool):
            pool.memset(mean[:], 1.0 / 16).then_inc(s.consts, 1)

        @block.tensor
        def _(pe):
            pe.wait_ge(s.loads, 16)
            pe.wait_ge(s.consts, 1)
            with pe.Fori(0, BATCH) as b:
                for j in range(2):
                    tok = bass.ds(b * SEQ + j * TB, TB)
                    pe.wait_ge(s.c_ready, b * 2 + j + 1)
                    pe.nop(nofuse=True)
                    for t in range(2):
                        mm = nc.tensor.matmul(c_ps[:, j, :], wc[:, t, :], xc[t][:, tok], start=(t == 0), stop=(t == 1))
                    mm.then_inc(s.c_product, 1)
                    pe.wait_ge(s.c_ready, b * 2 + j + 3)
                    pe.wait_ge(s.g_ready, b * 2 + j + 1)
                    nc.tensor.matmul(g_ps[:, j, :], mean[:], c[:, j, :], start=True, stop=True).then_inc(s.g_product, 1)

        @block.scalar
        def _(act):
            act.sem_inc(s.c_ready, 2)
            act.sem_inc(s.g_ready, 2)
            with act.Fori(0, BATCH) as b:
                for j in range(2):
                    act.wait_ge(s.c_product, b * 2 + j + 1)
                    nc.scalar.activation(c[:, j, :], c_ps[:, j, :], ACT.Copy).then_inc(s.c_ready, 1)
                    act.wait_ge(s.g_product, b * 2 + j + 1)
                    act.nop(nofuse=True)
                    nc.scalar.activation(gate[:, bass.ds(b * SEQ + j * TB, TB)], g_ps[:, j, :],
                                         ACT.Sigmoid).then_inc(s.g_ready, 1)
    release(nc, s)


def selective_scan(nc, name, u, b_rows, c_rows, y, delta=None, a_log=None, decay_rows=None):
    N, NT = 16, 2
    shared_decay = decay_rows is not None
    sources = [b_rows, c_rows] + ([decay_rows] if shared_decay else [])
    rows_of, stack = [r for r, _, _ in sources], [t for _, _, t in sources]
    R = len(sources)
    with ExitStack() as ctx:
        def sb(n, shape, dt=F32):
            return ctx.enter_context(nc.sbuf_tensor(f"{name}_{n}", shape, dt))

        row_ps = ctx.enter_context(nc.psum_tensor(f"{name}_row_ps", [128, 2, 2, TB], F32))
        y_ps = ctx.enter_context(nc.psum_tensor(f"{name}_y_ps", [128, NT, 2, TB], F32))
        ident = sb("ident", [128, 128])
        split_all = sb("split", [128, 3, SEQ], BF16)
        rest_all = sb("rest", [128, SEQ])
        split, rest = ([t[base:base + N] for _, base, _ in sources] for t in (split_all, rest_all))
        pick = sb("pick", [3 * N, N], BF16)
        a_col = sb("a_col", [128, NT, N])
        bn = sb("bn", [128, 2, SEQ])
        cn = sb("cn", [128, 2, SEQ])
        decay = sb("decay", [128, 2, SEQ])
        bu = sb("bu", [128, 2, SEQ])
        hs = sb("hs", [128, SEQ])
        hc = sb("hc", [128, 2, SEQ])
        s = semaphores(nc, name, "loads consts a_step part1 rest_ready part2 part3 stacked "
                                 "rows rows_read decay_ready bu_ready state hc_ready summed y_read")
        K = N * NT
        SPLIT_AT = (3, 5, 7)[:R]
        block = ctx.enter_context(nc.Block())

        @block.sync
        def _(sp):
            if a_log is not None:
                sp.dma_start(a_col[:], a_log.rearrange("(t p) n -> p t n", p=128)).then_inc(s.loads, 16)
            with sp.Fori(0, BATCH) as b:
                for r in range(R):
                    sp.wait_ge(s.part3, b * R + r + 2)
                    sp.nop(nofuse=True)
                    for i in range(3):
                        sp.dma_start(stack[r][i * N:(i + 1) * N, bass.ds(b * SEQ, SEQ)],
                                     split[r][:, i, :]).then_inc(s.stacked, 16)

        @block.gpsimd
        def _(pool):
            pool.memset(ident[:], 0.0).then_inc(s.consts, 1)
            pool.wait_ge(s.consts, 1)
            pool.affine_select(out=ident[:], in_=ident[:], compare_op=ALU.not_equal, fill=1.0, base=0,
                               pattern=[[-1, 128]], channel_multiplier=1).then_inc(s.consts, 1)
            pool.memset(pick[:], 0.0).then_inc(s.consts, 1)
            for i in range(3):
                pool.wait_ge(s.consts, 3 + i)
                pool.affine_select(out=pick[:], in_=pick[:], compare_op=ALU.not_equal, fill=1.0, base=-i * N,
                                   pattern=[[-1, N]], channel_multiplier=1).then_inc(s.consts, 1)
            pool.sem_inc(s.rest_ready, 1)
            pool.sem_inc(s.part3, 1)

            def split_rows(b, r):
                m = b * R + r
                pool.wait_ge(s.part1, m + 1)
                pool.wait_ge(s.part3, m + 1)
                pool.nop(nofuse=True)
                nc.gpsimd.tensor_tensor(rest[r], rows_of[r][:, bass.ds(b * SEQ, SEQ)], split[r][:, 0, :],
                                        ALU.subtract).then_inc(s.rest_ready, 1)
                pool.wait_ge(s.part2, m + 1)
                pool.wait_ge(s.rest_ready, m + 2)
                nc.gpsimd.tensor_tensor(split[r][:, 2, :], rest[r], split[r][:, 1, :],
                                        ALU.subtract).then_inc(s.part3, 1)

            for r in range(R):
                split_rows(0, r)

            def products(b, last):
                for n in range(N):
                    if not last and n in SPLIT_AT:
                        pool.wait_ge(s.bu_ready, b * K + n * NT)
                        split_rows(b + 1, SPLIT_AT.index(n))
                        pool.wait_ge(s.part3, (b + 1) * R + SPLIT_AT.index(n) + 2)
                    for t in range(NT):
                        k = n * NT + t
                        if t == 0:
                            pool.wait_ge(s.rows_read, b * (N * R) + n * R + 3)
                        pool.wait_ge(s.state, b * K + k + 1)
                        pool.nop(nofuse=True)
                        nc.gpsimd.tensor_tensor(bu[:, k % 2], u[t][:, bass.ds(b * SEQ, SEQ)], bn[:, n % 2],
                                                ALU.mult).then_inc(s.bu_ready, 1)

            pool.wait_ge(s.part3, R + 1)
            with pool.Fori(0, BATCH - 1) as b:
                products(b, last=False)
            products(BATCH - 1, last=True)

        @block.tensor
        def _(pe):
            pe.wait_ge(s.consts, 6)

            def repeat(b, n):
                for r in range(R):
                    m = n * R + r
                    pe.wait_ge(s.rows_read, b * (N * R) + m + 1)
                    pe.nop(nofuse=True)
                    for j in range(2):
                        mm = nc.tensor.matmul(row_ps[:, m % 2, j, :],
                                              pick[:, n:n + 1].to_broadcast([3 * N, 128]),
                                              stack[r][:, bass.ds(b * SEQ + j * TB, TB)], start=True, stop=True)
                    mm.then_inc(s.rows, 1)

            with pe.Fori(0, BATCH) as b:
                pe.wait_ge(s.stacked, (b + 1) * (16 * 3 * R))
                repeat(b, 0)
                for n in range(N):
                    if n + 1 < N:
                        repeat(b, n + 1)
                    for t in range(NT):
                        k = n * NT + t
                        pe.wait_ge(s.hc_ready, b * K + k + 3)
                        if n == 0:
                            pe.wait_ge(s.y_read, b * NT + t + 1)
                        for j in range(2):
                            mm = nc.tensor.matmul(y_ps[:, t, j, :], ident[:], hc[:, k % 2, j * TB:(j + 1) * TB],
                                                  start=(n == 0), stop=(n == N - 1))
                        mm.then_inc(s.summed, 1)

        @block.scalar
        def _(act):
            act.sem_inc(s.rows_read, 2)
            act.sem_inc(s.y_read, NT)
            if a_log is not None:
                act.wait_ge(s.loads, 16)
                nc.scalar.activation(a_col[:], a_col[:], ACT.Exp).then_inc(s.a_step, 1)
                act.wait_ge(s.a_step, 1)
                nc.scalar.activation(a_col[:], a_col[:], ACT.Copy, scale=-1.0).then_inc(s.a_step, 1)
                act.wait_ge(s.a_step, 2)

            def split_rows(b, r, first=False):
                m = b * R + r
                if not first:
                    act.wait_ge(s.stacked, m * (16 * 3))
                act.nop(nofuse=True)
                nc.scalar.activation(split[r][:, 0, :], rows_of[r][:, bass.ds(b * SEQ, SEQ)],
                                     ACT.Copy).then_inc(s.part1, 1)
                act.wait_ge(s.rest_ready, m + 2)
                nc.scalar.activation(split[r][:, 1, :], rest[r], ACT.Copy).then_inc(s.part2, 1)

            for r in range(R):
                split_rows(0, r, first=r == 0)

            def batch(b, last):
                for n in range(N):
                    if not last and n in SPLIT_AT:
                        split_rows(b + 1, SPLIT_AT.index(n))
                    targets = [bn, cn] + ([decay] if shared_decay else [])
                    for r, to in enumerate(targets):
                        m = n * R + r
                        act.wait_ge(s.rows, b * (N * R) + m + 1)
                        if r == 0:
                            act.wait_ge(s.hc_ready, b * K + max(n * NT, 1))
                        nc.scalar.activation(to[:, n % 2], row_ps[:, m % 2].rearrange("p j t -> p (j t)"),
                                                 ACT.Copy).then_inc(s.rows_read, 1)
                    if not shared_decay:
                        for t in range(NT):
                            k = n * NT + t
                            act.wait_ge(s.state, b * K + k + 1)
                            act.nop(nofuse=True)
                            nc.scalar.activation(decay[:, k % 2], delta[t][:, bass.ds(b * SEQ, SEQ)], ACT.Exp,
                                                 scale=a_col[:, t, n:n + 1]).then_inc(s.decay_ready, 1)
                for t in range(NT):
                    act.wait_ge(s.summed, b * K + K - NT + t + 3)
                    act.nop(nofuse=True)
                    nc.scalar.activation(y[t][:, bass.ds(b * SEQ, SEQ)], y_ps[:, t].rearrange("p j t -> p (j t)"),
                                         ACT.Copy).then_inc(s.y_read, 1)

            with act.Fori(0, BATCH - 1) as b:
                batch(b, last=False)
            batch(BATCH - 1, last=True)

        @block.vector
        def _(dve):
            dve.sem_inc(s.state, 2)
            dve.sem_inc(s.hc_ready, 2)
            dve.sem_inc(s.summed, 2)
            with dve.Fori(0, BATCH) as b:
                for n in range(N):
                    for t in range(NT):
                        k = n * NT + t
                        dve.wait_ge(s.bu_ready, b * K + k + 1)
                        if shared_decay:
                            dve.wait_ge(s.rows_read, b * (N * R) + n * R + 5)
                        else:
                            dve.wait_ge(s.rows_read, b * (N * R) + n * R + 4)
                            dve.wait_ge(s.decay_ready, b * K + k + 1)
                        dve.wait_ge(s.hc_ready, b * K + k + 2)
                        nc.vector.tensor_tensor_scan(hs[:], decay[:, n % 2 if shared_decay else k % 2], bu[:, k % 2],
                                                     0.0, ALU.mult, ALU.add).then_inc(s.state, 1)
                        dve.wait_ge(s.state, b * K + k + 3)
                        dve.wait_ge(s.summed, b * K + k + 1)
                        nc.vector.tensor_tensor(hc[:, k % 2], hs[:], cn[:, n % 2], ALU.mult).then_inc(s.hc_ready, 1)
    release(nc, s)


def softplus(nc, name, tiles):
    nt = len(tiles)
    with ExitStack() as ctx:
        a = ctx.enter_context(nc.sbuf_tensor(f"{name}_a", [128, 2, SEQ], F32))
        s = semaphores(nc, name, "a_step done")
        block = ctx.enter_context(nc.Block())

        @block.scalar
        def _(act):
            act.sem_inc(s.done, 2)
            with act.Fori(0, BATCH) as b:
                for t in range(nt):
                    act.wait_ge(s.done, b * nt + t + 1)
                    act.nop(nofuse=True)
                    steps = (
                        lambda: nc.scalar.activation(a[:, t % 2], tiles[t][:, bass.ds(b * SEQ, SEQ)], ACT.Abs),
                        lambda: nc.scalar.activation(a[:, t % 2], a[:, t % 2], ACT.Exp, scale=-1.0),
                        lambda: nc.scalar.activation(a[:, t % 2], a[:, t % 2], ACT.Ln, bias=1.0),
                    )
                    for n, step in enumerate(steps):
                        step().then_inc(s.a_step, 1)
                        act.wait_ge(s.a_step, b * (3 * nt) + 3 * t + n + 1)

        @block.vector
        def _(dve):
            with dve.Fori(0, BATCH) as b:
                for t in range(nt):
                    tok = bass.ds(b * SEQ, SEQ)
                    dve.wait_ge(s.a_step, b * (3 * nt) + 3 * t + 3)
                    nc.vector.scalar_tensor_tensor(out=tiles[t][:, tok], in0=tiles[t][:, tok], scalar=0.0,
                                                   in1=a[:, t % 2], op0=ALU.max, op1=ALU.add).then_inc(s.done, 1)
    release(nc, s)


def clipped_decay(nc, name, rows):
    s = semaphores(nc, name, "clipped step")
    with nc.Block() as block:
        @block.vector
        def _(dve):
            with dve.Fori(0, BATCH) as b:
                r = rows[:, bass.ds(b * SEQ, SEQ)]
                nc.vector.tensor_scalar(r, r, -5.0, 0.0, ALU.max, ALU.min).then_inc(s.clipped, 1)

        @block.scalar
        def _(act):
            with act.Fori(0, BATCH) as b:
                r = rows[:, bass.ds(b * SEQ, SEQ)]
                act.wait_ge(s.clipped, b + 1)
                act.nop(nofuse=True)
                nc.scalar.activation(r, r, ACT.Exp).then_inc(s.step, 1)
                act.wait_ge(s.step, b * 2 + 1)
                act.nop(nofuse=True)
                nc.scalar.activation(r, r, ACT.Exp, scale=-1.0).then_inc(s.step, 1)
    release(nc, s)


def feature_map(nc, name, q, k, scale):
    with ExitStack() as ctx:
        low = ctx.enter_context(nc.sbuf_tensor(f"{name}_low", [128, 2, SEQ], F32))
        s = semaphores(nc, name, "low_ready expd done")
        block = ctx.enter_context(nc.Block())

        @block.vector
        def _(dve):
            dve.sem_inc(s.done, 2)
            with dve.Fori(0, BATCH) as b:
                tok = bass.ds(b * SEQ, SEQ)
                for z, t in enumerate((q, k)):
                    dve.wait_ge(s.done, b * 2 + z + 1)
                    nc.vector.tensor_scalar(low[:, z], t[:, tok], scale if z == 0 else 1.0, 0.0, ALU.mult,
                                            ALU.min).then_inc(s.low_ready, 1)
                for z, t in enumerate((q, k)):
                    dve.wait_ge(s.expd, b * 2 + z + 1)
                    nc.vector.tensor_scalar(t[:, tok], t[:, tok], 0.0, scale if z == 0 else 1.0, ALU.max,
                                            ALU.mult).then_inc(s.low_ready, 1)
                    dve.wait_ge(s.low_ready, b * 4 + z + 3)
                    nc.vector.tensor_tensor(t[:, tok], t[:, tok], low[:, z], ALU.add).then_inc(s.done, 1)

        @block.scalar
        def _(act):
            with act.Fori(0, BATCH) as b:
                for z in range(2):
                    act.wait_ge(s.low_ready, b * 4 + z + 1)
                    nc.scalar.activation(low[:, z], low[:, z], ACT.Exp).then_inc(s.expd, 1)
    release(nc, s)


def gated_linear_attention(nc, name, q, k, v, gate, y):
    NT = 8
    with ExitStack() as ctx:
        def sb(n, shape):
            return ctx.enter_context(nc.sbuf_tensor(f"{name}_{n}", shape, F32))

        rep_ps = ctx.enter_context(nc.psum_tensor(f"{name}_rep_ps", [128, 3, 2, TB], F32))
        y_ps = ctx.enter_context(nc.psum_tensor(f"{name}_y_ps", [128, 2, TB], F32))
        sel_i = sb("sel_i", [128, NT, 128])
        sel_j = sb("sel_j", [128, NT, 128])
        sel_g = sb("sel_g", [HEADS, NT, 128])
        sum_j = sb("sum_j", [128, NT, 128])
        ks = sb("ks", [128, SEQ])
        gs = sb("gs", [128, 2, SEQ])
        kv = sb("kv", [128, 2, SEQ])
        st = sb("st", [128, SEQ])
        qst = sb("qst", [128, 2, SEQ])
        s = semaphores(nc, name, "consts rep ks_ready gs_ready kv_ready state qs_ready summed y_read")
        K = NT
        block = ctx.enter_context(nc.Block())

        @block.gpsimd
        def _(pool):
            def view(t):
                return t[:].rearrange("p t (h i j) -> p t h i j", h=2, i=8)

            pool.memset(sel_i[:], 1.0).then_inc(s.consts, 1)
            pool.memset(sel_j[:], 0.0).then_inc(s.consts, 1)
            pool.memset(sel_g[:], 1.0).then_inc(s.consts, 1)
            pool.memset(sum_j[:], 0.0).then_inc(s.consts, 1)
            pool.wait_ge(s.consts, 4)
            pool.affine_select(out=sel_i[:], in_=sel_i[:], compare_op=ALU.is_ge, fill=0.0, base=0,
                               pattern=[[128, NT], [1, 128]], channel_multiplier=-8).then_inc(s.consts, 1)
            pool.wait_ge(s.consts, 5)
            pool.affine_select(out=sel_i[:], in_=sel_i[:], compare_op=ALU.is_ge, fill=0.0, base=7,
                               pattern=[[-128, NT], [-1, 128]], channel_multiplier=8).then_inc(s.consts, 1)
            pool.affine_select(out=sel_g[:], in_=sel_g[:], compare_op=ALU.is_ge, fill=0.0, base=0,
                               pattern=[[128, NT], [1, 128]], channel_multiplier=-64).then_inc(s.consts, 1)
            pool.wait_ge(s.consts, 7)
            pool.affine_select(out=sel_g[:], in_=sel_g[:], compare_op=ALU.is_ge, fill=0.0, base=63,
                               pattern=[[-128, NT], [-1, 128]], channel_multiplier=64).then_inc(s.consts, 1)
            n = 8
            for h in range(2):
                part = sel_j[:, :, 64 * h:64 * h + 64].rearrange("p t (i j) -> p t i j", i=8)
                pool.affine_select(out=part, in_=part, compare_op=ALU.not_equal, fill=1.0, base=-8 * h,
                                   pattern=[[-16, NT], [0, 8], [-1, 8]], channel_multiplier=1).then_inc(s.consts, 1)
                n += 1
                pool.wait_ge(s.consts, n)
            for i in range(8):
                for t in range(NT):
                    part = sum_j[:, t, 16 * t:16 * t + 16].rearrange("p (h j) -> p h j", h=2)
                    pool.affine_select(out=part, in_=part, compare_op=ALU.not_equal, fill=1.0, base=-8 * i,
                                       pattern=[[-64, 2], [-1, 8]], channel_multiplier=1).then_inc(s.consts, 1)
                n += NT
                pool.wait_ge(s.consts, n)

        CONSTS = 10 + 8 * NT

        @block.tensor
        def _(pe):
            pe.wait_ge(s.consts, CONSTS)

            def add_up(b, t):
                pe.wait_ge(s.qs_ready, b * K + t + 3)
                if t == 0:
                    pe.wait_ge(s.y_read, b + 1)
                for j in range(2):
                    mm = nc.tensor.matmul(y_ps[:, j, :], sum_j[:, t, :], qst[:, t % 2, j * TB:(j + 1) * TB],
                                          start=(t == 0), stop=(t == NT - 1))
                mm.then_inc(s.summed, 1)

            with pe.Fori(0, BATCH) as b:
                for t in range(NT):
                    g = b * K + t
                    for r, (slot, sel, rows) in enumerate(((1, sel_j, v), (2, sel_g, gate), (0, sel_i, k),
                                                           (0, sel_i, q))):
                        if r == 0:
                            pe.wait_ge(s.kv_ready, g + 1)
                        if r == 1:
                            pe.wait_ge(s.gs_ready, g + 1)
                        if r == 2:
                            pe.wait_ge(s.qs_ready, g + 2)
                        if r == 3:
                            if t > 0:
                                add_up(b, t - 1)
                            pe.wait_ge(s.ks_ready, g + 2)
                        pe.nop(nofuse=True)
                        for j in range(2):
                            mm = nc.tensor.matmul(rep_ps[:, slot, j, :], sel[:, t, :],
                                                  rows[:, bass.ds(b * SEQ + j * TB, TB)], start=True, stop=True)
                        mm.then_inc(s.rep, 1)
                add_up(b, NT - 1)

        @block.scalar
        def _(act):
            act.sem_inc(s.ks_ready, 1)
            act.sem_inc(s.gs_ready, 1)
            act.sem_inc(s.y_read, 1)
            with act.Fori(0, BATCH) as b:
                for t in range(NT):
                    g = b * K + t
                    act.wait_ge(s.rep, g * 4 + 2)
                    act.wait_ge(s.state, g + 1)
                    nc.scalar.activation(gs[:, t % 2], rep_ps[:, 2].rearrange("p j t -> p (j t)"), ACT.Copy).then_inc(
                        s.gs_ready, 1)
                    act.wait_ge(s.rep, g * 4 + 3)
                    act.wait_ge(s.kv_ready, g + 1)
                    nc.scalar.activation(ks[:], rep_ps[:, 0].rearrange("p j t -> p (j t)"), ACT.Copy).then_inc(
                        s.ks_ready, 1)
                act.wait_ge(s.summed, b * K + K + 2)
                act.nop(nofuse=True)
                nc.scalar.activation(y[:, bass.ds(b * SEQ, SEQ)], y_ps[:].rearrange("p j t -> p (j t)"),
                                     ACT.Copy).then_inc(s.y_read, 1)

        @block.vector
        def _(dve):
            dve.sem_inc(s.kv_ready, 1)
            dve.sem_inc(s.state, 2)
            dve.sem_inc(s.qs_ready, 2)
            dve.sem_inc(s.summed, 2)
            with dve.Fori(0, BATCH) as b:
                for t in range(NT):
                    g = b * K + t
                    dve.wait_ge(s.ks_ready, g + 2)
                    dve.wait_ge(s.rep, g * 4 + 1)
                    dve.wait_ge(s.state, g + 1)
                    nc.vector.tensor_tensor(kv[:, t % 2], ks[:], rep_ps[:, 1].rearrange("p j t -> p (j t)"),
                                            ALU.mult).then_inc(s.kv_ready, 1)
                    dve.wait_ge(s.kv_ready, g + 2)
                    dve.wait_ge(s.gs_ready, g + 2)
                    dve.wait_ge(s.qs_ready, g + 2)
                    nc.vector.tensor_tensor_scan(st[:], gs[:, t % 2], kv[:, t % 2], 0.0, ALU.mult,
                                                 ALU.add).then_inc(s.state, 1)
                    dve.wait_ge(s.rep, g * 4 + 4)
                    dve.wait_ge(s.state, g + 3)
                    dve.wait_ge(s.summed, g + 1)
                    nc.vector.tensor_tensor(qst[:, t % 2], st[:], rep_ps[:, 0].rearrange("p j t -> p (j t)"),
                                            ALU.mult).then_inc(s.qs_ready, 1)
    release(nc, s)


WAVE_HEADS, POS, SAMPLES = 8, 16, 33
SUBS = TB // 128


def wave_attention_weights(nc, name, h, rows, attn, index, p):
    WH, H, S = 3 * WAVE_HEADS, WAVE_HEADS, SAMPLES
    with ExitStack() as ctx:
        def sb(n, shape, dt=F32):
            return ctx.enter_context(nc.sbuf_tensor(f"{name}_{n}", shape, dt))

        tok_ps = ctx.enter_context(nc.psum_tensor(f"{name}_tok_ps", [128, SUBS, 128], F32))
        query_ps = ctx.enter_context(nc.psum_tensor(f"{name}_query_ps", [128, SUBS, 128], F32))
        wave_ps = ctx.enter_context(nc.psum_tensor(f"{name}_wave_ps", [128, SUBS, WH], F32))
        ident = sb("ident", [128, 128])
        w_wave, w_query = sb("w_wave", [128, WH]), sb("w_query", [128, H * POS])
        b_wave, b_query, key = sb("b_wave", [128, WH]), sb("b_query", [128, H * POS]), sb("key", [128, POS])
        grid_i, grid, grid_abs = sb("grid_i", [128, S], I32), sb("grid", [128, S]), sb("grid_abs", [128, S])
        centre_i, centre = sb("centre_i", [128, SUBS], I32), sb("centre", [128, SUBS])
        hb = sb("hb", [128, TB])
        tok = sb("tok", [128, SUBS, 128])
        wave = sb("wave", [128, SUBS, WH])
        wave_f = sb("wave_f", [128, 3, SUBS, H])
        query = sb("query", [128, SUBS, H * POS])
        avg = sb("avg", [128, 3, SUBS])
        qk = sb("qk", [128, SUBS, H])
        pos, cell, mask, rel, env, t33 = (sb(m, [128, SUBS, S]) for m in ("pos", "cell", "mask", "rel", "env", "t33"))
        cell_i = sb("cell_i", [128, SUBS, S], I32)
        sc = sb("sc", [128, SUBS * H, S])
        first = sb("first", [128, 1])
        zero33 = sb("zero33", [128, SUBS, S])
        big = sb("big", [128, SUBS * H])
        big2 = sb("big2", [128, SUBS * H])
        s = semaphores(nc, name, "loads consts setup copied products tok_ready written wave_in wave_silu query_in "
                                 "query_silu wave_done env_in env_done exp_in exp_done chain done next_first")
        loads = [(w_wave[:], p["w_wave"]), (w_query[:], p["w_query"]),
                 (b_wave[:], p["b_wave"].partition_broadcast(128)), (b_query[:], p["b_query"].partition_broadcast(128)),
                 (key[:], p["key_weight"].partition_broadcast(128))]
        block = ctx.enter_context(nc.Block())

        @block.sync
        def _(sp):
            for to, source in loads:
                sp.dma_start(to, source).then_inc(s.loads, 16)
            sp.sem_inc(s.written, 1)
            with sp.Fori(0, NTB) as b:
                sp.wait_ge(s.tok_ready, b + 1)
                sp.dma_start(rows[bass.ds(b * TB, TB), :].rearrange("(q p) c -> p q c", p=128), tok[:]).then_inc(
                    s.written, 16)
            sp.wait_ge(s.written, 16 * NTB + 1)

        @block.gpsimd
        def _(pool):
            pool.memset(ident[:], 0.0).then_inc(s.consts, 1)
            pool.iota(grid_i[:], pattern=[[1, S]], base=-(S // 2), channel_multiplier=0).then_inc(s.consts, 1)
            pool.iota(centre_i[:], pattern=[[128, SUBS]], base=0, channel_multiplier=1).then_inc(s.consts, 1)
            pool.wait_ge(s.consts, 3)
            pool.affine_select(out=ident[:], in_=ident[:], compare_op=ALU.not_equal, fill=1.0, base=0,
                               pattern=[[-1, 128]], channel_multiplier=1).then_inc(s.consts, 1)

        @block.tensor
        def _(pe):
            pe.wait_ge(s.loads, 16 * len(loads))
            pe.wait_ge(s.consts, 4)
            with pe.Fori(0, NTB) as b:
                pe.wait_ge(s.copied, b + 1)
                pe.wait_ge(s.done, b + 1)
                for q in range(SUBS):
                    nc.tensor.transpose(tok_ps[:, q, :], hb[:, q * 128:(q + 1) * 128], ident[:])
                    nc.tensor.matmul(wave_ps[:, q, :], hb[:, q * 128:(q + 1) * 128], w_wave[:], start=True, stop=True)
                    mm = nc.tensor.matmul(query_ps[:, q, :], hb[:, q * 128:(q + 1) * 128], w_query[:],
                                          start=True, stop=True)
                mm.then_inc(s.products, 1)

        @block.scalar
        def _(act):
            with act.Fori(0, NTB) as b:
                act.wait_ge(s.done, b + 1)
                act.nop(nofuse=True)
                nc.scalar.activation(hb[:], h[:, bass.ds(b * TB, TB)], ACT.Copy).then_inc(s.copied, 1)
                act.wait_ge(s.products, b + 1)
                act.wait_ge(s.written, b * 16 + 1)
                nc.scalar.activation(tok[:], tok_ps[:], ACT.Copy).then_inc(s.tok_ready, 1)
                act.wait_ge(s.query_in, b + 1)
                nc.scalar.activation(query[:], query[:], ACT.Silu).then_inc(s.query_silu, 1)
                nc.scalar.activation(wave[:], wave[:], ACT.Silu).then_inc(s.wave_silu, 1)
                act.wait_ge(s.wave_silu, b + 1)
                w = wave[:].rearrange("p q (f h) -> p f q h", f=3)
                nc.scalar.activation(wave_f[:, 0], w[:, 0], ACT.Sigmoid)
                nc.scalar.activation(wave_f[:, 2], w[:, 2], ACT.Sigmoid)
                nc.scalar.activation(wave_f[:, 1], w[:, 1], ACT.Tanh).then_inc(s.wave_done, 1)
                act.wait_ge(s.env_in, b + 1)
                nc.scalar.activation(env[:], env[:], ACT.Exp).then_inc(s.env_done, 1)
                act.wait_ge(s.exp_in, b + 1)
                nc.scalar.activation(sc[:], sc[:], ACT.Exp).then_inc(s.exp_done, 1)

        @block.vector
        def _(dve):
            V, tt = nc.vector, nc.vector.tensor_tensor
            dve.sem_inc(s.done, 1)
            dve.wait_ge(s.loads, 16 * len(loads))
            dve.wait_ge(s.consts, 4)
            V.tensor_copy(grid[:], grid_i[:]).then_inc(s.setup, 1)
            V.tensor_copy(centre[:], centre_i[:]).then_inc(s.setup, 1)
            dve.wait_ge(s.setup, 2)
            V.scalar_tensor_tensor(out=grid_abs[:], in0=grid[:], scalar=-1.0, in1=grid[:], op0=ALU.mult,
                                   op1=ALU.max).then_inc(s.setup, 1)
            V.memset(first[:], 0.0).then_inc(s.setup, 1)
            V.memset(zero33[:], 0.0).then_inc(s.setup, 1)
            dve.wait_ge(s.setup, 5)
            LINKS = 33
            with dve.Fori(0, BATCH) as b:
                for j in range(2):
                    k = b * 2 + j
                    links = [0]

                    def link(ins):
                        links[0] += 1
                        ins.then_inc(s.chain, 1)
                        dve.wait_ge(s.chain, k * LINKS + links[0])

                    def over_samples(a):
                        return a.unsqueeze(2).to_broadcast([128, SUBS, S])

                    def over_tiles(a, n=S):
                        return a.unsqueeze(1).to_broadcast([128, SUBS, n])

                    dve.wait_ge(s.products, k + 1)
                    link(tt(wave[:], wave_ps[:], over_tiles(b_wave[:], WH), ALU.add))
                    tt(query[:], query_ps[:], over_tiles(b_query[:], H * POS), ALU.add).then_inc(s.query_in, 1)
                    dve.wait_ge(s.query_silu, k + 1)
                    q4 = query[:].rearrange("p q (h d) -> p (q h) d", d=POS)
                    link(tt(q4, q4, key[:].unsqueeze(1).to_broadcast([128, SUBS * H, POS]), ALU.mult))
                    link(V.tensor_reduce(qk[:].rearrange("p q h -> p (q h)"), q4, AX.X, ALU.add))
                    link(V.tensor_scalar(qk[:], qk[:], float(POS) ** -0.5, None, ALU.mult))
                    dve.wait_ge(s.wave_done, k + 1)
                    for f, (scale, shift) in enumerate(((15.0, 1.0), (16.0, 0.0), (9.5, 0.5))):
                        last = V.tensor_scalar(wave_f[:, f], wave_f[:, f], scale, shift, ALU.mult, ALU.add)
                    link(last)
                    link(V.tensor_reduce(avg[:], wave_f[:], AX.X, ALU.add))
                    link(V.tensor_scalar(avg[:], avg[:], 1.0 / H, None, ALU.mult))
                    link(tt(pos[:], over_tiles(grid[:]), over_samples(avg[:, 0]), ALU.mult))
                    link(V.scalar_tensor_tensor(out=pos[:], in0=over_samples(centre[:]), scalar=float(j * TB),
                                                in1=pos[:], op0=ALU.add, op1=ALU.add))
                    link(tt(pos[:], pos[:], over_samples(avg[:, 1]), ALU.add))
                    V.tensor_scalar(mask[:], pos[:], 0.0, None, ALU.is_ge)
                    link(V.tensor_scalar(t33[:], pos[:], float(SEQ), None, ALU.is_lt))
                    link(tt(mask[:], mask[:], t33[:], ALU.mult))
                    link(V.tensor_scalar(pos[:], pos[:], 0.0, float(SEQ - 1), ALU.max, ALU.min))
                    link(V.tensor_copy(cell_i[:], pos[:]))
                    link(V.tensor_copy(cell[:], cell_i[:]))
                    link(tt(t33[:], cell[:], pos[:], ALU.is_gt))
                    link(tt(cell[:], cell[:], t33[:], ALU.subtract))
                    V.scalar_tensor_tensor(out=index[:, bass.ds(k * SUBS, SUBS), :], in0=cell[:], scalar=first[:],
                                           in1=zero33[:], op0=ALU.add, op1=ALU.add)
                    tt(rel[:], over_tiles(grid_abs[:]), over_samples(avg[:, 0]), ALU.mult)
                    link(V.tensor_scalar(big[:, 0:SUBS], avg[:, 2], 0.1, None, ALU.max))
                    link(V.reciprocal(big2[:, 0:SUBS], big[:, 0:SUBS]))
                    link(V.tensor_scalar(big2[:, 0:SUBS], big2[:, 0:SUBS], -1.0, None, ALU.mult))
                    tt(env[:], rel[:], over_samples(big2[:, 0:SUBS]), ALU.mult).then_inc(s.env_in, 1)
                    link(tt(rel[:], rel[:], mask[:], ALU.mult))
                    link(V.tensor_scalar(t33[:], mask[:], 1.0e30, -1.0e30, ALU.mult, ALU.add))
                    for q in range(SUBS):
                        last = tt(sc[:, q * H:(q + 1) * H, :], rel[:, q].unsqueeze(1).to_broadcast([128, H, S]),
                                  qk[:, q].unsqueeze(2).to_broadcast([128, H, S]), ALU.mult)
                    link(last)
                    for q in range(SUBS):
                        last = tt(sc[:, q * H:(q + 1) * H, :], sc[:, q * H:(q + 1) * H, :],
                                  t33[:, q].unsqueeze(1).to_broadcast([128, H, S]), ALU.add)
                    link(last)
                    link(V.tensor_reduce(big[:], sc[:], AX.X, ALU.max))
                    wide = lambda a: a.unsqueeze(2).to_broadcast([128, SUBS * H, S])
                    tt(sc[:], sc[:], wide(big[:]), ALU.subtract).then_inc(s.exp_in, 1)
                    dve.wait_ge(s.exp_done, k + 1)
                    dve.wait_ge(s.env_done, k + 1)
                    link(V.tensor_reduce(big[:], sc[:], AX.X, ALU.add))
                    link(V.reciprocal(big2[:], big[:]))
                    link(tt(sc[:], sc[:], wide(big2[:]), ALU.mult))
                    link(tt(env[:], env[:], mask[:], ALU.mult))
                    for q in range(SUBS):
                        last = tt(sc[:, q * H:(q + 1) * H, :], sc[:, q * H:(q + 1) * H, :],
                                  env[:, q].unsqueeze(1).to_broadcast([128, H, S]), ALU.mult)
                    link(last)
                    link(V.tensor_reduce(big[:], sc[:], AX.X, ALU.add))
                    link(V.tensor_scalar(big[:], big[:], 1e-8, None, ALU.add))
                    link(V.reciprocal(big2[:], big[:]))
                    tt(attn[:, bass.ds(k * SUBS, SUBS)].rearrange("p q h s -> p (q h) s"), sc[:], wide(big2[:]),
                       ALU.mult).then_inc(s.done, 1)
                    assert links[0] == LINKS, links[0]
                dve.wait_ge(s.done, b * 2 + 3)
                V.tensor_scalar(first[:], first[:], float(SEQ), None, ALU.add).then_inc(s.next_first, 1)
                dve.wait_ge(s.next_first, b + 1)
    release(nc, s)


def wave_gather(nc, name, rows, attn, index, out):
    NT, H, S = TOKENS // 128, WAVE_HEADS, SAMPLES
    with ExitStack() as ctx:
        def sb(n, shape, dt=F32):
            return ctx.enter_context(nc.sbuf_tensor(f"{name}_{n}", shape, dt))

        turn_ps = ctx.enter_context(nc.psum_tensor(f"{name}_turn_ps", [128, 2, 512], F32))
        ident = sb("ident", [128, 128])
        vals = sb("vals", [128, 2, S, 128])
        idx = sb("idx", [128, 2, S], I32)
        acc = sb("acc", [128, 2, 128])
        s = semaphores(nc, name, "consts idx_ready gathered0 gathered1 weighted summed turned out_ready")
        gathered = (s.gathered0, s.gathered1)
        block = ctx.enter_context(nc.Block())

        @block.gpsimd
        def _(pool):
            pool.memset(ident[:], 0.0).then_inc(s.consts, 1)
            pool.wait_ge(s.consts, 1)
            pool.affine_select(out=ident[:], in_=ident[:], compare_op=ALU.not_equal, fill=1.0, base=0,
                               pattern=[[-1, 128]], channel_multiplier=1).then_inc(s.consts, 1)
            with pool.Fori(0, NT // 2) as i:
                for j in range(2):
                    pool.wait_ge(s.idx_ready, i * 2 + j + 3)
                    pool.wait_ge(s.summed, i * 2 + j + 1)
                    pool.nop(nofuse=True)
                    for n in range(S):
                        pool.indirect_dma_start(
                            out=vals[:, j, n, :], out_offset=None, in_=rows,
                            in_offset=bass.IndirectOffsetOnAxis(ap=idx[:, j, n:n + 1], axis=0)).then_inc(
                                gathered[j], 16)

        @block.scalar
        def _(act):
            act.sem_inc(s.idx_ready, 2)
            act.sem_inc(s.out_ready, 2)

            def copy_index(i, j):
                nc.scalar.copy(idx[:, j], index[:, bass.ds(i * 2 + j, 1), :].rearrange(
                    "p a s -> p (a s)")).then_inc(s.idx_ready, 1)

            def output(i, j):
                act.wait_ge(s.turned, i * 2 + j + 1)
                act.nop(nofuse=True)
                nc.scalar.activation(out[:, bass.ds(i * 256 + j * 128, 128)], turn_ps[:, j, 0:128],
                                     ACT.Copy).then_inc(s.out_ready, 1)

            for j in range(2):
                copy_index(0, j)
            with act.Fori(0, NT // 2 - 1) as i:
                for j in range(2):
                    output(i, j)
                    act.wait_ge(s.summed, i * 2 + j + 3)
                    act.nop(nofuse=True)
                    copy_index(i + 1, j)
            for j in range(2):
                output(NT // 2 - 1, j)

        @block.vector
        def _(dve):
            dve.sem_inc(s.summed, 2)
            with dve.Fori(0, NT // 2) as i:
                for j in range(2):
                    k = i * 2 + j
                    dve.wait_ge(gathered[j], (i + 1) * (16 * S))
                    for n in range(H):
                        view = vals[:, j, :, 16 * n:16 * n + 16]
                        w = attn[:, bass.ds(k, 1), n, :].rearrange("p a s -> p (a s)").unsqueeze(2).to_broadcast(
                            [128, S, 16])
                        last = nc.vector.tensor_tensor(view, view, w, ALU.mult)
                    last.then_inc(s.weighted, 1)
                    dve.wait_ge(s.weighted, k + 1)
                    dve.wait_ge(s.out_ready, k + 1)
                    nc.vector.tensor_reduce(acc[:, j, :], vals[:, j].rearrange("p s c -> p c s"), AX.X,
                                            ALU.add).then_inc(s.summed, 1)

        @block.tensor
        def _(pe):
            pe.wait_ge(s.consts, 2)
            with pe.Fori(0, NT // 2) as i:
                for j in range(2):
                    pe.wait_ge(s.summed, i * 2 + j + 3)
                    pe.wait_ge(s.out_ready, i * 2 + j + 1)
                    nc.tensor.transpose(turn_ps[:, j, 0:128], acc[:, j, :], ident[:]).then_inc(s.turned, 1)
    release(nc, s)


def add_tile(nc, name, dst, src):
    s = semaphores(nc, name, "done")
    with nc.Block() as block:
        @block.vector
        def _(dve):
            with dve.Fori(0, 4) as i:
                tok = bass.ds(i * 1024, 1024)
                nc.vector.tensor_tensor(dst[:, tok], dst[:, tok], src[:, tok], ALU.add).then_inc(s.done, 1)

        @block.gpsimd
        def _(pool):
            pool.wait_ge(s.done, 4)
    release(nc, s)


def moe_weights(kind, w):
    col = column
    if kind == "L0":
        return dict(wr=w["gate_w"], br=w["gate_b"], wa=w["W1"], wd=w["W2"], bias_a=w["b1"],
                    down_bias=w["b2"])
    if kind == "L1":
        return dict(wr=w["gate_w"], br=w["gate_b"],
                    wa=w["rw1"][:, :, 0:128].rearrange("e d f -> d e f"),
                    wb=w["rw1"][:, :, 128:256].rearrange("e d f -> d e f"),
                    wd=w["rw2"].rearrange("e f d -> f e d"),
                    bias_a=w["rb1"][:, 0:128].rearrange("e f -> f e"),
                    bias_b=w["rb1"][:, 128:256].rearrange("e f -> f e"), down_bias=w["rb2"],
                    sa=w["sw1"][0, :, 0:128], sb=w["sw1"][0, :, 128:256], sd=w["sw2"][0],
                    bias_sa=col(w["sb1"][0, 0:128]), bias_sb=col(w["sb1"][0, 128:256]), bias_sd=col(w["sb2"][0]))
    if kind == "L2":
        return dict(wr=w["router_weight"], br=w["e_bias"],
                    wa=w["gate_w"],
                    wb=w["up_w"], wd=w["down_w"], sa=w["sh_gate_w"], sb=w["sh_up_w"], sd=w["sh_down_w"])
    return dict(wr=w["Wr"], br=w["br"], wa=w["Wg"], wb=w["Wu"],
                wd=w["Wd"].rearrange("(t e) i h -> (e i) t h", e=2),
                bias_a=w["bg"].rearrange("(t e) i -> (e i) t", e=2),
                bias_b=w["bu"].rearrange("(t e) i -> (e i) t", e=2), down_bias=w["bd"],
                sa=w["Wg_s"], sb=w["Wu_s"], sd=w["Wd_s"],
                bias_sa=col(w["bg_s"]), bias_sb=col(w["bu_s"]), bias_sd=col(w["bd_s"]))


def sub_params(a, prefix):
    return {k[len(prefix):]: v for k, v in a.items() if k.startswith(prefix)}


def program(nc, a, x_dram, out_dram, stages):
    with ExitStack() as ctx:
        x = ctx.enter_context(nc.sbuf_tensor("x", [128, TOKENS], F32))
        xn = ctx.enter_context(nc.sbuf_tensor("xn", [128, TOKENS], F32))
        s = semaphores(nc, "io", "loaded stored")
        with nc.Block() as block:
            @block.sync
            def _(sp):
                sp.dma_start(x[:], x_dram).then_inc(s.loaded, 16)
                sp.wait_ge(s.loaded, 16)
        scratch = nc.dram_tensor("heads", (2, PARTS, BATCH * HEADS, DH, SEQ), BF16, kind="Internal").ap()
        for n in stages:
            if n in (1, 3):
                p = sub_params(a, "L0_ffn_")
                norm(nc, f"n{n}", [x], [xn], 1e-5)
                with ExitStack() as inner:
                    h = inner.enter_context(nc.sbuf_tensor(f"h{n}", [128, TOKENS], F32))
                    v_all = inner.enter_context(nc.sbuf_tensor(f"v{n}", [128, BATCH * HEADS, 8, DH + 1], F32))
                    norm(nc, f"na{n}", [xn], [h], 1e-5, gain=p["ln1_g"], shift=p["ln1_b"])
                    q = dict(interleaved=False, causal=False, wq=p["w_qkv"][:, 0:128], wk=p["w_qkv"][:, 128:256],
                             wv=p["w_qkv"][:, 256:384], bq=p["b_qkv"][0:128], bk=p["b_qkv"][128:256],
                             bv=p["b_qkv"][256:384], wo=p["w_o"], bo=p["b_o"])
                    attention_inputs(nc, f"i{n}", h, scratch, v_all, q)
                    attention(nc, f"a{n}", scratch, v_all, xn, q)
                with ExitStack() as inner:
                    h = inner.enter_context(nc.sbuf_tensor(f"hm{n}", [128, TOKENS], F32))
                    add_tile(nc, f"r{n}", x, xn)
                    norm(nc, f"nb{n}", [xn], [h], 1e-5, gain=p["ln2_g"], shift=p["ln2_b"])
                    moe(nc, f"m{n}", "L0", h, x, moe_weights("L0", p))
            if n == 0:
                p = sub_params(a, "L0_attn_a_")
                norm(nc, f"n{n}", [x], [xn], 1e-5)
                with ExitStack() as inner:
                    tile = lambda m, r=128: inner.enter_context(nc.sbuf_tensor(f"{m}{n}", [r, TOKENS], F32))
                    o = tile("o")
                    rows = nc.dram_tensor("rows", (TOKENS, C), F32, kind="Internal").ap()
                    with ExitStack() as weights:
                        attn = weights.enter_context(nc.sbuf_tensor(
                            "wave_attn", [128, TOKENS // 128, WAVE_HEADS, SAMPLES], F32))
                        index = weights.enter_context(nc.sbuf_tensor(
                            "wave_index", [128, TOKENS // 128, SAMPLES], I32))
                        wave_attention_weights(nc, f"w{n}", xn, rows, attn, index, p)
                        wave_gather(nc, f"g{n}", rows, attn, index, o)
                    se1, se = tile("se1", 32), tile("se")
                    project(nc, f"p1{n}", [o], [dict(dst=se1, func=ACT.Silu, w=[p["w_se1"]], bias=p["b_se1"])])
                    project(nc, f"p2{n}", [se1], [dict(dst=se, func=ACT.Sigmoid, w=[p["w_se2"]], bias=p["b_se2"])])
                    pointwise(nc, f"e{n}", [(o, o, se, ALU.mult)])
                    project(nc, f"po{n}", [o], [dict(dst=se, func=ACT.Silu, w=[p["w_out"]])])
                    add_tile(nc, f"r{n}", x, se)
            if n == 2:
                p = sub_params(a, "L0_attn_b_")
                norm(nc, f"n{n}", [x], [xn], 1e-5)
                with ExitStack() as inner:
                    tile = lambda m, r=128: inner.enter_context(nc.sbuf_tensor(f"{m}{n}", [r, TOKENS], F32))
                    u, z = [tile("u0"), tile("u1")], [tile("z0"), tile("z1")]
                    cut = lambda m: [p["W_in"][:, 128 * m:128 * m + 128]]
                    project(nc, f"p{n}", [xn], [dict(dst=u[m], func=ACT.Silu, w=cut(m)) for m in range(2)])
                    project(nc, f"pz{n}", [xn], [dict(dst=z[m], func=ACT.Sigmoid, w=cut(2 + m)) for m in range(2)])
                    pointwise(nc, f"e{n}", [(u[m], u[m], z[m], ALU.mult) for m in range(2)])
                    stacks = z[0][0:48].bitcast(BF16), z[1][0:48].bitcast(BF16)
                    rows = dict(A=(z[0][64:80], 64, stacks[0][:, 0:TOKENS]),
                                B=(z[0][96:112], 96, stacks[0][:, TOKENS:2 * TOKENS]),
                                C=(z[1][64:80], 64, stacks[1][:, 0:TOKENS]))
                    project(nc, f"pr{n}", u, [dict(dst=rows[c][0], w=[p["W_" + c][0:128, :], p["W_" + c][128:256, :]])
                                              for c in "ABC"])
                    clipped_decay(nc, f"d{n}", rows["A"][0])
                    selective_scan(nc, f"s{n}", u, rows["B"], rows["C"], u, decay_rows=rows["A"])
                    norm(nc, f"nb{n}", u, u, 1.1920929e-07, center=False, gain=p["norm_w"])
                    project(nc, f"po{n}", u, [dict(dst=x, add=True, w=[p["W_out"][128 * m:128 * m + 128, :]
                                                                        for m in range(2)])])
            if n == 4:
                p = sub_params(a, "L1_attn_a_")
                norm(nc, f"n{n}", [x], [xn], 1e-5)
                with ExitStack() as inner:
                    tile = lambda m, r=128: inner.enter_context(nc.sbuf_tensor(f"{m}{n}", [r, TOKENS], F32))
                    xc, dl, u = ([tile(f"{m}{r}") for r in range(2)] for m in ("xc", "dl", "u"))
                    norm(nc, f"na{n}", [xn], [u[0]], 1e-5, center=False, gain=p["norm_w"])
                    half = lambda m: slice(128 * m, 128 * m + 128)
                    project(nc, f"p{n}", [u[0]], [dict(dst=xc[m], w=[p["in_w"][:, half(m)]]) for m in range(2)])
                    causal_conv(nc, f"c{n}", xc, p["conv_w"], p["conv_b"])
                    project(nc, f"pd{n}", xc, [dict(dst=u[0], w=[p["wd1"][half(m), :] for m in range(2)])])
                    project(nc, f"pe{n}", [u[0]], [dict(dst=dl[m], w=[p["wd2"][:, half(m)]], bias=p["wd2_b"][half(m)])
                                                  for m in range(2)])
                    softplus(nc, f"sp{n}", dl)
                    pointwise(nc, f"e{n}", [(u[m], dl[m], xc[m], ALU.mult) for m in range(2)])
                    with ExitStack() as rows_ctx:
                        both = rows_ctx.enter_context(nc.sbuf_tensor(f"rows{n}", [128, TOKENS], F32))
                        stacks = both[0:48].bitcast(BF16)
                        rows = dict(b=(both[64:80], 64, stacks[:, 0:TOKENS]),
                                    c=(both[96:112], 96, stacks[:, TOKENS:2 * TOKENS]))
                        project(nc, f"pr{n}", xc, [dict(dst=rows[c][0], w=[p["w" + c][half(m), :] for m in range(2)])
                                                  for c in "bc"])
                        selective_scan(nc, f"s{n}", u, rows["b"], rows["c"], u, delta=dl, a_log=p["A_log"])
                    pointwise(nc, f"f{n}", [(u[m], xc[m], p["W_D"][half(m)], u[m], ALU.mult, ALU.add)
                                           for m in range(2)])
                    norm(nc, f"nb{n}", [xn], [dl[0]], 1e-5, center=False, gain=p["norm_w"])
                    project(nc, f"ps{n}", [dl[0]], [dict(dst=xc[m], func=ACT.Silu, w=[p["skip_w"][:, half(m)]])
                                                    for m in range(2)])
                    pointwise(nc, f"g{n}", [(u[m], u[m], xc[m], ALU.mult) for m in range(2)] + [(x, x, xn, ALU.add)])
                    project(nc, f"po{n}", u, [dict(dst=x, add=True, w=[p["out_w"][half(m), :] for m in range(2)])])
            if n == 14:
                p = sub_params(a, "L3_attn_b_")
                norm(nc, f"n{n}", [x], [xn], 1e-5)
                with ExitStack() as inner:
                    tile = lambda m, r=128: inner.enter_context(nc.sbuf_tensor(f"{m}{n}", [r, TOKENS], F32))
                    q, k, v, gate = tile("q"), tile("k"), tile("v"), tile("gate", 16)
                    project(nc, f"p{n}", [xn], [dict(dst=q, w=[p["Wq"]]), dict(dst=k, w=[p["Wk"]]),
                                                dict(dst=v, w=[p["Wv"]])])
                    project(nc, f"pg{n}", [xn], [dict(dst=gate, func=ACT.Sigmoid, w=[p["Wg"]], bias=p["bg"])])
                    feature_map(nc, f"f{n}", q, k, float(DH) ** -0.5)
                    gated_linear_attention(nc, f"l{n}", q, k, v, gate, q)
                    project(nc, f"po{n}", [q], [dict(dst=x, add=True, w=[p["Wo"]])])
            if n == 6:
                p = sub_params(a, "L1_attn_b_")
                norm(nc, f"n{n}", [x], [xn], 1e-5)
                with ExitStack() as inner:
                    tile = lambda m: inner.enter_context(nc.sbuf_tensor(f"{m}{n}", [128, TOKENS], F32))
                    h, xc, z = tile("h"), [tile("xc0"), tile("xc1")], [tile("z0"), tile("z1")]
                    norm(nc, f"na{n}", [xn], [h], 1e-5, gain=p["norm_w"], shift=p["norm_b"])
                    cut = lambda m: dict(w=[p["in_w"][:, 128 * m:128 * m + 128]], bias=p["in_b"][128 * m:128 * m + 128])
                    project(nc, f"p{n}", [h], [dict(dst=xc[m], **cut(m)) for m in range(2)])
                    project(nc, f"pz{n}", [h], [dict(dst=z[m], func=ACT.Silu, **cut(2 + m)) for m in range(2)])
                    causal_conv(nc, f"c{n}", xc, p["conv_w"], p["conv_b"])
                    mean_gate(nc, f"g{n}", xc, h, p["xproj_w"][:, 17:33])
                    pointwise(nc, f"e{n}", [st for m in range(2) for st in (
                        (xc[m], h, p["D"][128 * m:128 * m + 128], xc[m], ALU.add, ALU.mult),
                        (xc[m], xc[m], z[m], ALU.mult))] + [(x, x, xn, ALU.add)])
                    project(nc, f"po{n}", xc, [dict(dst=x, add=True, bias=p["out_b"],
                                                    w=[p["out_w"][128 * m:128 * m + 128, :] for m in range(2)])])
            if n == 8:
                p = sub_params(a, "L2_attn_a_")
                norm(nc, f"n{n}", [x], [xn], 1e-5)
                with ExitStack() as inner:
                    tile = lambda m: inner.enter_context(nc.sbuf_tensor(f"{m}{n}", [128, TOKENS], F32))
                    h, u = tile("h"), [tile(f"u{m}") for m in range(4)]
                    norm(nc, f"na{n}", [xn], [h], 1e-5, gain=p["ln_conv_g"], shift=p["ln_conv_b"])
                    grouped_conv(nc, f"c{n}", h, xn, p["conv_w"], p["conv_b"])
                    norm(nc, f"nb{n}", [xn], [h], 1e-5, gain=p["ln_attn_g"], shift=p["ln_attn_b"])
                    project(nc, f"p{n}", [h], [dict(dst=u[m], w=[p["W" + c]], bias=p["b" + c])
                                               for m, c in enumerate("qkv")])
                    pooled_mix(nc, f"m{n}", u[0], u[1], u[2], xn)
                    norm(nc, f"nc{n}", [xn], [h], 1e-5, gain=p["ln_boom_g"], shift=p["ln_boom_b"])
                    project(nc, f"pb{n}", [h], [dict(dst=u[m], func=ACT.Gelu, w=[p["Wb"][:, 128 * m:128 * m + 128]],
                                                     bias=p["bb"][128 * m:128 * m + 128]) for m in range(4)])
                    add_tile(nc, f"r{n}", x, xn)
                    project(nc, f"pu{n}", u, [dict(dst=x, add=True, bias=p["bu"],
                                                   w=[p["Wu"][128 * m:128 * m + 128, :] for m in range(4)])])
            if n == 10:
                p = sub_params(a, "L2_attn_b_")
                norm(nc, f"n{n}", [x], [xn], 1e-5)
                with ExitStack() as inner:
                    v_all = inner.enter_context(nc.sbuf_tensor(f"v{n}", [128, BATCH * HEADS, 8, DH + 1], F32))
                    q = dict(interleaved=True, causal=False, wq=p["W_qkv"][0], wk=p["W_qkv"][1], wv=p["W_qkv"][2],
                             bq=p["b_qkv"][0], bk=p["b_qkv"][1],
                             bv=p["b_qkv"][2].rearrange("(r n) -> r n", r=2), wo=p["W_out"], bo=p["b_out"])
                    attention_inputs(nc, f"i{n}", xn, scratch, v_all, q)
                    attention(nc, f"a{n}", scratch, v_all, x, q)
            if n == 12:
                p = sub_params(a, "L3_attn_a_")
                norm(nc, f"n{n}", [x], [xn], 1e-5)
                norm(nc, f"na{n}", [xn], [xn], 1e-5, gain=p["g_ln"])
                with ExitStack() as inner:
                    v_all = inner.enter_context(nc.sbuf_tensor(f"v{n}", [128, BATCH * HEADS, 8, DH + 1], F32))
                    q = dict(interleaved=False, causal=True, wq=p["Wq"], wk=p["Wkv"][:, 0:128],
                             wv=p["Wkv"][:, 128:256], wo=p["Wo"])
                    attention_inputs(nc, f"i{n}", xn, scratch, v_all, q)
                    attention(nc, f"a{n}", scratch, v_all, x, q)
            if n in (5, 7, 9, 11, 13, 15):
                kind = "L" + str(n // 4)
                norm(nc, f"n{n}", [x], [xn], 1e-5)
                moe(nc, f"m{n}", kind, xn, x, moe_weights(kind, sub_params(a, kind + "_ffn_")))
        with nc.Block() as block:
            @block.sync
            def _(sp):
                sp.dma_start(out_dram, x[:]).then_inc(s.stored, 16)
                sp.wait_ge(s.stored, 16)


def layouts(inputs):
    import numpy as np

    t = {k: np.asarray(v) for k, v in inputs.items()}
    out = dict(t)
    T = lambda name, *axes: out.__setitem__(name, np.ascontiguousarray(t[name].transpose(*axes)))
    out["L0_ffn_W1"] = np.ascontiguousarray(t["L0_ffn_W1"].transpose(1, 0, 2)).reshape(128, 32, 128)
    out["L0_ffn_W2"] = np.ascontiguousarray(t["L0_ffn_W2"].reshape(32, 128, 128).transpose(1, 0, 2))
    out["L0_ffn_b1"] = np.ascontiguousarray(t["L0_ffn_b1"].reshape(32, 128).T)
    T("L2_ffn_router_weight", 1, 0)
    for n in ("L1_attn_b_in_w", "L1_attn_b_xproj_w", "L1_attn_b_out_w", "L2_attn_a_Wq", "L2_attn_a_Wk",
              "L2_attn_a_Wv", "L2_attn_a_Wb", "L2_attn_a_Wu", "L1_attn_a_skip_w", "L1_attn_a_in_w",
              "L1_attn_a_wd1", "L1_attn_a_wd2", "L1_attn_a_wb", "L1_attn_a_wc", "L1_attn_a_out_w",
              "L3_attn_b_Wq", "L3_attn_b_Wk", "L3_attn_b_Wv", "L3_attn_b_Wo", "L3_attn_b_Wg"):
        T(n, 1, 0)
    out["L1_attn_b_conv_w"] = t["L1_attn_b_conv_w"].reshape(256, 4)
    T("L2_attn_a_conv_w", 2, 1, 0)
    for n in ("gate_w", "up_w"):
        out["L2_ffn_" + n] = np.ascontiguousarray(t["L2_ffn_" + n].transpose(2, 0, 1)).reshape(128, 8, 128)
    out["L2_ffn_down_w"] = np.ascontiguousarray(
        t["L2_ffn_down_w"].reshape(8, 2, 128, 64).transpose(1, 3, 0, 2)).reshape(128, 8, 128)
    for n in ("sh_gate_w", "sh_up_w", "sh_down_w"):
        T("L2_ffn_" + n, 1, 0)
    f = t["L2_attn_b_W_qkv"].reshape(16, 3, 8, 128)
    fb = t["L2_attn_b_b_qkv"].reshape(16, 3, 8)
    qk, qkb = f[:, 0:2].transpose(1, 3, 2, 0).reshape(2, 128, 128), fb[:, 0:2].transpose(1, 2, 0).reshape(2, 128)
    v = f[:, 2].reshape(8, 2, 8, 128).transpose(3, 1, 0, 2).reshape(1, 128, 128)
    vb = fb[:, 2].reshape(8, 2, 8).transpose(1, 0, 2).reshape(1, 128)
    out["L2_attn_b_W_qkv"] = np.ascontiguousarray(np.concatenate([qk, v]))
    out["L2_attn_b_b_qkv"] = np.ascontiguousarray(np.concatenate([qkb, vb]))
    T("L2_attn_b_W_out", 1, 0)
    for n in ("Wg", "Wu"):
        out["L3_ffn_" + n] = np.ascontiguousarray(t["L3_ffn_" + n].transpose(1, 0, 2)).reshape(128, 16, 128)
    return out


def kernel(**inputs):
    import numpy as np
    import concourse.bacc as bacc
    from concourse.bass_utils import run_bass_kernel_spmd

    nc = bacc.Bacc("TRN2", target_bir_lowering=False, num_devices=1)
    arrays, a = {}, {}
    for name, value in layouts(inputs).items():
        if value.dtype.kind in "iu":
            continue
        if name == "L0_attn_a_x":
            value = np.ascontiguousarray(value.reshape(TOKENS, C).T)
        arrays[f"in_{name}"] = value
        a[name] = nc.dram_tensor(f"in_{name}", value.shape, mybir.dt.from_np(value.dtype), kind="ExternalInput").ap()
    out = nc.dram_tensor("out", (C, TOKENS), F32, kind="ExternalOutput").ap()
    program(nc, a, a["L0_attn_a_x"], out, range(16))
    result = run_bass_kernel_spmd(nc, [arrays], core_ids=[0])
    return np.ascontiguousarray(result.results[0]["out"].T).reshape(BATCH, SEQ, C)
```
